# Optimizing a Trainium2 kernel written in Bass

```python
import numpy as np
import jax
import jax.numpy as jnp

def _softmax(x, axis=-1):
    return jax.nn.softmax(x, axis=axis)

def _gelu(x):
    return jax.nn.gelu(x, approximate=True)

def _silu(x):
    return jax.nn.silu(x)

def _sigmoid(x):
    return jax.nn.sigmoid(x)

def _layernorm(x, axis=-1, eps=1e-05):
    m = jnp.mean(x, axis=axis, keepdims=True)
    v = jnp.var(x, axis=axis, keepdims=True)
    return (x - m) / jnp.sqrt(v + eps)

def _scatter_add(tgt, idx, src, axis=0):
    return tgt.at[idx].add(src)

def _segment_sum(src, seg, n):
    return jax.ops.segment_sum(src, seg, n)
kernel_name = 'mk_xattn_ffn_d2_seqx_r8_498000'

def setup_inputs(seed: int=0):
    np.random.seed(seed)
    _w = jnp.asarray

    def _rec_inputs():
        import jax
        import jax.numpy as jnp
        _rk = jax.random.key(seed)
        x = 7.22e-05 + 1 * jax.random.normal(jax.random.fold_in(_rk, 1), (2, 512, 128), jnp.float32)
        _lenS = 512 - jax.random.randint(jax.random.fold_in(_rk, 7), (2,), 0, max(1, 512 // 4) + 1, jnp.int32)
        _lenS2 = 154 - jax.random.randint(jax.random.fold_in(_rk, 8), (2,), 0, max(1, 154 // 4) + 1, jnp.int32)
        _ctx_768P = jax.random.normal(jax.random.fold_in(_rk, 11), (2, 16, 96), jnp.float32)
        _ctx_768c = jax.random.dirichlet(jax.random.fold_in(_rk, 511), 0.3 * jnp.ones((16,), jnp.float32), (2, 154))
        _ctx_768t = jnp.einsum('bsk,bkd->bsd', _ctx_768c, _ctx_768P)
        _ctx_768t = _ctx_768t * jax.lax.rsqrt(jnp.mean(jnp.square(_ctx_768t)) + 1e-12) * 0.953939
        ctx_768 = -0.000191848 + 0.999787 * (_ctx_768t + 0.3 * jax.random.normal(jax.random.fold_in(_rk, 611), (2, 154, 96), jnp.float32))
        _validS = jnp.arange(512)[None, :] < _lenS[:, None]
        _validS2 = jnp.arange(154)[None, :] < _lenS2[:, None]
        _causal = jnp.tril(jnp.ones((512, 512), dtype=bool))
        mask_1x1xSxS2_bk0 = jnp.logical_not(jnp.broadcast_to(_validS2[0:1, None, None, :], (1, 1, 512, 154)))
        return (x, ctx_768, mask_1x1xSxS2_bk0)
    x, ctx_768, mask_1x1xSxS2_bk0 = _rec_inputs()

    def _L0_xattn_setup():
        import jax, jax.numpy as jnp
        import numpy as np
        B, T, Q_DIM, KV_DIM = (4, 256, 128, 96)
        HEADS, DIM_HEAD = (16, 64)
        INNER = HEADS * DIM_HEAD
        NUM_FRAMES, NUM_PATCHES = (8, 32)
        LN_EPS = 1e-05

        def diagonal_frame_mask(num_patches, num_frames):
            fid = np.repeat(np.arange(num_frames), num_patches)
            m = fid[:, None] == fid[None, :]
            return jnp.asarray(m[None, None])
        key = jax.random.key(seed)
        ks = jax.random.split(key, 6)
        s = lambda d: 1.0 / np.sqrt(d)
        return {'x': jax.random.normal(ks[0], (B, T, Q_DIM), jnp.float32), 'context': jax.random.normal(ks[1], (B, T, KV_DIM), jnp.float32), 'ln_gamma': jnp.ones((Q_DIM,), jnp.float32), 'ln_beta': jnp.zeros((Q_DIM,), jnp.float32), 'Wq': jax.random.normal(ks[2], (Q_DIM, INNER), jnp.float32) * s(Q_DIM), 'Wkv': jax.random.normal(ks[3], (KV_DIM, 2 * INNER), jnp.float32) * s(KV_DIM), 'Wo': jax.random.normal(ks[4], (INNER, Q_DIM), jnp.float32) * s(INNER), 'bo': jnp.zeros((Q_DIM,), jnp.float32), 'mask': diagonal_frame_mask(NUM_PATCHES, NUM_FRAMES)}
    _L0_xattn_all = _L0_xattn_setup()
    _L0_xattn_in = {k: v for k, v in _L0_xattn_all.items() if k in ('ln_gamma', 'ln_beta', 'Wq', 'Wkv', 'Wo', 'bo')}
    del _L0_xattn_all

    def _L0_ffn_setup():
        import jax, jax.numpy as jnp
        import numpy as np
        D_MODEL = 128
        HIDDEN = 128
        NUM_EXPERTS = 8
        TOP_K = 2
        key = jax.random.key(seed)
        ks = jax.random.split(key, 10)
        s = 0.02
        return {'x': jax.random.normal(ks[0], (2, 256, D_MODEL), dtype=jnp.float32), 'gate_w': jax.random.normal(ks[1], (NUM_EXPERTS, D_MODEL), dtype=jnp.float32) * s, 'up_w': jax.random.normal(ks[2], (NUM_EXPERTS, D_MODEL, HIDDEN), dtype=jnp.float32) * s, 'up_b': jnp.zeros((NUM_EXPERTS, HIDDEN), dtype=jnp.float32), 'down_w': jax.random.normal(ks[3], (NUM_EXPERTS, HIDDEN, D_MODEL), dtype=jnp.float32) * s, 'down_b': jnp.zeros((NUM_EXPERTS, D_MODEL), dtype=jnp.float32), 'sh_up_w': jax.random.normal(ks[4], (D_MODEL, HIDDEN), dtype=jnp.float32) * s, 'sh_up_b': jnp.zeros((HIDDEN,), dtype=jnp.float32), 'sh_down_w': jax.random.normal(ks[5], (HIDDEN, D_MODEL), dtype=jnp.float32) * s, 'sh_down_b': jnp.zeros((D_MODEL,), dtype=jnp.float32)}
    _L0_ffn_all = _L0_ffn_setup()
    _L0_ffn_in = {k: v for k, v in _L0_ffn_all.items() if k in ('gate_w', 'up_w', 'up_b', 'down_w', 'down_b', 'sh_up_w', 'sh_up_b', 'sh_down_w', 'sh_down_b')}
    del _L0_ffn_all

    def _L1_xattn_setup():
        import jax, jax.numpy as jnp
        import numpy as np
        HEADS = 8
        DIM_HEAD = 64
        QUERY_DIM = 128
        CONTEXT_DIM = 96
        INNER = HEADS * DIM_HEAD
        key = jax.random.key(seed)
        ks = jax.random.split(key, 7)
        B, Sq, Skv = (4, 512, 128)
        x = jax.random.normal(ks[0], (B, Sq, QUERY_DIM), dtype=jnp.float32)
        context = jax.random.normal(ks[1], (B, Skv, CONTEXT_DIM), dtype=jnp.float32)
        Wq = jax.random.normal(ks[2], (QUERY_DIM, INNER), dtype=jnp.float32) * QUERY_DIM ** (-0.5)
        Wk = jax.random.normal(ks[3], (CONTEXT_DIM, INNER), dtype=jnp.float32) * CONTEXT_DIM ** (-0.5)
        Wv = jax.random.normal(ks[4], (CONTEXT_DIM, INNER), dtype=jnp.float32) * CONTEXT_DIM ** (-0.5)
        Wo = jax.random.normal(ks[5], (INNER, QUERY_DIM), dtype=jnp.float32) * INNER ** (-0.5)
        bo = jax.random.normal(ks[6], (QUERY_DIM,), dtype=jnp.float32) * 0.01
        return {'x': x, 'context': context, 'Wq': Wq, 'Wk': Wk, 'Wv': Wv, 'Wo': Wo, 'bo': bo}
    _L1_xattn_all = _L1_xattn_setup()
    _L1_xattn_in = {k: v for k, v in _L1_xattn_all.items() if k in ('Wq', 'Wk', 'Wv', 'Wo', 'bo')}
    del _L1_xattn_all

    def _L1_ffn_setup():
        import jax, jax.numpy as jnp
        import numpy as np
        D_MODEL = 128
        N_HEADS = 16
        N_EXPERTS = 8
        TOP_K = 2
        EXPERT_HIDDEN = D_MODEL * 4 // N_EXPERTS

        def layer_norm(x, g, b, eps=1e-05):
            mu = jnp.mean(x, axis=-1, keepdims=True)
            var = jnp.var(x, axis=-1, keepdims=True)
            return (x - mu) * jax.lax.rsqrt(var + eps) * g + b
        key = jax.random.key(seed)
        ks = jax.random.split(key, 12)
        s = 1.0 / np.sqrt(D_MODEL)
        return {'x': jax.random.normal(ks[0], (2, 256, D_MODEL), dtype=jnp.float32), 'Wq': jax.random.normal(ks[1], (D_MODEL, D_MODEL), dtype=jnp.float32) * s, 'Wk': jax.random.normal(ks[2], (D_MODEL, D_MODEL), dtype=jnp.float32) * s, 'Wv': jax.random.normal(ks[3], (D_MODEL, D_MODEL), dtype=jnp.float32) * s, 'Wo': jax.random.normal(ks[4], (D_MODEL, D_MODEL), dtype=jnp.float32) * s, 'g1': jnp.ones((D_MODEL,), jnp.float32), 'b1': jnp.zeros((D_MODEL,), jnp.float32), 'g2': jnp.ones((D_MODEL,), jnp.float32), 'b2': jnp.zeros((D_MODEL,), jnp.float32), 'Wg': jax.random.normal(ks[5], (D_MODEL, N_EXPERTS), dtype=jnp.float32) * s, 'W1': jax.random.normal(ks[6], (N_EXPERTS, D_MODEL, EXPERT_HIDDEN), dtype=jnp.float32) * s, 'W2': jax.random.normal(ks[7], (N_EXPERTS, EXPERT_HIDDEN, D_MODEL), dtype=jnp.float32) * (1.0 / np.sqrt(EXPERT_HIDDEN))}
    _L1_ffn_all = _L1_ffn_setup()
    _L1_ffn_in = {k: v for k, v in _L1_ffn_all.items() if k in ('Wq', 'Wk', 'Wv', 'Wo', 'g1', 'b1', 'g2', 'b2', 'Wg', 'W1', 'W2')}
    del _L1_ffn_all
    return {'x': x, 'ctx_768': ctx_768, 'mask_1x1xSxS2_bk0': mask_1x1xSxS2_bk0, 'L0_xattn_ln_gamma': _L0_xattn_in['ln_gamma'], 'L0_xattn_ln_beta': _L0_xattn_in['ln_beta'], 'L0_xattn_Wq': _L0_xattn_in['Wq'], 'L0_xattn_Wkv': _L0_xattn_in['Wkv'], 'L0_xattn_Wo': _L0_xattn_in['Wo'], 'L0_xattn_bo': _L0_xattn_in['bo'], 'L0_ffn_gate_w': _L0_ffn_in['gate_w'], 'L0_ffn_up_w': _L0_ffn_in['up_w'], 'L0_ffn_up_b': _L0_ffn_in['up_b'], 'L0_ffn_down_w': _L0_ffn_in['down_w'], 'L0_ffn_down_b': _L0_ffn_in['down_b'], 'L0_ffn_sh_up_w': _L0_ffn_in['sh_up_w'], 'L0_ffn_sh_up_b': _L0_ffn_in['sh_up_b'], 'L0_ffn_sh_down_w': _L0_ffn_in['sh_down_w'], 'L0_ffn_sh_down_b': _L0_ffn_in['sh_down_b'], 'L1_xattn_Wq': _L1_xattn_in['Wq'], 'L1_xattn_Wk': _L1_xattn_in['Wk'], 'L1_xattn_Wv': _L1_xattn_in['Wv'], 'L1_xattn_Wo': _L1_xattn_in['Wo'], 'L1_xattn_bo': _L1_xattn_in['bo'], 'L1_ffn_Wq': _L1_ffn_in['Wq'], 'L1_ffn_Wk': _L1_ffn_in['Wk'], 'L1_ffn_Wv': _L1_ffn_in['Wv'], 'L1_ffn_Wo': _L1_ffn_in['Wo'], 'L1_ffn_g1': _L1_ffn_in['g1'], 'L1_ffn_b1': _L1_ffn_in['b1'], 'L1_ffn_g2': _L1_ffn_in['g2'], 'L1_ffn_b2': _L1_ffn_in['b2'], 'L1_ffn_Wg': _L1_ffn_in['Wg'], 'L1_ffn_W1': _L1_ffn_in['W1'], 'L1_ffn_W2': _L1_ffn_in['W2']}

def reference(x, ctx_768, mask_1x1xSxS2_bk0, L0_xattn_ln_gamma, L0_xattn_ln_beta, L0_xattn_Wq, L0_xattn_Wkv, L0_xattn_Wo, L0_xattn_bo, L0_ffn_gate_w, L0_ffn_up_w, L0_ffn_up_b, L0_ffn_down_w, L0_ffn_down_b, L0_ffn_sh_up_w, L0_ffn_sh_up_b, L0_ffn_sh_down_w, L0_ffn_sh_down_b, L1_xattn_Wq, L1_xattn_Wk, L1_xattn_Wv, L1_xattn_Wo, L1_xattn_bo, L1_ffn_Wq, L1_ffn_Wk, L1_ffn_Wv, L1_ffn_Wo, L1_ffn_g1, L1_ffn_b1, L1_ffn_g2, L1_ffn_b2, L1_ffn_Wg, L1_ffn_W1, L1_ffn_W2):
    import jax
    import jax.numpy as jnp

    def _L0_xattn_ref(x, context, ln_gamma, ln_beta, Wq, Wkv, Wo, bo, mask):
        import jax, jax.numpy as jnp
        import numpy as np
        B, T, Q_DIM, KV_DIM = (4, 256, 128, 96)
        HEADS, DIM_HEAD = (16, 64)
        INNER = HEADS * DIM_HEAD
        NUM_FRAMES, NUM_PATCHES = (8, 32)
        LN_EPS = 1e-05

        def diagonal_frame_mask(num_patches, num_frames):
            fid = np.repeat(np.arange(num_frames), num_patches)
            m = fid[:, None] == fid[None, :]
            return jnp.asarray(m[None, None])
        mu = jnp.mean(x, axis=-1, keepdims=True)
        var = jnp.mean(jnp.square(x - mu), axis=-1, keepdims=True)
        xn = (x - mu) * jax.lax.rsqrt(var + LN_EPS) * ln_gamma + ln_beta
        scale = DIM_HEAD ** (-0.5)
        q = xn @ Wq
        kv = context @ Wkv
        k, v = jnp.split(kv, 2, axis=-1)
        split_heads = lambda t: t.reshape(t.shape[0], t.shape[1], HEADS, DIM_HEAD).transpose(0, 2, 1, 3)
        q, k, v = (split_heads(q), split_heads(k), split_heads(v))
        dots = jnp.einsum('bhnd,bhmd->bhnm', q, k) * scale
        dots = jnp.where(mask, dots, -jnp.inf)
        attn = jax.nn.softmax(dots, axis=-1)
        out = jnp.einsum('bhnm,bhmd->bhnd', attn, v)
        out = out.transpose(0, 2, 1, 3).reshape(x.shape[0], x.shape[1], INNER)
        return out @ Wo + bo

    def _L0_ffn_ref(x, gate_w, up_w, up_b, down_w, down_b, sh_up_w, sh_up_b, sh_down_w, sh_down_b):
        import jax, jax.numpy as jnp
        import numpy as np
        D_MODEL = 128
        HIDDEN = 128
        NUM_EXPERTS = 8
        TOP_K = 2
        b, s, d = x.shape
        xf = x.reshape(-1, d)
        shared = jax.nn.silu(x @ sh_up_w + sh_up_b) @ sh_down_w + sh_down_b
        logits = xf @ gate_w.T
        scores = jax.nn.softmax(logits, axis=-1)
        topk_w, topk_i = jax.lax.top_k(scores, TOP_K)
        topk_w = topk_w / (topk_w.sum(axis=-1, keepdims=True) + 1e-20)
        comb = (jax.nn.one_hot(topk_i, NUM_EXPERTS, dtype=xf.dtype) * topk_w[..., None]).sum(axis=1)
        h = jnp.einsum('nd,edh->neh', xf, up_w) + up_b
        h = jax.nn.silu(h)
        ye = jnp.einsum('neh,ehd->ned', h, down_w) + down_b
        y = jnp.einsum('ned,ne->nd', ye, comb).reshape(b, s, d)
        return y + shared

    def _L1_xattn_ref(x, context, Wq, Wk, Wv, Wo, bo):
        import jax, jax.numpy as jnp
        import numpy as np
        HEADS = 8
        DIM_HEAD = 64
        QUERY_DIM = 128
        CONTEXT_DIM = 96
        INNER = HEADS * DIM_HEAD
        B, Sq, _ = x.shape
        h, d = (HEADS, DIM_HEAD)
        scale = d ** (-0.5)
        q = (x @ Wq).reshape(B, Sq, h, d).transpose(0, 2, 1, 3)
        k = (context @ Wk).reshape(B, -1, h, d).transpose(0, 2, 1, 3)
        v = (context @ Wv).reshape(B, -1, h, d).transpose(0, 2, 1, 3)
        scores = jnp.einsum('bhid,bhjd->bhij', q, k) * scale
        attn = jax.nn.softmax(scores, axis=-1)
        out = jnp.einsum('bhij,bhjd->bhid', attn, v)
        out = out.transpose(0, 2, 1, 3).reshape(B, Sq, h * d)
        return out @ Wo + bo

    def _L1_ffn_ref(x, Wq, Wk, Wv, Wo, g1, b1, g2, b2, Wg, W1, W2):
        import jax, jax.numpy as jnp
        import numpy as np
        D_MODEL = 128
        N_HEADS = 16
        N_EXPERTS = 8
        TOP_K = 2
        EXPERT_HIDDEN = D_MODEL * 4 // N_EXPERTS

        def layer_norm(x, g, b, eps=1e-05):
            mu = jnp.mean(x, axis=-1, keepdims=True)
            var = jnp.var(x, axis=-1, keepdims=True)
            return (x - mu) * jax.lax.rsqrt(var + eps) * g + b
        B, S, D = x.shape
        H, dk = (N_HEADS, D // N_HEADS)
        xn = layer_norm(x, g1, b1)
        q = (xn @ Wq).reshape(B, S, H, dk).transpose(0, 2, 1, 3)
        k = (xn @ Wk).reshape(B, S, H, dk).transpose(0, 2, 1, 3)
        v = (xn @ Wv).reshape(B, S, H, dk).transpose(0, 2, 1, 3)
        scores = jnp.einsum('bhqd,bhkd->bhqk', q, k) / np.sqrt(dk)
        attn = jax.nn.softmax(scores, axis=-1)
        o = jnp.einsum('bhqk,bhkd->bhqd', attn, v)
        o = o.transpose(0, 2, 1, 3).reshape(B, S, D) @ Wo
        x = x + o
        xn2 = layer_norm(x, g2, b2)
        xf = xn2.reshape(B * S, D)
        gate = xf @ Wg
        topv, topi = jax.lax.top_k(gate, TOP_K)
        probs = jax.nn.softmax(topv, axis=-1)
        cw = jnp.sum(jax.nn.one_hot(topi, N_EXPERTS, dtype=xf.dtype) * probs[..., None], axis=1)
        h = jax.nn.relu(jnp.einsum('td,edh->teh', xf, W1))
        y = jnp.einsum('teh,ehd->ted', h, W2)
        moe = jnp.einsum('ted,te->td', y, cw).reshape(B, S, D)
        return x + moe
    x = x + _L0_xattn_ref(_layernorm(x, axis=-1), ctx_768, L0_xattn_ln_gamma, L0_xattn_ln_beta, L0_xattn_Wq, L0_xattn_Wkv, L0_xattn_Wo, L0_xattn_bo, mask_1x1xSxS2_bk0)
    x = x + _L0_ffn_ref(_layernorm(x, axis=-1), L0_ffn_gate_w, L0_ffn_up_w, L0_ffn_up_b, L0_ffn_down_w, L0_ffn_down_b, L0_ffn_sh_up_w, L0_ffn_sh_up_b, L0_ffn_sh_down_w, L0_ffn_sh_down_b)
    x = x + _L1_xattn_ref(_layernorm(x, axis=-1), ctx_768, L1_xattn_Wq, L1_xattn_Wk, L1_xattn_Wv, L1_xattn_Wo, L1_xattn_bo)
    x = x + _L1_ffn_ref(_layernorm(x, axis=-1), L1_ffn_Wq, L1_ffn_Wk, L1_ffn_Wv, L1_ffn_Wo, L1_ffn_g1, L1_ffn_b1, L1_ffn_g2, L1_ffn_b2, L1_ffn_Wg, L1_ffn_W1, L1_ffn_W2)
    return x

_drawn_inputs = setup_inputs


def setup_inputs(seed=0):
    import zlib

    import numpy as np

    out = dict(_drawn_inputs(seed))
    spreads = {'L0_xattn_ln_gamma': (1.0, 0.2),
     'L0_xattn_ln_beta': (0.0, 0.1),
     'L0_xattn_bo': (0.0, 0.1),
     'L0_ffn_up_b': (0.0, 0.559),
     'L0_ffn_down_b': (0.0, 0.1),
     'L0_ffn_sh_up_b': (0.0, 0.33),
     'L0_ffn_sh_down_b': (0.0, 0.1),
     'L1_ffn_g1': (1.0, 0.2),
     'L1_ffn_b1': (0.0, 0.1),
     'L1_ffn_g2': (1.0, 0.2),
     'L1_ffn_b2': (0.0, 0.1)}
    factors = {'L1_xattn_bo': 2.808}
    for name, (base, spread) in spreads.items():
        noise = np.random.default_rng([zlib.crc32(name.encode()), seed]).standard_normal(out[name].shape)
        drawn = base * np.exp(spread * noise) if base else spread * noise
        out[name] = jnp.asarray(drawn.astype(out[name].dtype))
    for name, factor in factors.items():
        out[name] = (out[name] * factor).astype(out[name].dtype)
    return out
```

```python
from contextlib import ExitStack

import concourse.bass as bass
from concourse import mybir

F32 = mybir.dt.float32
BF16 = mybir.dt.bfloat16
U32 = mybir.dt.uint32
ALU = mybir.AluOpType
ACT = mybir.ActivationFunctionType
AX = mybir.AxisListType

P = 128
EPS = 1e-5
BLOCKED = -float(2.0 ** 100)


def build(nc, t, out, stop=4):
    B, S, D = t["x"].shape
    _, T, C = t["ctx_768"].shape
    QT = S // P
    R = T - P
    STRIP = 32
    G4 = 4
    DH = 64
    H0 = t["L0_xattn_Wq"].shape[1] // DH
    H1 = t["L1_xattn_Wq"].shape[1] // DH
    E = t["L0_ffn_up_w"].shape[0]
    HS, DS = 16, 8
    XSCALE = float(DH) ** -0.5
    SSCALE = float(DS) ** -0.5
    EH = t["L1_ffn_W1"].shape[2]
    assert (B, S, D, DH, QT) == (2, 512, 128, 64, 4) and R <= STRIP and HS * DS == D and 2 * EH == P

    ctx = ExitStack()
    with ctx:
        def sb(name, shape, dt=F32):
            return ctx.enter_context(nc.sbuf_tensor(name, shape, dt))

        def sem(name):
            return ctx.enter_context(nc.semaphore(name))

        x = sb("x", [P, B, QT, D])
        OT_ = sb("OT", [P, H0 // 2 * S])
        xh = sb("xh", [P, B, QT, D])
        xT = sb("xT", [P, B, S])
        ident = sb("ident", [P, P])
        identb = sb("identb", [P, P], BF16)
        rows = sb("rows", [16, P])
        cols = sb("cols", [P, 16])
        bo = sb("bo", [P, 3, D])
        mhalf = sb("mhalf", [P, 16])
        stats = sb("stats", [P, B, QT, 6])
        mv = sb("mv", [P, B, QT, 2])
        ve = sb("ve", [P, B, QT])
        rstd = sb("rstd", [P, B, QT])
        v2 = sb("v2", [P, B, QT])
        r2 = sb("r2", [P, B, QT])
        ctxm = sb("ctxm", [P, B, C])
        ctxr = sb("ctxr", [STRIP, B, C])
        ctxT = sb("ctxT", [C, B, T])
        ctxR = sb("ctxR", [C, B, P])
        masku = sb("masku", [P, QT, T], mybir.dt.uint8)
        maskb = sb("maskb", [P, QT, T], BF16)
        maskr = sb("maskr", [P, QT, G4, STRIP], BF16)
        maskT = sb("maskT", [P, 2, S], BF16)
        maskf = OT_[:, 0:QT * T].rearrange("p (q k) -> p q k", q=QT)
        allow = sb("allow", [P, QT, 4])
        selm = sb("selm", [8, G4 + 1, P], BF16)
        class X:
            pass
        xa = []
        for n, H in enumerate((H0, H1)):
            a = X()
            a.n, a.H, a.G = n, H, H // G4
            a.Wq = sb(f"Wq{n}", [P, H * DH])
            a.Wk = sb(f"Wk{n}", [C, H * DH])
            a.Wv = sb(f"Wv{n}", [C, H * DH])
            a.Wo = sb(f"Wo{n}", [P, H // 2, D])
            a.WqT = sb(f"WqT{n}", [P, H // 2, P])
            a.arena = sb(f"arena{n}", [P, H // 2 * B * T + B * H * T + B * H * (DH + 1)])
            w = H // 2 * B * T
            a.KT = a.arena[:, 0:w].rearrange("p (c b k) -> p c b k", c=H // 2, b=B)
            a.KP = a.arena[:, w:w + B * H * T].rearrange("p (b h k) -> p b h k", b=B, h=H)
            a.VA = a.arena[:, w + B * H * T:w + B * H * (T + DH + 1)].rearrange("p (b h d) -> p b h d", b=B, h=H)
            a.KR = sb(f"KR{n}", [P, B, H // G4, G4, STRIP])
            a.VR = sb(f"VR{n}", [P, B, H // G4, G4, DH + 1])
            xa.append(a)
        OT = OT_[:, :].rearrange("p (c s) -> p c s", s=S)
        Ou = sb("Ou", [P, 2, QT, G4 * DH])
        NPT = 16
        PT = sb("PT", [P, NPT, S])
        HT = PT[:, 0:E + 1, :]
        mx = sb("mx", [P, 2, QT, G4])
        mr = sb("mr", [P, 2, QT, G4])
        mparts = sb("mparts", [P, 2, QT, 2, G4], BF16)
        mT = sb("mT", [8, 2, S], BF16)
        rz = sb("rz", [P, 2, QT, G4])
        gwr = sb("gwr", [E, D])
        gateT = sb("gateT", [P, E])
        upw = sb("upw", [P, E + 1, P])
        dnw = sb("dnw", [P, E + 1, D])
        dnb = sb("dnb", [E, D])
        Wg = sb("Wg", [P, E])
        W1 = sb("W1", [P, E, EH])
        W2 = sb("W2", [P, E // 2, D])
        lg = sb("lg", [P, B, QT, E])
        ex = sb("ex", [P, B, QT, E])
        g1 = sb("g1", [P, B, QT, 4])
        top = sb("top", [P, B, QT, 8])
        topi = sb("topi", [P, B, QT, 8], U32)
        topf = sb("topf", [P, B, QT, 8])
        iota = sb("iota", [P, E])
        iotai = sb("iotai", [P, E], mybir.dt.int32)
        oh = sb("oh", [P, B, QT, 2, E])
        comb = sb("comb", [P, B, QT, E])
        combT = xa[0].Wk[0:E, 0:S]
        wy = OT[:, 0:4, :].rearrange("p c s -> p (c s)").rearrange("p (i e d) -> p i e d", i=2, e=E)
        wys = sb("wys", [P, 2, D])
        Ws = sb("Ws", [P, 4, D])
        y = xa[0].WqT[:, :, :].rearrange("p (b q) d -> p b q d", b=B)
        room = Ou[:, :, :, :].rearrange("p u q f -> p (u q f)")
        qk = [[room[:, (3 * i + j) * (S // 2):(3 * i + j + 1) * (S // 2)].bitcast(BF16) for j in range(3)]
              for i in range(2)]
        qkr = xa[0].Wq[:, :].rearrange("p (i s) -> p i s", i=2)
        arena = xa[0].arena
        stack = [[arena[:, (2 * b + i) * 2048:(2 * b + i + 1) * 2048].bitcast(BF16).rearrange(
            "p (c s) -> p c s", s=S) for i in range(2)] for b in range(B)]
        VS = [xa[1].arena[:, b * QT * HS * STRIP:(b + 1) * QT * HS * STRIP].rearrange(
            "p (q h d) -> p q h d", q=QT, h=HS) for b in range(B)]
        OS = xa[0].Wo[:, :, :].rearrange("p c d -> p (c d)").rearrange("p (i s) -> p i s", i=2)
        On = room[:, 3 * S:4 * S].rearrange("p (q h d) -> p q h d", q=QT, h=HS)
        zs = sb("zs", [P, 2, QT, G4])

        scratch = nc.dram_tensor("parts_scratch", [B, 2, 3, P, S], BF16).ap()

        pS = [ctx.enter_context(nc.psum_tensor(f"pS{i}", [P, 1024], F32)) for i in range(2)]
        pT = [ctx.enter_context(nc.psum_tensor(f"pT{i}", [P, 512], F32)) for i in range(2)]
        pC = [ctx.enter_context(nc.psum_tensor(f"pC{i}", [P, 512], F32)) for i in range(2)]
        RING = {"S": pS, "T": pT, "C": pC}
        FULL = {r: [sem(f"{r}{i}_full") for i in range(2)] for r in RING}
        FREE = {r: [sem(f"{r}{i}_free") for i in range(2)] for r in RING}
        uses = {r: 0 for r in RING}
        at = {}

        W = {k: sem(f"ld_{k}") for k in ("x", "ctx", "rows", "mask", "Wq0", "Wk0", "Wv0", "Wo0", "bo", "gate",
                                         "upw", "dnw", "Wq1", "Wk1", "Wv1", "Wo1", "Wg", "Ws", "W1", "W2")}
        consts = sem("consts")
        stats_ready = sem("stats_ready")
        rstd_ready = sem("rstd_ready")
        xh_ready = sem("xh_ready")
        xb_ready = sem("xb_ready")
        x_ready = sem("x_ready")
        mask_ready = sem("mask_ready")
        mp_ready = sem("mp_ready")
        lg_ready = sem("lg_ready")
        ex_ready = sem("ex_ready")
        comb_ready = sem("comb_ready")
        part_ready = sem("part_ready")
        pads_ready = sem("pads_ready")
        parked = sem("parked")
        stacked = sem("stacked")
        mrow_ready = sem("mrow_ready")
        p_used = sem("p_used")
        stored = sem("stored")
        chain = {e: sem(f"{e}_chain") for e in ("dve", "act", "pool")}
        links = dict.fromkeys(chain, 0)

        block = ctx.enter_context(nc.Block())
        units = [[(b, g) for b in range(B) for g in range(H // G4)] for H in (H0, H1, HS)]
        before = [0, len(units[0]), len(units[0]) + len(units[1])]

        def filled(eng, key):
            ring, buf, turn = at[key]
            eng.wait_ge(FULL[ring][buf], turn + 1)
            return RING[ring][buf]

        def freed(key):
            ring, buf, _ = at[key]
            return FREE[ring][buf]

        def taken(eng, key):
            eng.wait_ge(freed(key), at[key][2] + 1)

        def link(eng, name, ins):
            links[name] += 1
            ins.then_inc(chain[name], 1)
            eng.wait_ge(chain[name], links[name])

        @block.tensor
        def _(pe):
            mm = nc.tensor.matmul
            tr = nc.tensor.transpose

            def claim(ring, key):
                buf, turn = uses[ring] % 2, uses[ring] // 2
                uses[ring] += 1
                assert key not in at, key
                at[key] = (ring, buf, turn)
                if turn:
                    pe.wait_ge(FREE[ring][buf], turn)
                return RING[ring][buf]

            def full(key):
                return FULL[at[key][0]][at[key][1]]

            def xt(stage, b):
                pe.wait_ge(xh_ready, stage * B + b + 1)
                ps = claim("C", ("xT", stage, b))
                for q in range(QT):
                    last = tr(ps[:, q * P:(q + 1) * P], xh[:, b, q, :], ident[:, :])
                last.then_inc(full(("xT", stage, b)), 1)

            def first():
                pe.wait_ge(consts, 2)
                pe.wait_ge(W["ctx"], 32)
                ps = claim("T", "ctxT")
                for b in range(B):
                    tr(ps[0:C, b * T:b * T + P], ctxm[:, b, :], ident[:, :])
                    last = tr(ps[0:C, b * T + P:(b + 1) * T], ctxr[0:R, b, :], ident[0:R, 0:R])
                last.then_inc(full("ctxT"), 1)
                pe.wait_ge(W["rows"], 16 * 8)
                ps = claim("C", "cols")
                tr(ps[:, 0:15], rows[0:15, :], ident[0:15, 0:15]).then_inc(full("cols"), 1)
                pe.wait_ge(W["gate"], 16)
                ps = claim("C", "gateT")
                tr(ps[:, 0:E], gwr[:, :], ident[0:E, 0:E]).then_inc(full("gateT"), 1)

            def mask_rows():
                pe.wait_ge(mask_ready, 2)
                for part in range(2):
                    ps = claim("C", ("maskT", part))
                    for q in range(QT):
                        src = maskb[:, q, 0:P] if part == 0 else maskr[:, q, :, :].rearrange("p s k -> p (s k)")
                        last = tr(ps[:, q * 64:(q + 1) * 64].bitcast(BF16), src, identb[:, :])
                    last.then_inc(full(("maskT", part)), 1)

            def prework(a):
                n = a.n
                pe.wait_ge(W[f"Wq{n}"], 16)
                for c0 in range(0, a.H // 2, 4):
                    ps = claim("T", ("wqT", n, c0))
                    for c in range(c0, c0 + 4):
                        last = tr(ps[:, (c - c0) * P:(c - c0 + 1) * P], a.Wq[:, c * P:(c + 1) * P], ident[:, :])
                    last.then_inc(full(("wqT", n, c0)), 1)
                pe.wait_ge(W[f"Wk{n}"], 16)
                taken(pe, "ctxT")
                for c in range(a.H // 2):
                    ps = claim("C", ("kT", n, c))
                    mm(ps[:, 0:B * T], a.Wk[:, c * P:(c + 1) * P], ctxT[:, :, :].rearrange("c b k -> c (b k)"),
                       start=True, stop=True).then_inc(full(("kT", n, c)), 1)
                for h in range(a.H):
                    c, r = h // 2, DH * (h % 2)
                    taken(pe, ("wqT", n, c // 4 * 4))
                    taken(pe, ("kT", n, c))
                    ps = claim("T", ("kp", n, h))
                    mm(ps[:, 0:B * T], a.WqT[r:r + DH, c, :], a.KT[r:r + DH, c, :, :].rearrange("p b k -> p (b k)"),
                       start=True, stop=True).then_inc(full(("kp", n, h)), 1)
                pe.wait_ge(W[f"Wv{n}"], 16)
                for b in range(B):
                    for h0 in range(0, a.H, 8):
                        ps = claim("S", ("v", n, b, h0))
                        w = a.Wv[:, h0 * DH:(h0 + 8) * DH]
                        mm(ps[:, 0:512], ctxT[:, b, 0:P], w, start=True, stop=True)
                        mm(ps[:, 512:1024], ctxR[:, b, :], w, start=True, stop=True)\
                            .then_inc(full(("v", n, b, h0)), 1)

            def cross(a):
                n, uu = a.n, units[a.n]

                def scores(u):
                    b, g = uu[u]
                    if g == 0:
                        xt(2 * n, b)
                        taken(pe, ("xT", 2 * n, b))
                    taken(pe, ("kp", n, G4 * g + 2))
                    taken(pe, ("kp", n, G4 * g + 3))
                    for q in range(QT):
                        ps = claim("S", ("s", n, u, q))
                        for i in range(2):
                            last = mm(ps[:, 512 * i:512 * i + 2 * T], xT[:, b, q * P:(q + 1) * P],
                                      a.KP[:, b, G4 * g + 2 * i:G4 * g + 2 * i + 2, :].rearrange("p h k -> p (h k)"),
                                      start=True, stop=(n == 1))
                            if n == 0:
                                for j in range(2):
                                    last = mm(ps[:, 512 * i + j * T:512 * i + (j + 1) * T], identb[:, :],
                                              maskb[:, q, :], start=False, stop=(j == 1))
                        last.then_inc(full(("s", n, u, q)), 1)

                def maxima(u):
                    pe.wait_ge(mp_ready, before[n] + u + 1)
                    ps = claim("C", ("mT", n, u))
                    for q in range(QT):
                        last = tr(ps[0:8, q * 64:(q + 1) * 64].bitcast(BF16),
                                  mparts[:, u % 2, q, :, :].rearrange("p a h -> p (a h)"), identb[:, :])
                    last.then_inc(full(("mT", n, u)), 1)

                def scoresT(u):
                    b, g = uu[u]
                    if n == 0 and u == 0:
                        taken(pe, ("maskT", 1))
                        taken(pe, ("maskT", 0))
                    for j in range(G4 + 1):
                        ps = claim("T", ("st", n, u, j))
                        w = a.KP[:, b, G4 * g + j, 0:P] if j < G4 else a.KR[:, b, g, :, :].rearrange("p h k -> p (h k)")
                        mm(ps[:, :], w, xT[:, b, :], start=True, stop=False)
                        if n == 0:
                            mm(ps[:, :], identb[:, :], maskT[:, int(j == G4), :], start=False, stop=False)
                        if j == 0:
                            taken(pe, ("mT", n, u))
                        mm(ps[:, :], selm[:, j, :], mT[:, u % 2, :], start=False, stop=True)\
                            .then_inc(full(("st", n, u, j)), 1)

                def values(u):
                    b, g = uu[u]
                    taken(pe, ("st", n, u, 4))
                    taken(pe, ("v", n, b, G4 * g // 8 * 8))
                    for q in range(QT):
                        ps = claim("C", ("pv", n, u, q))
                        for j in range(G4 + 1):
                            if j < G4:
                                o, v = ps[:, j * (DH + 1):(j + 1) * (DH + 1)], a.VA[:, b, G4 * g + j, :]
                            else:
                                o, v = ps[:, 0:G4 * (DH + 1)], a.VR[:, b, g, :, :].rearrange("p h d -> p (h d)")
                            last = mm(o, PT[:, 5 * (u % 2) + j, q * P:(q + 1) * P], v,
                                      start=(j == 0), stop=(j == G4), skip_group_check=True)
                        last.then_inc(full(("pv", n, u, q)), 1)

                def outT(u):
                    taken(pe, ("pv", n, u, QT - 1))
                    for c in range(2):
                        ps = claim("C", ("oT", n, u, c))
                        for q in range(QT):
                            last = tr(ps[:, q * P:(q + 1) * P], Ou[:, u % 2, q, c * P:(c + 1) * P], ident[:, :])
                        last.then_inc(full(("oT", n, u, c)), 1)

                def project(u):
                    b, g = uu[u]
                    pe.wait_ge(W[f"Wo{n}"], 16)
                    taken(pe, ("oT", n, u, 1))
                    for q in range(QT):
                        ps = claim("C", ("proj", n, b, q))
                        for c in range(a.H // 2):
                            last = mm(ps[:, 0:D], OT[:, c, q * P:(q + 1) * P], a.Wo[:, c, :],
                                      start=(c == 0), stop=(c == a.H // 2 - 1))
                        last.then_inc(full(("proj", n, b, q)), 1)

                scores(0)
                for u in range(len(uu)):
                    if u + 1 < len(uu):
                        scores(u + 1)
                    maxima(u)
                    scoresT(u)
                    if u:
                        outT(u - 1)
                        if uu[u - 1][1] == a.G - 1:
                            project(u - 1)
                    values(u)
                outT(len(uu) - 1)
                project(len(uu) - 1)

            def ffn(n, b):
                taken(pe, ("xT", 1 + 3 * n, b))
                if n == 0:
                    taken(pe, "gateT")
                else:
                    pe.wait_ge(W["Wg"], 16)
                ps = claim("C", ("gate", n, b))
                for q in range(QT):
                    last = mm(ps[:, q * E:(q + 1) * E], xT[:, b, q * P:(q + 1) * P],
                              gateT[:, :] if n == 0 else Wg[:, :], start=True, stop=True)
                last.then_inc(full(("gate", n, b)), 1)
                if n == 0:
                    pe.wait_ge(W["upw"], 32)
                else:
                    pe.wait_ge(W["W1"], 16)
                ups = E + 1 if n == 0 else E // 2
                for e in range(ups):
                    ps = claim("T", ("up", n, b, e))
                    w = upw[:, e, :] if n == 0 else W1[:, 2 * e:2 * e + 2, :].rearrange("p e h -> p (e h)")
                    mm(ps[:, :], w, xT[:, b, :], start=True, stop=True).then_inc(full(("up", n, b, e)), 1)
                if n == 0:
                    pe.wait_ge(comb_ready, b + 1)
                    ps = claim("C", ("combT", b))
                    for q in range(QT):
                        last = tr(ps[0:E, q * P:(q + 1) * P], comb[:, b, q, :], ident[:, :])
                    last.then_inc(full(("combT", b)), 1)
                    pe.wait_ge(W["dnw"], 48)
                    taken(pe, ("combT", b))
                else:
                    pe.wait_ge(W["W2"], 16)
                taken(pe, ("up", n, b, ups - 1))
                for q in range(QT):
                    ps = claim("S", ("dn", n, b, q))
                    for e in range(E):
                        place = e if n == 0 else E // 2 * (e % 2) + e // 2
                        o = ps[:, place * D:(place + 1) * D]
                        if n == 0:
                            last = mm(o, HT[:, e, q * P:(q + 1) * P], dnw[:, e, :], start=True, stop=True)
                        else:
                            r = EH * (e % 2)
                            last = mm(o, HT[r:r + EH, e // 2, q * P:(q + 1) * P], W2[r:r + EH, e // 2, :],
                                      start=True, stop=True)
                    last.then_inc(full(("dn", n, b, q)), 1)
                    if n == 0:
                        ps = claim("C", ("sh", b, q))
                        mm(ps[:, 0:D], HT[:, E, q * P:(q + 1) * P], dnw[:, E, :], start=True, stop=False)
                        mm(ps[:, 0:D], combT[:, q * P:(q + 1) * P], dnb[:, :], start=False, stop=True)\
                            .then_inc(full(("sh", b, q)), 1)

            def self_in(b):
                pe.wait_ge(W["Ws"], 64)
                xt(3, b)
                taken(pe, ("xT", 3, b))
                for i in range(2):
                    ps = claim("C", ("qk", b, i))
                    mm(ps[:, :], Ws[:, i, :], xT[:, b, :], start=True, stop=True).then_inc(full(("qk", b, i)), 1)
                ps = claim("C", ("vs", b))
                for q in range(QT):
                    last = mm(ps[:, q * D:(q + 1) * D], xT[:, b, q * P:(q + 1) * P], Ws[:, 2, :],
                              start=True, stop=True)
                last.then_inc(full(("vs", b)), 1)

            def self_attention():
                uu = units[2]

                def strip(side, b, h, s, n_rows):
                    r = 64 * (h % 2)
                    return stack[b][side][r:r + n_rows, h // 2, s]

                def score_pair(u, k):
                    b, g = uu[u]
                    if g == 0 and k == 0:
                        pe.wait_ge(stacked, 16 * 24 * (b + 1))
                    q = k // 2
                    ps = claim("S", ("ss", u, k))
                    for i in range(2):
                        h = G4 * g + 2 * (k % 2) + i
                        last = mm(ps[:, 512 * i:512 * i + 512], strip(0, b, h, slice(q * P, (q + 1) * P), 48),
                                  strip(1, b, h, slice(0, S), 48), start=True, stop=True)
                    last.then_inc(full(("ss", u, k)), 1)

                def values(u, kt, pv):
                    b, g = uu[u]
                    taken(pe, ("sst", u, kt, G4 - 1))
                    for j in range(G4):
                        last = mm(pv[STRIP * j:STRIP * (j + 1), :], VS[b][:, kt, G4 * g + j, :],
                                  PT[:, (4 * kt + j) % NPT, :], start=(kt == 0), stop=(kt == QT - 1))
                    last.then_inc(full(("spv", u)) if kt == QT - 1 else p_used, 1)

                self_in(0)
                for k in range(8):
                    score_pair(0, k)
                for u in range(len(uu)):
                    b, g = uu[u]
                    pe.wait_ge(mp_ready, before[2] + u + 1)
                    ps = claim("C", ("smT", u))
                    for q in range(QT):
                        last = tr(ps[0:8, q * 64:(q + 1) * 64].bitcast(BF16),
                                  mparts[:, u % 2, q, :, :].rearrange("p a h -> p (a h)"), identb[:, :])
                    last.then_inc(full(("smT", u)), 1)
                    if u == 0:
                        self_in(1)
                    more = list(range(8)) if u + 1 < len(uu) else []
                    for k in more[0:3]:
                        score_pair(u + 1, k)
                    if u == 0 or g == 0:
                        taken(pe, ("vs", b))
                    pe.wait_ge(mrow_ready, 16 * 4 * (u + 1))
                    for kt in range(QT):
                        for j in range(G4):
                            h = G4 * g + j
                            ps = claim("T", ("sst", u, kt, j))
                            mm(ps[:, :], strip(1, b, h, slice(kt * P, (kt + 1) * P), 50),
                               strip(0, b, h, slice(0, S), 50), start=True, stop=True)\
                                .then_inc(full(("sst", u, kt, j)), 1)
                            if j == 1 and more[3 + 2 * kt:4 + 2 * kt]:
                                score_pair(u + 1, more[3 + 2 * kt])
                        if kt == 0:
                            pv = claim("C", ("spv", u))
                        else:
                            values(u, kt - 1, pv)
                        if more[4 + 2 * kt:5 + 2 * kt]:
                            score_pair(u + 1, more[4 + 2 * kt])
                    values(u, QT - 1, pv)
                    taken(pe, ("spv", u))
                    ps = claim("C", ("sO", u))
                    for q in range(QT):
                        last = tr(ps[:, q * P:(q + 1) * P], OS[:, u % 2, q * P:(q + 1) * P], ident[:, :])
                    last.then_inc(full(("sO", u)), 1)
                    if g == HS // G4 - 1:
                        taken(pe, ("sO", u))
                        ps = claim("C", ("onT", b))
                        for q in range(QT):
                            last = tr(ps[:, q * P:(q + 1) * P], On[:, q, :, :].rearrange("p h d -> p (h d)"),
                                      ident[:, :])
                        last.then_inc(full(("onT", b)), 1)
                        taken(pe, ("onT", b))
                        ps = claim("C", ("sproj", b))
                        for q in range(QT):
                            last = mm(ps[:, q * D:(q + 1) * D], OT[:, b, q * P:(q + 1) * P], Ws[:, 3, :],
                                      start=True, stop=True)
                        last.then_inc(full(("sproj", b)), 1)

            first()
            mask_rows()
            prework(xa[0])
            cross(xa[0])
            if stop >= 2:
                prework(xa[1])
                for b in range(B):
                    xt(1, b)
                    ffn(0, b)
            if stop >= 3:
                cross(xa[1])
            if stop >= 4:
                self_attention()
                for b in range(B):
                    xt(4, b)
                    ffn(1, b)

        @block.scalar
        def _(act):
            A = nc.scalar
            cp = A.copy

            def xt(stage, b):
                ps = filled(act, ("xT", stage, b))
                if stage in (0, 3, 4):
                    c = {0: 0, 3: 2, 4: 4}[stage]
                    if (stage, b) == (0, 0):
                        taken(act, "cols")
                    A.activation(xT[:, b, :], ps[:, :], ACT.Identity, bias=cols[:, c + 1:c + 2],
                                 scale=cols[:, c:c + 1]).then_inc(freed(("xT", stage, b)), 1)
                else:
                    cp(xT[:, b, :], ps[:, :]).then_inc(freed(("xT", stage, b)), 1)

            def prework(a):
                n = a.n
                for c in range(a.H // 2):
                    ps = filled(act, ("kT", n, c))
                    cp(a.KT[:, c, :, :].rearrange("p b k -> p (b k)"), ps[:, 0:B * T])\
                        .then_inc(freed(("kT", n, c)), 1)
                for h in range(0, a.H, 2):
                    ps = filled(act, ("kp", n, h))
                    v = ps[:, 0:B * T].rearrange("p (b k) -> p b k", b=B)
                    cp(a.KP[:, :, h, :], v)
                    cp(a.KR[:, :, h // G4, h % G4, 0:R], v[:, :, P:T]).then_inc(freed(("kp", n, h)), 1)

            def cross(a):
                n, uu = a.n, units[a.n]

                def outT(u):
                    b, g = uu[u]
                    for c in range(2):
                        ps = filled(act, ("oT", n, u, c))
                        cp(OT[:, 2 * g + c, :], ps[:, :]).then_inc(freed(("oT", n, u, c)), 1)

                xt(2 * n, 0)
                for u in range(len(uu)):
                    b, g = uu[u]
                    if u + 1 < len(uu) and uu[u + 1][1] == 0:
                        xt(2 * n, uu[u + 1][0])
                    ps = filled(act, ("mT", n, u))
                    cp(mT[:, u % 2, :], ps[0:8, 0:256].bitcast(BF16)).then_inc(freed(("mT", n, u)), 1)
                    if u >= 2:
                        filled(act, ("pv", n, u - 2, QT - 1))
                    for j in range(G4 + 1):
                        ps = filled(act, ("st", n, u, j))
                        A.activation(PT[:, 5 * (u % 2) + j, :], ps[:, :], ACT.Exp, scale=XSCALE)\
                            .then_inc(freed(("st", n, u, j)), 1)
                    if u:
                        outT(u - 1)
                outT(len(uu) - 1)

            def ffn(n, b):
                act.wait_ge(lg_ready, B * n + b + 1)
                A.activation(ex[:, b, :, :], ex[:, b, :, :], ACT.Exp).then_inc(ex_ready, 1)
                for e in range(E + 1 if n == 0 else E // 2):
                    ps = filled(act, ("up", n, b, e))
                    if n == 0:
                        A.activation(HT[:, e, :], ps[:, :], ACT.Silu, bias=cols[:, 6 + e:7 + e])\
                            .then_inc(freed(("up", n, b, e)), 1)
                    else:
                        A.activation(HT[:, e, :], ps[:, :], ACT.Relu).then_inc(freed(("up", n, b, e)), 1)
                if n == 0:
                    ps = filled(act, ("combT", b))
                    cp(combT[:, :], ps[0:E, :]).then_inc(freed(("combT", b)), 1)

            def self_attention():
                uu = units[2]

                def self_in(b):
                    xt(3, b)
                    for i in range(2):
                        pass
                    ps = filled(act, ("vs", b))
                    act.wait_ge(pads_ready, b + 1)
                    cp(VS[b][:, :, :, 0:DS], ps[:, :].rearrange("p (q h d) -> p q h d", q=QT, h=HS))\
                        .then_inc(freed(("vs", b)), 1)

                self_in(0)
                for u in range(len(uu)):
                    b, g = uu[u]
                    ps = filled(act, ("smT", u))
                    if u >= 2:
                        act.wait_ge(mrow_ready, 16 * 4 * (u - 1))
                    cp(mT[:, u % 2, :], ps[0:8, 0:256].bitcast(BF16)).then_inc(freed(("smT", u)), 1)
                    if u == 0:
                        self_in(1)
                    for kt in range(QT):
                        if u:
                            if kt < QT - 1:
                                act.wait_ge(p_used, 3 * (u - 1) + kt + 1)
                            else:
                                filled(act, ("spv", u - 1))
                        for j in range(G4):
                            ps = filled(act, ("sst", u, kt, j))
                            A.activation(PT[:, 4 * kt + j, :], ps[:, :], ACT.Exp, scale=SSCALE)\
                                .then_inc(freed(("sst", u, kt, j)), 1)
                    ps = filled(act, ("spv", u))
                    cp(OS[:, u % 2, :], ps[:, :]).then_inc(freed(("spv", u)), 1)
                    if g == HS // G4 - 1:
                        ps = filled(act, ("onT", b))
                        cp(OT[:, b, :], ps[:, :]).then_inc(freed(("onT", b)), 1)

            act.dma_start(ctxm[:, :, :], t["ctx_768"][:, 0:P, :].rearrange("b k c -> k b c")).then_inc(W["ctx"], 16)
            act.dma_start(ctxr[0:R, :, :], t["ctx_768"][:, P:T, :].rearrange("b k c -> k b c")).then_inc(W["ctx"], 16)
            act.dma_start(xa[0].Wk[:, :], t["L0_xattn_Wkv"][:, 0:H0 * DH]).then_inc(W["Wk0"], 16)
            act.dma_start(xa[0].Wv[:, :], t["L0_xattn_Wkv"][:, H0 * DH:2 * H0 * DH]).then_inc(W["Wv0"], 16)
            ps = filled(act, "ctxT")
            cp(ctxT[:, :, :].rearrange("c b k -> c (b k)"), ps[0:C, 0:B * T])
            for s in range(G4):
                last = cp(ctxR[:, :, s * STRIP:s * STRIP + R],
                          ps[0:C, 0:B * T].rearrange("c (b k) -> c b k", b=B)[:, :, P:T])
            last.then_inc(freed("ctxT"), 1)
            ps = filled(act, "cols")
            cp(cols[:, 0:15], ps[:, 0:15]).then_inc(freed("cols"), 1)
            ps = filled(act, "gateT")
            cp(gateT[:, :], ps[:, 0:E]).then_inc(freed("gateT"), 1)
            for part in range(2):
                ps = filled(act, ("maskT", part))
                cp(maskT[:, part, :], ps[:, 0:256].bitcast(BF16)).then_inc(freed(("maskT", part)), 1)
            prework(xa[0])
            cross(xa[0])
            if stop >= 2:
                prework(xa[1])
                for b in range(B):
                    xt(1, b)
                    ffn(0, b)
            if stop >= 3:
                cross(xa[1])
            if stop >= 4:
                self_attention()
                for b in range(B):
                    xt(4, b)
                    ffn(1, b)

        @block.vector
        def _(dve):
            V = nc.vector
            tt = V.tensor_tensor

            def seq(ins):
                link(dve, "dve", ins)

            def norm(stage, b):
                src = y if stage == 4 else x
                if stage == 0:
                    dve.wait_ge(W["x"], 16 * (b + 1))
                for q in range(QT):
                    ins = V.bn_stats(stats[:, b, q, :], src[:, b, q, :])
                seq(ins)
                for q in range(QT):
                    ins = V.bn_aggr(mv[:, b, q, :], stats[:, b, q, :])
                ins.then_inc(stats_ready, 1)
                dve.wait_ge(rstd_ready, B * stage + b + 1)
                r = r2 if stage == 0 else rstd
                for q in range(QT):
                    dst = y if stage == 3 else xh
                    ins = V.tensor_scalar(dst[:, b, q, :], src[:, b, q, :], mv[:, b, q, 0:1], r[:, b, q:q + 1],
                                          ALU.subtract, ALU.mult)
                if stage == 3:
                    seq(ins)
                    ins = tt(xh[:, b, :, :], y[:, b, :, :],
                             r2[:, b, :].unsqueeze(2).broadcast_to([P, QT, D]), ALU.mult)
                ins.then_inc(xh_ready, 1)

            def prework(a):
                n = a.n
                for c0 in range(0, a.H // 2, 4):
                    ps = filled(dve, ("wqT", n, c0))
                    V.tensor_copy(a.WqT[:, c0:c0 + 4, :].rearrange("p c k -> p (c k)"), ps[:, :])\
                        .then_inc(freed(("wqT", n, c0)), 1)
                for h in range(1, a.H, 2):
                    ps = filled(dve, ("kp", n, h))
                    v = ps[:, 0:B * T].rearrange("p (b k) -> p b k", b=B)
                    V.tensor_copy(a.KP[:, :, h, :], v)
                    if h == 1:
                        dve.wait_ge(consts, 2)
                    V.tensor_copy(a.KR[:, :, h // G4, h % G4, 0:R], v[:, :, P:T])\
                        .then_inc(freed(("kp", n, h)), 1)
                for b in range(B):
                    for h0 in range(0, a.H, 8):
                        ps = filled(dve, ("v", n, b, h0))
                        V.tensor_copy(a.VA[:, b, h0:h0 + 8, 0:DH],
                                      ps[:, 0:512].rearrange("p (h d) -> p h d", h=8))
                        for j in range(G4):
                            r = slice(STRIP * j, STRIP * (j + 1))
                            ins = V.tensor_copy(
                                a.VR[r, b, h0 // G4:h0 // G4 + 2, j, 0:DH],
                                ps[r, 512:1024].rearrange("p (g j d) -> p g j d", g=2, j=G4)[:, :, j, :])
                        ins.then_inc(freed(("v", n, b, h0)), 1)

            def parts(n, u):
                m, r = mx[:, u % 2, :, :], mr[:, u % 2, :, :]
                hi, lo = (mparts[:, u % 2, :, a, :] for a in range(2))
                seq(V.tensor_copy(hi, m))
                seq(tt(r, m, hi, ALU.subtract))
                V.tensor_copy(lo, r).then_inc(mp_ready, 1)

            def cross(a):
                n, uu = a.n, units[a.n]

                def maxima(u):
                    for q in range(QT):
                        ps = filled(dve, ("s", n, u, q))
                        V.tensor_reduce(mx[:, u % 2, q, :],
                                        ps[:, :].rearrange("p (i k) -> p i k", i=2)[:, :, 0:2 * T].rearrange(
                                            "p i (j k) -> p i j k", j=2), AX.X, ALU.max)\
                            .then_inc(freed(("s", n, u, q)), 1)
                    taken(dve, ("s", n, u, QT - 1))
                    parts(n, u)

                def outputs(u):
                    for q in range(QT):
                        ps = filled(dve, ("pv", n, u, q))
                        v = ps[:, 0:G4 * (DH + 1)].rearrange("p (h d) -> p h d", h=G4)
                        z = rz[:, u % 2, q, :]
                        seq(V.reciprocal(z, v[:, :, DH]))
                        if n == 0:
                            seq(tt(z, z, allow[:, q, 2:3].broadcast_to([P, G4]), ALU.add))
                        tt(Ou[:, u % 2, q, :].rearrange("p (h d) -> p h d", h=G4), v[:, :, 0:DH],
                           z.unsqueeze(2).broadcast_to([P, G4, DH]), ALU.mult).then_inc(freed(("pv", n, u, q)), 1)

                def project(b):
                    dve.wait_ge(xb_ready, B * 2 * n + b + 1)
                    for q in range(QT):
                        ps = filled(dve, ("proj", n, b, q))
                        tt(x[:, b, q, :], ps[:, 0:D], x[:, b, q, :], ALU.add).then_inc(freed(("proj", n, b, q)), 1)
                    taken(dve, ("proj", n, b, QT - 1))
                    if stop > 1 + 2 * n:
                        norm(2 * n + 1, b)

                maxima(0)
                for u in range(len(uu)):
                    if u + 1 < len(uu):
                        maxima(u + 1)
                    if u and uu[u - 1][1] == a.G - 1:
                        project(uu[u - 1][0])
                    outputs(u)
                project(B - 1)

            def gate(n, b):
                l, e_, m, z = lg[:, b, :, :], ex[:, b, :, :], g1[:, b, :, 0:1], g1[:, b, :, 1:2]
                wide = [P, QT, E]
                ps = filled(dve, ("gate", n, b))
                V.tensor_copy(l.rearrange("p q e -> p (q e)"), ps[:, 0:QT * E]).then_inc(freed(("gate", n, b)), 1)
                taken(dve, ("gate", n, b))
                seq(V.tensor_reduce(g1[:, b, :, 0], l, AX.X, ALU.max))
                tt(e_, l, m.broadcast_to(wide), ALU.subtract).then_inc(lg_ready, 1)
                dve.wait_ge(ex_ready, B * n + b + 1)
                if n == 0:
                    seq(V.tensor_reduce(g1[:, b, :, 1], e_, AX.X, ALU.add))
                    seq(V.reciprocal(g1[:, b, :, 1], g1[:, b, :, 1]))
                    seq(tt(e_, e_, z.broadcast_to(wide), ALU.mult))
                    ranked = ex
                else:
                    ranked = lg
                for q in range(QT):
                    seq(V.max(top[:, b, q, :], ranked[:, b, q, :]))
                    seq(V.max_index(topi[:, b, q, :], top[:, b, q, :], ranked[:, b, q, :]))
                seq(V.tensor_copy(topf[:, b, :, :], topi[:, b, :, :]))
                for k in range(2):
                    ins = tt(oh[:, b, :, k, :], iota[:, :].unsqueeze(1).broadcast_to(wide),
                             topf[:, b, :, k:k + 1].broadcast_to(wide), ALU.is_equal)
                    seq(ins)
                seq(tt(oh[:, b, :, 0, :], oh[:, b, :, 0, :], oh[:, b, :, 1, :], ALU.add))
                c = comb[:, b, :, :]
                seq(tt(c, e_, oh[:, b, :, 0, :], ALU.mult))
                seq(V.tensor_reduce(g1[:, b, :, 2], c, AX.X, ALU.add))
                if n == 0:
                    seq(V.tensor_scalar(g1[:, b, :, 2], g1[:, b, :, 2], 1e-20, None, ALU.add))
                seq(V.reciprocal(g1[:, b, :, 3], g1[:, b, :, 2]))
                ins = tt(c, c, g1[:, b, :, 3:4].broadcast_to(wide), ALU.mult)
                if n == 0:
                    ins.then_inc(comb_ready, 1)
                    dve.wait_ge(comb_ready, b + 1)
                else:
                    seq(ins)

            def ffn(n, b):
                gate(n, b)
                for q in range(QT):
                    w = wy[:, q % 2, :, :]
                    ps = filled(dve, ("dn", n, b, q))
                    c = comb[:, b, q, :].rearrange("p (i c) -> p i c" if n == 0 else "p (c i) -> p i c", i=2)
                    tt(w.rearrange("p (i c) d -> p i c d", i=2),
                       ps[:, :].rearrange("p (i c d) -> p i c d", i=2, c=E // 2),
                       c.unsqueeze(3).broadcast_to([P, 2, E // 2, D]), ALU.mult)\
                        .then_inc(freed(("dn", n, b, q)), 1)
                    taken(dve, ("dn", n, b, q))
                    seq(V.tensor_reduce(wys[:, q % 2, :], w.rearrange("p e d -> p d e"), AX.X, ALU.add))
                    if n == 0:
                        ps = filled(dve, ("sh", b, q))
                        tt(wys[:, q % 2, :], wys[:, q % 2, :], ps[:, 0:D], ALU.add).then_inc(freed(("sh", b, q)), 1)
                        taken(dve, ("sh", b, q))
                    if q == 0:
                        dve.wait_ge(xb_ready, B * (1 + 2 * n) + b + 1)
                    tt(x[:, b, q, :], x[:, b, q, :], wys[:, q % 2, :], ALU.add).then_inc(x_ready, 1)
                dve.wait_ge(x_ready, QT * (B * n + b + 1))

            def self_attention():
                uu = units[2]

                def self_in(b):
                    for i in range(2):
                        ps = filled(dve, ("qk", b, i))
                        if b:
                            dve.wait_ge(parked, 16 * 3 * (i + 1))
                        p1, p2, p3 = (z[:, :] for z in qk[i])
                        V.tensor_copy(p1, ps[:, :]).then_inc(part_ready, 1)
                        dve.wait_ge(part_ready, 3 * (2 * b + i) + 1)
                        tt(qkr[:, i, :], ps[:, :], p1, ALU.subtract).then_inc(freed(("qk", b, i)), 1)
                        taken(dve, ("qk", b, i))
                        V.tensor_copy(p2, qkr[:, i, :]).then_inc(part_ready, 1)
                        dve.wait_ge(part_ready, 3 * (2 * b + i) + 2)
                        tt(p3, qkr[:, i, :], p2, ALU.subtract).then_inc(part_ready, 1)

                def maxima(u):
                    for k in range(8):
                        ps = filled(dve, ("ss", u, k))
                        j = 2 * (k % 2)
                        V.tensor_reduce(mx[:, u % 2, k // 2, j:j + 2], ps[:, :].rearrange("p (i k) -> p i k", i=2),
                                        AX.X, ALU.max).then_inc(freed(("ss", u, k)), 1)
                    taken(dve, ("ss", u, 7))
                    parts(2, u)

                self_in(0)
                maxima(0)
                self_in(1)
                for u in range(len(uu)):
                    b, g = uu[u]
                    if u + 1 < len(uu):
                        maxima(u + 1)
                    ps = filled(dve, ("sO", u))
                    v = ps[:, :].rearrange("p (q j d) -> p q j d", q=QT, j=G4)
                    z = zs[:, u % 2, :, :]
                    seq(V.reciprocal(z, v[:, :, :, DS]))
                    tt(On[:, :, G4 * g:G4 * (g + 1), :], v[:, :, :, 0:DS],
                       z.unsqueeze(3).broadcast_to([P, QT, G4, DS]), ALU.mult).then_inc(freed(("sO", u)), 1)
                    if g == HS // G4 - 1:
                        ps = filled(dve, ("sproj", b))
                        tt(y[:, b, :, :].rearrange("p q d -> p (q d)"), ps[:, :],
                           y[:, b, :, :].rearrange("p q d -> p (q d)"), ALU.add).then_inc(freed(("sproj", b)), 1)
                        taken(dve, ("sproj", b))
                        norm(4, b)

            dve.wait_ge(W["mask"], 16)
            dve.wait_ge(consts, 2)
            seq(V.tensor_scalar(maskb[:, :, :], masku[:, :, :], -BLOCKED, BLOCKED, ALU.mult, ALU.add))
            dve.wait_ge(W["mask"], 16)
            V.tensor_copy(maskr[:, :, :, 0:R], maskb[:, :, P:T].unsqueeze(2).broadcast_to([P, QT, G4, R]))\
                .then_inc(mask_ready, 2)
            norm(0, 0)
            norm(0, 1)
            seq(V.tensor_copy(maskf[:, :, :], masku[:, :, :]))
            seq(V.tensor_reduce(allow[:, :, 0], maskf[:, :, :], AX.X, ALU.add))
            seq(V.reciprocal(allow[:, :, 1], allow[:, :, 0]))
            seq(V.tensor_scalar(allow[:, :, 2], allow[:, :, 1], 0.0, None, ALU.mult))
            prework(xa[0])
            cross(xa[0])
            if stop >= 2:
                prework(xa[1])
                for b in range(B):
                    ffn(0, b)
                    if stop >= 3:
                        norm(2, b)
            if stop >= 3:
                cross(xa[1])
            if stop >= 4:
                self_attention()
                for b in range(B):
                    ffn(1, b)

        @block.gpsimd
        def _(pool):
            G = nc.gpsimd

            def seq(ins):
                link(pool, "pool", ins)

            for m in (ident, identb):
                G.memset(m[:, :], 0.0)
            G.memset(selm[:, :, :], 0.0)
            seq(G.memset(mhalf[:, :], -0.5))
            for m in (ident, identb):
                last = G.affine_select(out=m[:, :], in_=m[:, :], compare_op=ALU.not_equal, fill=1.0, base=0,
                                       pattern=[[-1, P]], channel_multiplier=1)
            for part in range(2):
                o = selm[:, 0:G4, :]
                G.affine_select(out=o, in_=o, compare_op=ALU.not_equal, fill=-1.0, base=-G4 * part,
                                pattern=[[-1, G4], [0, P]], channel_multiplier=1)
                o = selm[:, G4, :].rearrange("p (s k) -> p s k", s=G4)[:, :, 0:R]
                seq(G.affine_select(out=o, in_=o, compare_op=ALU.not_equal, fill=-1.0, base=-G4 * part,
                                    pattern=[[-1, G4], [0, R]], channel_multiplier=1))
            G.memset(ctxR[:, :, :], 0.0)
            G.memset(maskr[:, :, :, :], 0.0)
            for a in xa:
                G.memset(a.KR[:, :, :, :, :], 0.0)
                G.memset(a.VA[:, :, :, DH:DH + 1], 1.0)
                seq(G.memset(a.VR[:, :, :, :, :], 0.0))
                for j in range(G4):
                    seq(G.memset(a.VR[STRIP * j:STRIP * j + R, :, :, j, DH:DH + 1], 1.0))
            G.iota(iotai[:, :], pattern=[[1, E]], base=0, channel_multiplier=0).then_inc(consts, 1)
            pool.wait_ge(consts, 1)
            G.tensor_copy(iota[:, :], iotai[:, :]).then_inc(consts, 1)

            def norm(stage, b):
                pool.wait_ge(stats_ready, B * stage + b + 1)
                half = mhalf[:, 0:QT]
                twice = stage in (0, 3)
                seq(G.tensor_scalar(ve[:, b, :], mv[:, b, :, 1], EPS, None, ALU.add))
                ins = G.tensor_tensor(rstd[:, b, :], ve[:, b, :], half, ALU.pow)
                if twice:
                    seq(ins)
                    seq(G.tensor_tensor(v2[:, b, :], mv[:, b, :, 1], rstd[:, b, :], ALU.mult))
                    seq(G.tensor_tensor(v2[:, b, :], v2[:, b, :], rstd[:, b, :], ALU.mult))
                    seq(G.tensor_scalar(v2[:, b, :], v2[:, b, :], EPS, None, ALU.add))
                    ins = G.tensor_tensor(r2[:, b, :], v2[:, b, :], half, ALU.pow)
                    if stage == 0:
                        seq(ins)
                        ins = G.tensor_tensor(r2[:, b, :], r2[:, b, :], rstd[:, b, :], ALU.mult)
                ins.then_inc(rstd_ready, 1)

            def add_bias(stage, b):
                pool.wait_ge(xh_ready, B * stage + b + 1)
                if stage == 0 and b == 0:
                    pool.wait_ge(W["bo"], 48)
                o = x[:, b, :, :]
                G.tensor_tensor(o, o, bo[:, stage, :].unsqueeze(1).broadcast_to([P, QT, D]), ALU.add)\
                    .then_inc(xb_ready, 1)

            for stage in range(min(stop, 3)):
                for b in range(B):
                    norm(stage, b)
                    if stage:
                        add_bias(stage, b)
                if stage == 0:
                    for b in range(B):
                        add_bias(0, b)
                if stage == 1 and stop >= 4:
                    pool.wait_ge(xb_ready, B * 2)
                    for b in range(B):
                        for r in (32, 96):
                            seq(G.memset(stack[b][1][r:r + 32, :, :], -1.0))
            if stop >= 4:
                norm(3, 0)
                norm(3, 1)
                pool.wait_ge(rstd_ready, 4 * B)
                for b in range(B):
                    seq(G.memset(VS[b][:, :, :, DS:STRIP], 0.0))
                    G.memset(VS[b][:, :, :, DS:DS + 1], 1.0).then_inc(pads_ready, 1)
                    pool.wait_ge(pads_ready, b + 1)
                for b in range(B):
                    norm(4, b)
                    pool.wait_ge(xh_ready, B * 4 + b + 1)
                    G.tensor_tensor(x[:, b, :, :], x[:, b, :, :], y[:, b, :, :], ALU.add).then_inc(xb_ready, 1)

        @block.sync
        def _(sp):
            def load(dst, src, name):
                sp.dma_start(dst, src).then_inc(W[name], 16)

            def row(v):
                return v.rearrange("(a d) -> a d", a=1)

            for b in range(B):
                load(x[:, b, :, :], t["x"][b].rearrange("(q p) d -> p q d", p=P), "x")
            load(xa[0].Wq[:, :], t["L0_xattn_Wq"], "Wq0")
            load(masku[:, :, :], t["mask_1x1xSxS2_bk0"][0, 0].rearrange("(q p) k -> p q k", p=P), "mask")
            for i, k in enumerate(("L0_xattn_ln_gamma", "L0_xattn_ln_beta", "L1_ffn_g1", "L1_ffn_b1",
                                   "L1_ffn_g2", "L1_ffn_b2")):
                load(rows[i:i + 1, :], row(t[k]), "rows")
            load(rows[6:14, :], t["L0_ffn_up_b"], "rows")
            load(rows[14:15, :], row(t["L0_ffn_sh_up_b"]), "rows")
            load(gwr[:, :], t["L0_ffn_gate_w"], "gate")
            for i, k in enumerate(("L0_xattn_bo", "L0_ffn_sh_down_b", "L1_xattn_bo")):
                load(bo[:, i, :], t[k].partition_broadcast(P), "bo")
            load(xa[0].Wo[:, :, :], t["L0_xattn_Wo"].rearrange("(c p) d -> p c d", p=P), "Wo0")
            load(xa[1].Wq[:, :], t["L1_xattn_Wq"], "Wq1")
            load(xa[1].Wk[:, :], t["L1_xattn_Wk"], "Wk1")
            load(xa[1].Wv[:, :], t["L1_xattn_Wv"], "Wv1")
            load(upw[:, 0:E, :], t["L0_ffn_up_w"].rearrange("e d h -> d e h"), "upw")
            load(upw[:, E, :], t["L0_ffn_sh_up_w"], "upw")
            load(dnw[:, 0:E, :], t["L0_ffn_down_w"].rearrange("e h d -> h e d"), "dnw")
            load(dnw[:, E, :], t["L0_ffn_sh_down_w"], "dnw")
            load(dnb[:, :], t["L0_ffn_down_b"], "dnw")
            load(xa[1].Wo[:, :, :], t["L1_xattn_Wo"].rearrange("(c p) d -> p c d", p=P), "Wo1")
            for i, k in enumerate(("Wq", "Wk", "Wv", "Wo")):
                load(Ws[:, i, :], t[f"L1_ffn_{k}"], "Ws")
            load(Wg[:, :], t["L1_ffn_Wg"], "Wg")
            load(W1[:, :, :], t["L1_ffn_W1"].rearrange("e d h -> d e h"), "W1")
            load(W2[:, :, :], t["L1_ffn_W2"].rearrange("(c i) h d -> (i h) c d", i=2), "W2")

            if stop >= 4:
                SIDES = ((0, 0, 1, 1, 0, 2), (0, 1, 0, 1, 2, 0))

                def fill_stacks(b):
                    for i in range(2):
                        sp.wait_ge(part_ready, 3 * (2 * b + i) + 3)
                        if b == 0 and i == 0:
                            sp.wait_ge(pads_ready, 1)
                        for j in range(3):
                            sp.dma_start(scratch[b, i, j], qk[i][j]).then_inc(parked, 16)
                        sp.wait_ge(parked, 16 * 3 * (2 * b + i + 1))
                        for r in range(6):
                            src = scratch[b, i, SIDES[i][r]].rearrange("(c par d) s -> par d c s", par=2, d=DS)
                            for par in range(2):
                                p0 = 64 * par + DS * r
                                sp.dma_start(stack[b][i][p0:p0 + DS, :, :], src[par]).then_inc(stacked, 16)

                def fill_maxima(u):
                    b, g = units[2][u]
                    taken(sp, ("smT", u))
                    for part in range(2):
                        for pair in range(2):
                            m0 = G4 * part + 2 * pair
                            sp.dma_start(stack[b][0][48 + part:P:64, 2 * g + pair, :], mT[m0:m0 + 2, u % 2, :])\
                                .then_inc(mrow_ready, 16)

                fill_stacks(0)
                fill_maxima(0)
                fill_stacks(1)
                for u in range(1, len(units[2])):
                    fill_maxima(u)
            for b in range(B):
                if stop >= 4:
                    sp.wait_ge(x_ready, QT * (B + b + 1))
                elif stop == 3:
                    taken(sp, ("proj", 1, b, QT - 1))
                elif stop == 2:
                    sp.wait_ge(x_ready, QT * (b + 1))
                else:
                    taken(sp, ("proj", 0, b, QT - 1))
                sp.dma_start(out[b].rearrange("(q p) d -> p q d", p=P), x[:, b, :, :]).then_inc(stored, 16)
            sp.wait_ge(stored, 16 * B)


_INS = ["x", "ctx_768", "mask_1x1xSxS2_bk0", "L0_xattn_ln_gamma", "L0_xattn_ln_beta", "L0_xattn_Wq",
        "L0_xattn_Wkv", "L0_xattn_Wo", "L0_xattn_bo", "L0_ffn_gate_w", "L0_ffn_up_w", "L0_ffn_up_b",
        "L0_ffn_down_w", "L0_ffn_down_b", "L0_ffn_sh_up_w", "L0_ffn_sh_up_b", "L0_ffn_sh_down_w",
        "L0_ffn_sh_down_b", "L1_xattn_Wq", "L1_xattn_Wk", "L1_xattn_Wv", "L1_xattn_Wo", "L1_xattn_bo",
        "L1_ffn_Wq", "L1_ffn_Wk", "L1_ffn_Wv", "L1_ffn_Wo", "L1_ffn_g1", "L1_ffn_b1", "L1_ffn_g2", "L1_ffn_b2",
        "L1_ffn_Wg", "L1_ffn_W1", "L1_ffn_W2"]


def kernel(**inputs):
    import numpy as _np
    import concourse.bacc as _bacc
    from concourse import mybir as _mybir
    from concourse.bass_utils import run_bass_kernel_spmd as _run

    nc = _bacc.Bacc("TRN2", target_bir_lowering=False, num_devices=1)
    arrays, aps = {}, {}
    for name in _INS:
        a = _np.ascontiguousarray(inputs[name])
        arrays[f"in_{name}_dram"] = a
        aps[name] = nc.dram_tensor(f"in_{name}_dram", a.shape, _mybir.dt.from_np(a.dtype),
                                   kind="ExternalInput").ap()
    shape = inputs["x"].shape
    out = nc.dram_tensor("out_0_dram", shape, _mybir.dt.float32, kind="ExternalOutput").ap()
    build(nc, aps, out)
    r = _run(nc, [arrays], core_ids=[0])
    return r.results[0]["out_0_dram"]
```

```python
from contextlib import ExitStack

import concourse.bass as bass
from concourse import mybir

F32 = mybir.dt.float32
BF16 = mybir.dt.bfloat16
U32 = mybir.dt.uint32
ALU = mybir.AluOpType
ACT = mybir.ActivationFunctionType
AX = mybir.AxisListType

P = 128
EPS = 1e-5
BLOCKED = -float(2.0 ** 100)


def build(nc, t, out, stop=4):
    B, S, D = t["x"].shape
    _, T, C = t["ctx_768"].shape
    QT = S // P
    R = T - P
    STRIP = 32
    G4 = 4
    DH = 64
    H0 = t["L0_xattn_Wq"].shape[1] // DH
    H1 = t["L1_xattn_Wq"].shape[1] // DH
    E = t["L0_ffn_up_w"].shape[0]
    HS, DS = 16, 8
    XSCALE = float(DH) ** -0.5
    SSCALE = float(DS) ** -0.5
    EH = t["L1_ffn_W1"].shape[2]
    CHUNKS = [(c, min(P, G4 * T - c), list(range(c // T, (min(c + P, G4 * T) - 1) // T + 1)))
              for c in range(0, G4 * T, P)]
    BLOCKS = [(k, h) for k, (_, _, hs) in enumerate(CHUNKS) for h in hs]
    FIRST = [BLOCKS.index((k, hs[0])) for k, (_, _, hs) in enumerate(CHUNKS)]
    assert (B, S, D, DH, QT) == (2, 512, 128, 64, 4) and R <= STRIP and HS * DS == D and 2 * EH == P

    ctx = ExitStack()
    with ctx:
        def sb(name, shape, dt=F32):
            return ctx.enter_context(nc.sbuf_tensor(name, shape, dt))

        def sem(name):
            return ctx.enter_context(nc.semaphore(name))

        class Room:
            def __init__(self, tensor):
                self.tensor, self.used = tensor, 0

            def take(self, n, dt=F32):
                v = self.tensor[:, self.used:self.used + n]
                self.used += n
                return v if dt is F32 else v.bitcast(dt)

        NPT = 16
        PT = sb("PT", [P, NPT, S])
        m = Room(PT[:, 10:NPT, :].rearrange("p c s -> p (c s)"))
        x = sb("x", [P, B, QT, D])
        OT_ = sb("OT", [P, (H0 // 2 + 1) * S])
        xh = sb("xh", [P, B, QT, D])
        xT = sb("xT", [P, B, S])
        ident = sb("ident", [P, P])
        identb = sb("identb", [P, P], BF16)
        rows = sb("rows", [16, P])
        cols = sb("cols", [P, 16])
        bo = sb("bo", [P, 3, D])
        mhalf = sb("mhalf", [P, 16])
        stats = sb("stats", [P, B, QT, 6])
        mv = sb("mv", [P, B, QT, 2])
        ve = sb("ve", [P, B, QT])
        rstd = sb("rstd", [P, B, QT])
        v2 = sb("v2", [P, B, QT])
        r2 = sb("r2", [P, B, QT])
        ctxm = m.take(B * C).rearrange("p (b c) -> p b c", b=B)
        ctxr = m.take(B * C).rearrange("p (b c) -> p b c", b=B)[0:STRIP]
        ctxT = m.take(B * G4 * T).rearrange("p (b r k) -> p b r k", b=B, r=G4)[0:C]
        masku = m.take(QT * T // 4, mybir.dt.uint8).rearrange("p (q k) -> p q k", q=QT)
        maskb = m.take(QT * T // 2, BF16).rearrange("p (q k) -> p q k", q=QT)
        Wqk = m.take(2 * D).rearrange("p (i d) -> p i d", i=2)
        maskf = OT_[:, 0:QT * T].rearrange("p (q k) -> p q k", q=QT)
        allow = sb("allow", [P, QT, 4])
        own = sb("own", [P, len(BLOCKS)])
        class Layer:
            pass

        xa = []
        for n, H in enumerate((H0, H1)):
            a = Layer()
            a.n, a.H, a.G = n, H, H // G4
            words = H * DH * 2 + H // 2 * D + H // 2 * B * T + B * H * T + B * H // G4 * len(BLOCKS) * (DH + 1)
            if n == 0:
                words = max(words + 2 * (E + 1) * P, B * S + 3 * S + 2 * S + B * HS // 4 * S + B * HS // 2 * S + QT * HS * STRIP)
            a.space = sb(f"space{n}", [P, words])
            m = Room(a.space)
            a.Wk = sb(f"Wk{n}", [C, H * DH])
            a.Wv = sb(f"Wv{n}", [C, H * DH])
            a.Wq = m.take(H * DH)
            a.WqT = m.take(H // 2 * P).rearrange("p (c k) -> p c k", k=P)
            a.Wo = m.take(H // 2 * D).rearrange("p (c d) -> p c d", d=D)
            a.KT = m.take(H // 2 * B * T).rearrange("p (c b k) -> p c b k", c=H // 2, b=B)
            a.KP = m.take(B * H * T).rearrange("p (b h k) -> p b h k", b=B, h=H)
            a.VB = m.take(B * a.G * len(BLOCKS) * (DH + 1)).rearrange("p (b g k d) -> p b g k d", b=B, g=a.G,
                                                                      d=DH + 1)
            if n == 0:
                upw = m.take((E + 1) * P).rearrange("p (e h) -> p e h", h=P)
                dnw = m.take((E + 1) * D).rearrange("p (e d) -> p e d", d=D)
            xa.append(a)
        OT = OT_[:, :].rearrange("p (c s) -> p c s", s=S)
        Pq = PT[:, 5:10, :].rearrange("p c s -> p (c s)")[:, 0:QT * G4 * T].rearrange("p (q k) -> p q k", q=QT)
        Ou = sb("Ou", [P, 2, QT, G4 * DH])

        def hidden(b):
            return PT[:, 0:E + 1, :] if b == 0 else OT_[:, :].rearrange("p (c s) -> p c s", s=S)

        mx = sb("mx", [P, 2, QT, G4])
        nm = sb("nm", [P, 2, QT, G4])
        mr = sb("mr", [P, 2, QT, G4])
        mparts = sb("mparts", [P, 2, QT, 2, G4], BF16)
        cT = sb("cT", [3 * E, 2, S], BF16)
        mT = cT[0:2 * G4, :, :]
        rz = sb("rz", [P, 2, QT, G4])
        gwr = sb("gwr", [E, D])
        gateT = sb("gateT", [P, E])
        dnb = sb("dnb", [E, D])
        Wg = sb("Wg", [P, E])
        W1 = sb("W1", [P, E, EH])
        W2 = sb("W2", [P, E // 2, D])
        lg = sb("lg", [P, B, QT, E])
        ex = sb("ex", [P, B, QT, E])
        g1 = sb("g1", [P, B, QT, 4])
        top = sb("top", [P, B, QT, 8])
        topi = sb("topi", [P, B, QT, 8], U32)
        topf = sb("topf", [P, B, QT, 8])
        iota = sb("iota", [P, E])
        iotai = sb("iotai", [P, E], mybir.dt.int32)
        oh = sb("oh", [P, B, QT, 2, E])
        comb = sb("comb", [P, B, QT, E])
        combT = xa[0].Wk[0:E, 0:S]
        cr = sb("cr", [P, B, QT, E])
        cparts = sb("cparts", [P, B, QT, 3, E], BF16)
        selc = xa[0].Wk[0:3 * E, S:2 * S].bitcast(BF16).rearrange("p (e k) -> p e k", k=P)
        Ws = sb("Ws", [P, 4, D])
        m = Room(xa[0].space)
        y = m.take(B * QT * D).rearrange("p (b q d) -> p b q d", b=B, q=QT)
        qk = [[m.take(S // 2, BF16) for _ in range(3)] for _ in range(2)]
        qkr = m.take(2 * S).rearrange("p (i s) -> p i s", i=2)
        stackq = [m.take(HS // 2 * S // 2, BF16).rearrange("p (c s) -> p c s", s=S) for _ in range(B)]
        stackk = [m.take(HS * S // 2, BF16).rearrange("p (h s) -> p h s", s=S) for _ in range(B)]
        wide_v = QT * HS * STRIP
        VS = [m.take(wide_v), xa[1].space[:, 0:wide_v]]
        VS = [v.rearrange("p (q h d) -> p q h d", q=QT, h=HS) for v in VS]
        m = Room(Ou[:, :, :, :].rearrange("p u q f -> p (u q f)"))
        OS = m.take(2 * S).rearrange("p (i s) -> p i s", i=2)
        On = m.take(QT * HS * DS).rearrange("p (q h d) -> p q h d", q=QT, h=HS)
        zs = sb("zs", [P, 2, QT, G4])
        scratch = nc.dram_tensor("parts_scratch", [B, 2, 2, 6, P // 2, S], BF16).ap()

        pS = [ctx.enter_context(nc.psum_tensor(f"pS{i}", [P, 1024], F32)) for i in range(2)]
        pT = [ctx.enter_context(nc.psum_tensor(f"pT{i}", [P, 512], F32)) for i in range(2)]
        pC = [ctx.enter_context(nc.psum_tensor(f"pC{i}", [P, 512], F32)) for i in range(2)]
        RING = {"S": pS, "T": pT, "C": pC}
        FULL = {r: [sem(f"{r}{i}_full") for i in range(2)] for r in RING}
        FREE = {r: [sem(f"{r}{i}_free") for i in range(2)] for r in RING}
        uses = {r: 0 for r in RING}
        at = {}

        W = {k: sem(f"ld_{k}") for k in ("x", "ctx", "rows", "mask", "Wq0", "Wk0", "Wv0", "Wo0", "bo", "gate",
                                         "upw", "dnw", "Wq1", "Wk1", "Wv1", "Wo1", "Wg", "Ws", "W1", "W2")}
        ident_ready = sem("ident_ready")
        consts = sem("consts")
        ctx_ready = sem("ctx_ready")
        nm_ready = sem("nm_ready")
        stats_ready = sem("stats_ready")
        rstd_ready = sem("rstd_ready")
        xh_ready = sem("xh_ready")
        xb_ready = sem("xb_ready")
        x_ready = sem("x_ready")
        mask_ready = sem("mask_ready")
        mp_ready = sem("mp_ready")
        lg_ready = sem("lg_ready")
        ex_ready = sem("ex_ready")
        comb_ready = sem("comb_ready")
        part_ready = sem("part_ready")
        cparts_ready = sem("cparts_ready")
        kpads_ready = sem("kpads_ready")
        wqk_ready = sem("wqk_ready")
        vpads_ready = sem("vpads_ready")
        parked = [sem("q_parked"), sem("k_parked")]
        stacked = sem("stacked")
        mrow_ready = sem("mrow_ready")
        p_used = sem("p_used")
        stored = sem("stored")
        chain = {e: sem(f"{e}_chain") for e in ("dve", "act", "pool")}
        links = dict.fromkeys(chain, 0)

        block = ctx.enter_context(nc.Block())
        units = [[(b, g) for b in range(B) for g in range(H // G4)] for H in (H0, H1, HS)]
        AHEAD = units[1].index((1, H1 // G4 - 1))
        PARKS = (6, 8)
        STACK_LOADS = 4
        before = [0, len(units[0]), len(units[0]) + len(units[1])]

        def filled(eng, key):
            ring, buf, turn = at[key]
            eng.wait_ge(FULL[ring][buf], turn + 1)
            return RING[ring][buf]

        def freed(key):
            ring, buf, _ = at[key]
            return FREE[ring][buf]

        def taken(eng, key):
            eng.wait_ge(freed(key), at[key][2] + 1)

        def link(eng, name, ins):
            links[name] += 1
            ins.then_inc(chain[name], 1)
            eng.wait_ge(chain[name], links[name])

        @block.tensor
        def _(pe):
            mm = nc.tensor.matmul
            tr = nc.tensor.transpose

            def claim(ring, key):
                buf, turn = uses[ring] % 2, uses[ring] // 2
                uses[ring] += 1
                assert key not in at, key
                at[key] = (ring, buf, turn)
                if turn:
                    pe.wait_ge(FREE[ring][buf], turn)
                return RING[ring][buf]

            def full(key):
                return FULL[at[key][0]][at[key][1]]

            def xt(stage, b):
                pe.wait_ge(xh_ready, stage * B + b + 1)
                ps = claim("C", ("xT", stage, b))
                for q in range(QT):
                    last = tr(ps[:, q * P:(q + 1) * P], xh[:, b, q, :], ident[:, :])
                last.then_inc(full(("xT", stage, b)), 1)

            def context():
                pe.wait_ge(ident_ready, 1)
                pe.wait_ge(W["ctx"], 32)
                ps = claim("T", "ctxT")
                for b in range(B):
                    tr(ps[0:C, b * T:b * T + P], ctxm[:, b, :], ident[:, :])
                    last = tr(ps[0:C, b * T + P:(b + 1) * T], ctxr[0:R, b, :], ident[0:R, 0:R])
                last.then_inc(full("ctxT"), 1)

            def columns():
                pe.wait_ge(W["rows"], 16 * 8)
                ps = claim("C", "cols")
                tr(ps[:, 0:15], rows[0:15, :], ident[0:15, 0:15]).then_inc(full("cols"), 1)
                pe.wait_ge(W["gate"], 16)
                ps = claim("C", "gateT")
                tr(ps[:, 0:E], gwr[:, :], ident[0:E, 0:E]).then_inc(full("gateT"), 1)

            def prework(a):
                n = a.n
                pe.wait_ge(W[f"Wq{n}"], 16)
                for c0 in range(0, a.H // 2, 4):
                    ps = claim("T", ("wqT", n, c0))
                    for c in range(c0, c0 + 4):
                        last = tr(ps[:, (c - c0) * P:(c - c0 + 1) * P], a.Wq[:, c * P:(c + 1) * P], ident[:, :])
                    last.then_inc(full(("wqT", n, c0)), 1)
                pe.wait_ge(W[f"Wk{n}"], 16)
                pe.wait_ge(ctx_ready, 1)
                for c in range(a.H // 2):
                    ps = claim("C", ("kT", n, c))
                    mm(ps[:, 0:B * T].rearrange("p (b k) -> p b k", b=B), a.Wk[:, c * P:(c + 1) * P], ctxT[:, :, 0, :],
                       start=True, stop=True).then_inc(full(("kT", n, c)), 1)
                for h in range(a.H):
                    c, r = h // 2, DH * (h % 2)
                    taken(pe, ("wqT", n, c // 4 * 4))
                    taken(pe, ("kT", n, c))
                    ps = claim("T", ("kp", n, h))
                    mm(ps[:, 0:B * T], a.WqT[r:r + DH, c, :], a.KT[r:r + DH, c, :, :].rearrange("p b k -> p (b k)"),
                       start=True, stop=True).then_inc(full(("kp", n, h)), 1)
                pe.wait_ge(W[f"Wv{n}"], 16)
                taken(pe, "ctxT")
                wv = a.Wv[:, :].rearrange("c (g j d) -> c g j d", j=G4, d=DH)
                for b in range(B):
                    for k, (c0, size, hs) in enumerate(CHUNKS):
                        ps = claim("S", ("v", n, b, k))
                        o = ps[0:size, 0:a.G * len(hs) * DH].rearrange("p (g j d) -> p g j d", g=a.G, d=DH)
                        mm(o, ctxT[:, b, :, :].rearrange("c r k -> c (r k)")[:, c0:c0 + size],
                           wv[:, :, hs[0]:hs[-1] + 1, :], start=True, stop=True).then_inc(full(("v", n, b, k)), 1)

            def cross(a, ahead=None):
                n, uu = a.n, units[a.n]

                def scores(u, q):
                    if u == len(uu):
                        return
                    b, g = uu[u]
                    if q == 0:
                        if n == 0 and u == 0:
                            pe.wait_ge(mask_ready, 1)
                        if g == 0:
                            xt(2 * n, b)
                            taken(pe, ("xT", 2 * n, b))
                        taken(pe, ("kp", n, G4 * g + 2))
                        taken(pe, ("kp", n, G4 * g + 3))
                    ps = claim("S", ("s", n, u, q))
                    for i in range(2):
                        last = mm(ps[:, 512 * i:512 * i + 2 * T], xT[:, b, q * P:(q + 1) * P],
                                  a.KP[:, b, G4 * g + 2 * i:G4 * g + 2 * i + 2, :].rearrange("p h k -> p (h k)"),
                                  start=True, stop=(n == 1))
                        if n == 0:
                            last = mm(ps[:, 512 * i:512 * i + 2 * T].rearrange("p (j k) -> p j k", j=2),
                                      identb[:, :], maskb[:, q, :].unsqueeze(1).broadcast_to([P, 2, T]),
                                      start=False, stop=True)
                    last.then_inc(full(("s", n, u, q)), 1)

                def turn(u):
                    taken(pe, ("s", n, u, QT - 1))
                    for k, (c0, size, hs) in enumerate(CHUNKS):
                        ps = claim("TTCTC"[k], ("pt", n, u, k))
                        for q in range(QT):
                            last = tr(ps[0:size, q * P:(q + 1) * P], Pq[:, q, c0:c0 + size], ident[:, :])
                        last.then_inc(full(("pt", n, u, k)), 1)

                def values(u, q):
                    b, g = uu[u]
                    if q == 0:
                        if n == 0 and u == 0:
                            pe.wait_ge(consts, 2)
                        for k in (len(CHUNKS) - 1, len(CHUNKS) - 2):
                            if g == 0:
                                taken(pe, ("v", n, b, k))
                            taken(pe, ("pt", n, u, k))
                    ps = claim("C", ("pv", n, u, q))
                    for k, (c0, size, hs) in enumerate(CHUNKS):
                        v = a.VB[0:size, b, g, FIRST[k]:FIRST[k] + len(hs), :].rearrange("p j d -> p (j d)")
                        last = mm(ps[:, hs[0] * (DH + 1):(hs[-1] + 1) * (DH + 1)],
                                  PT[0:size, k, q * P:(q + 1) * P], v,
                                  start=(k == 0), stop=(k == len(CHUNKS) - 1), skip_group_check=True)
                    last.then_inc(full(("pv", n, u, q)), 1)

                def outT(u):
                    taken(pe, ("pv", n, u, QT - 1))
                    for c in range(2):
                        ps = claim("T", ("oT", n, u, c))
                        for q in range(QT):
                            last = tr(ps[:, q * P:(q + 1) * P], Ou[:, u % 2, q, c * P:(c + 1) * P], ident[:, :])
                        last.then_inc(full(("oT", n, u, c)), 1)

                def project(u):
                    b, g = uu[u]
                    pe.wait_ge(W[f"Wo{n}"], 16)
                    taken(pe, ("oT", n, u, 1))
                    ps = claim("C", ("proj", n, b))
                    for q in range(QT):
                        for c in range(a.H // 2):
                            last = mm(ps[:, q * D:(q + 1) * D], OT[:, c, q * P:(q + 1) * P], a.Wo[:, c, :],
                                      start=(c == 0), stop=(c == a.H // 2 - 1))
                    last.then_inc(full(("proj", n, b)), 1)

                for q in range(QT):
                    scores(0, q)
                for u in range(len(uu)):
                    row_end = u and uu[u - 1][1] == a.G - 1
                    turn(u)
                    scores(u + 1, 0)
                    scores(u + 1, 1)
                    if u:
                        outT(u - 1)
                    if ahead == u:
                        self_in(0)
                    values(u, 0)
                    scores(u + 1, 2)
                    values(u, 1)
                    scores(u + 1, 3)
                    values(u, 2)
                    if row_end:
                        project(u - 1)
                    values(u, 3)
                outT(len(uu) - 1)
                project(len(uu) - 1)

            def ffn(n):
                for b in range(B):
                    xt(1 + 3 * n, b)
                    taken(pe, ("xT", 1 + 3 * n, b))
                    if n == 0:
                        taken(pe, "gateT")
                        pe.wait_ge(W["upw"], 32)
                    else:
                        pe.wait_ge(W["Wg"], 16)
                        pe.wait_ge(W["W1"], 16)
                    ps = claim("C", ("gate", n, b))
                    for q in range(QT):
                        last = mm(ps[:, q * E:(q + 1) * E], xT[:, b, q * P:(q + 1) * P],
                                  gateT[:, :] if n == 0 else Wg[:, :], start=True, stop=True)
                    last.then_inc(full(("gate", n, b)), 1)
                    ups = E + 1 if n == 0 else E // 2
                    for e in range(ups):
                        ps = claim("T", ("up", n, b, e))
                        w = upw[:, e, :] if n == 0 else W1[:, 2 * e:2 * e + 2, :].rearrange("p e h -> p (e h)")
                        mm(ps[:, :], w, xT[:, b, :], start=True, stop=True).then_inc(full(("up", n, b, e)), 1)
                for b in range(B):
                    pe.wait_ge(cparts_ready, B * n + b + 1)
                    ps = claim("C", ("cT", n, b))
                    for q in range(QT):
                        last = tr(ps[0:3 * E, q * 64:(q + 1) * 64].bitcast(BF16),
                                  cparts[:, b, q, :, :].rearrange("p a e -> p (a e)"), identb[:, :])
                    last.then_inc(full(("cT", n, b)), 1)
                    if n == 0:
                        ps = claim("C", ("combT", b))
                        for q in range(QT):
                            last = tr(ps[0:E, q * P:(q + 1) * P], comb[:, b, q, :], ident[:, :])
                        last.then_inc(full(("combT", b)), 1)
                    taken(pe, ("cT", n, b))
                    if n == 0 and b == 0:
                        pe.wait_ge(consts, 3)
                    spread = E if n == 0 else E // 2
                    for e in range(spread):
                        ps = claim("T", ("cb", n, b, e))
                        if n == 0:
                            last = mm(ps[:, :], selc[:, e, :], cT[:, b, :], start=True, stop=True)
                        else:
                            for i in range(2):
                                last = mm(ps[EH * i:EH * (i + 1), :], selc[:, 2 * e + i, 0:EH], cT[:, b, :],
                                          start=True, stop=True)
                        last.then_inc(full(("cb", n, b, e)), 1)
                    if n == 0:
                        pe.wait_ge(W["dnw"], 48)
                        taken(pe, ("combT", b))
                        taken(pe, ("up", n, b, E))
                    else:
                        pe.wait_ge(W["W2"], 16)
                    taken(pe, ("cb", n, b, spread - 1))
                    ps = claim("S", ("dn", n, b))
                    for q in range(QT):
                        o, t_ = ps[:, q * D:(q + 1) * D], slice(q * P, (q + 1) * P)
                        if n == 0:
                            mm(o, combT[:, t_], dnb[:, :], start=True, stop=False)
                            mm(o, hidden(b)[:, E, t_], dnw[:, E, :], start=False, stop=False)
                        for e in range(spread):
                            last = mm(o, hidden(b)[:, e, t_], dnw[:, e, :] if n == 0 else W2[:, e, :],
                                      start=(n == 1 and e == 0), stop=(e == spread - 1))
                    last.then_inc(full(("dn", n, b)), 1)

            def self_in(b):
                pe.wait_ge(W["Ws"], 64)
                pe.wait_ge(wqk_ready, 4)
                xt(3, b)
                taken(pe, ("xT", 3, b))
                for i in range(2):
                    ps = claim("C", ("qk", b, i))
                    mm(ps[:, :], Wqk[:, i, :], xT[:, b, :],
                       start=True, stop=True).then_inc(full(("qk", b, i)), 1)
                ps = claim("C", ("vs", b))
                for q in range(QT):
                    last = mm(ps[:, q * D:(q + 1) * D], xT[:, b, q * P:(q + 1) * P], Ws[:, 2, :],
                              start=True, stop=True)
                last.then_inc(full(("vs", b)), 1)

            def self_attention():
                uu, G = units[2], HS // G4

                pairs = iter([(u, k) for u in range(len(uu)) for k in range(8)])

                def score_pair():
                    u, k = next(pairs, (None, None))
                    if u is None:
                        return
                    b, g = uu[u]
                    if g == 0 and k == 0:
                        pe.wait_ge(stacked, 16 * STACK_LOADS * (b + 1))
                    q = k // 2
                    ps = claim("S", ("ss", u, k))
                    for i in range(2):
                        h = G4 * g + 2 * (k % 2) + i
                        last = mm(ps[:, 512 * i:512 * i + 512], stackq[b][:, h // 2, q * P:(q + 1) * P],
                                  stackk[b][:, h, :], start=True, stop=True)
                    last.then_inc(full(("ss", u, k)), 1)

                def values(u, kt, pv):
                    b, g = uu[u]
                    taken(pe, ("sst", u, kt, G4 - 1))
                    for j in range(G4):
                        last = mm(pv[STRIP * j:STRIP * (j + 1), :], VS[b][:, kt, G4 * g + j, :],
                                  PT[:, (4 * kt + j) % NPT, :], start=(kt == 0), stop=(kt == QT - 1))
                    last.then_inc(full(("spv", u)) if kt == QT - 1 else p_used, 1)

                def maxima(u):
                    pe.wait_ge(mp_ready, u + 1)
                    ps = claim("T", ("smT", u))
                    for q in range(QT):
                        last = tr(ps[0:8, q * 64:(q + 1) * 64].bitcast(BF16),
                                  mparts[:, u % 2, q, :, :].rearrange("p a h -> p (a h)"), identb[:, :])
                    last.then_inc(full(("smT", u)), 1)

                def back(u):
                    taken(pe, ("spv", u))
                    ps = claim("C", ("sO", u))
                    for q in range(QT):
                        last = tr(ps[:, q * P:(q + 1) * P], OS[:, u % 2, q * P:(q + 1) * P], ident[:, :])
                    last.then_inc(full(("sO", u)), 1)

                def row_outT(b):
                    taken(pe, ("sO", b * G + G - 1))
                    ps = claim("T", ("onT", b))
                    for q in range(QT):
                        last = tr(ps[:, q * P:(q + 1) * P], On[:, q, :, :].rearrange("p h d -> p (h d)"), ident[:, :])
                    last.then_inc(full(("onT", b)), 1)

                def row_project(b):
                    taken(pe, ("onT", b))
                    ps = claim("T", ("sproj", b))
                    for q in range(QT):
                        last = mm(ps[:, q * D:(q + 1) * D], OT[:, b, q * P:(q + 1) * P], Ws[:, 3, :],
                                  start=True, stop=True)
                    last.then_inc(full(("sproj", b)), 1)

                for _ in range(10):
                    score_pair()
                maxima(0)
                for _ in range(2):
                    score_pair()
                self_in(1)
                for u in range(len(uu)):
                    b, g = uu[u]
                    if g == 0:
                        taken(pe, ("vs", b))
                    pe.wait_ge(mrow_ready, 16 * 4 * (u + 1))
                    for kt in range(QT):
                        for j in range(G4):
                            h = G4 * g + j
                            ps = claim("T", ("sst", u, kt, j))
                            mm(ps[:, :], stackk[b][:, h, kt * P:(kt + 1) * P], stackq[b][:, h // 2, :],
                               start=True, stop=True).then_inc(full(("sst", u, kt, j)), 1)
                            if j == 1:
                                score_pair()
                                if kt == QT - 1 and u + 1 < len(uu):
                                    maxima(u + 1)
                        if kt == 0:
                            pv = claim("C", ("spv", u))
                            if u:
                                back(u - 1)
                        else:
                            values(u, kt - 1, pv)
                        if u and g == 0 and kt == 1:
                            row_outT(b - 1)
                        if u and g == 0 and kt == 2:
                            row_project(b - 1)
                        score_pair()
                    values(u, QT - 1, pv)
                back(len(uu) - 1)
                row_outT(B - 1)
                row_project(B - 1)

            context()
            prework(xa[0])
            columns()
            cross(xa[0])
            prework(xa[1])
            ffn(0)
            cross(xa[1], ahead=AHEAD)
            self_attention()
            ffn(1)

        @block.scalar
        def _(act):
            A = nc.scalar
            cp = A.copy

            def xt(stage, b):
                ps = filled(act, ("xT", stage, b))
                if stage in (0, 3, 4):
                    c = {0: 0, 3: 2, 4: 4}[stage]
                    if (stage, b) == (0, 0):
                        taken(act, "cols")
                    A.activation(xT[:, b, :], ps[:, :], ACT.Identity, bias=cols[:, c + 1:c + 2],
                                 scale=cols[:, c:c + 1]).then_inc(freed(("xT", stage, b)), 1)
                else:
                    cp(xT[:, b, :], ps[:, :]).then_inc(freed(("xT", stage, b)), 1)

            def prework(a):
                n = a.n
                for c in range(a.H // 2):
                    ps = filled(act, ("kT", n, c))
                    cp(a.KT[:, c, :, :].rearrange("p b k -> p (b k)"), ps[:, 0:B * T])\
                        .then_inc(freed(("kT", n, c)), 1)
                for h in range(0, a.H, 2):
                    ps = filled(act, ("kp", n, h))
                    cp(a.KP[:, :, h, :], ps[:, 0:B * T].rearrange("p (b k) -> p b k", b=B))\
                        .then_inc(freed(("kp", n, h)), 1)
                if n == 0:
                    act.wait_ge(consts, 1)
                for b in range(B):
                    for k in range(0, len(CHUNKS), 2):
                        c0, size, hs = CHUNKS[k]
                        ps = filled(act, ("v", n, b, k))
                        v = ps[0:size, 0:a.G * len(hs) * DH].rearrange("p (g j d) -> p g j d", g=a.G, d=DH)
                        for j in range(len(hs)):
                            last = A.activation(a.VB[0:size, b, :, FIRST[k] + j, 0:DH], v[:, :, j, :], ACT.Copy,
                                                scale=own[0:size, FIRST[k] + j:FIRST[k] + j + 1])
                        last.then_inc(freed(("v", n, b, k)), 1)

            def self_in(b):
                xt(3, b)
                ps = filled(act, ("vs", b))
                act.wait_ge(vpads_ready, b + 1)
                cp(VS[b][:, :, :, 0:DS], ps[:, :].rearrange("p (q h d) -> p q h d", q=QT, h=HS))\
                    .then_inc(freed(("vs", b)), 1)

            def cross(a, ahead=None):
                n, uu = a.n, units[a.n]

                def outT(u):
                    b, g = uu[u]
                    for c in range(2):
                        ps = filled(act, ("oT", n, u, c))
                        cp(OT[:, 2 * g + c, :], ps[:, :]).then_inc(freed(("oT", n, u, c)), 1)

                def exponentials(u, q0, q1):
                    if u == len(uu):
                        return
                    if uu[u][1] == 0 and q0 == 0:
                        xt(2 * n, uu[u][0])
                    for q in range(q0, q1):
                        ps = filled(act, ("s", n, u, q))
                        act.wait_ge(nm_ready, QT * (n * len(units[0]) + u) + q + 1)
                        for j in range(G4):
                            c = 512 * (j // 2) + T * (j % 2)
                            last = A.activation(Pq[:, q, j * T:(j + 1) * T], ps[:, c:c + T], ACT.Exp,
                                                bias=nm[:, u % 2, q, j:j + 1], scale=XSCALE)
                        last.then_inc(freed(("s", n, u, q)), 1)

                exponentials(0, 0, QT)
                for u in range(len(uu)):
                    for k in range(0, len(CHUNKS), 2):
                        size = CHUNKS[k][1]
                        ps = filled(act, ("pt", n, u, k))
                        cp(PT[0:size, k, :], ps[0:size, :]).then_inc(freed(("pt", n, u, k)), 1)
                    exponentials(u + 1, 0, 2)
                    if u:
                        outT(u - 1)
                    if ahead == u:
                        self_in(0)
                    exponentials(u + 1, 2, QT)
                outT(len(uu) - 1)

            def ffn(n):
                for b in range(B):
                    xt(1 + 3 * n, b)
                    act.wait_ge(lg_ready, B * n + b + 1)
                    A.activation(ex[:, b, :, :], ex[:, b, :, :], ACT.Exp).then_inc(ex_ready, 1)
                    for e in range(E + 1 if n == 0 else E // 2):
                        ps = filled(act, ("up", n, b, e))
                        if n == 0:
                            A.activation(hidden(b)[:, e, :], ps[:, :], ACT.Silu, bias=cols[:, 6 + e:7 + e])\
                                .then_inc(freed(("up", n, b, e)), 1)
                        else:
                            A.activation(hidden(b)[:, e, :], ps[:, :], ACT.Relu)\
                                .then_inc(freed(("up", n, b, e)), 1)
                for b in range(B):
                    ps = filled(act, ("cT", n, b))
                    cp(cT[:, b, :], ps[0:3 * E, 0:256].bitcast(BF16)).then_inc(freed(("cT", n, b)), 1)
                    if n == 0:
                        ps = filled(act, ("combT", b))
                        if b:
                            filled(act, ("dn", n, 0))
                        cp(combT[:, :], ps[0:E, :]).then_inc(freed(("combT", b)), 1)

            def self_attention():
                uu, G = units[2], HS // G4

                def maxima(u):
                    ps = filled(act, ("smT", u))
                    if u >= 2:
                        act.wait_ge(mrow_ready, 16 * 4 * (u - 1))
                    cp(mT[:, u % 2, :], ps[0:8, 0:256].bitcast(BF16)).then_inc(freed(("smT", u)), 1)

                def back(u):
                    ps = filled(act, ("spv", u))
                    cp(OS[:, u % 2, :], ps[:, :]).then_inc(freed(("spv", u)), 1)

                def row_outT(b):
                    ps = filled(act, ("onT", b))
                    cp(OT[:, b, :], ps[:, :]).then_inc(freed(("onT", b)), 1)

                maxima(0)
                self_in(1)
                for u in range(len(uu)):
                    b, g = uu[u]
                    if u:
                        back(u - 1)
                    for kt in range(QT):
                        if u:
                            if kt < QT - 1:
                                act.wait_ge(p_used, 3 * (u - 1) + kt + 1)
                            else:
                                filled(act, ("spv", u - 1))
                        for j in range(G4):
                            if kt == QT - 1 and j == 2 and u + 1 < len(uu):
                                maxima(u + 1)
                            ps = filled(act, ("sst", u, kt, j))
                            A.activation(PT[:, 4 * kt + j, :], ps[:, :], ACT.Exp, scale=SSCALE)\
                                .then_inc(freed(("sst", u, kt, j)), 1)
                        if u and g == 0 and kt == 1:
                            row_outT(b - 1)
                back(len(uu) - 1)
                row_outT(B - 1)

            act.dma_start(ctxm[:, :, :], t["ctx_768"][:, 0:P, :].rearrange("b k c -> k b c")).then_inc(W["ctx"], 16)
            act.dma_start(ctxr[0:R, :, :], t["ctx_768"][:, P:T, :].rearrange("b k c -> k b c")).then_inc(W["ctx"], 16)
            act.dma_start(xa[0].Wk[:, :], t["L0_xattn_Wkv"][:, 0:H0 * DH]).then_inc(W["Wk0"], 16)
            act.dma_start(xa[0].Wv[:, :], t["L0_xattn_Wkv"][:, H0 * DH:2 * H0 * DH]).then_inc(W["Wv0"], 16)
            ps = filled(act, "ctxT")
            rows_ = ps[0:C, 0:B * T].rearrange("c (b k) -> c b k", b=B)
            cp(ctxT[:, :, 0, :], rows_).then_inc(ctx_ready, 1)
            cp(ctxT[:, :, 1:G4, :], rows_.unsqueeze(2).broadcast_to([C, B, G4 - 1, T])).then_inc(freed("ctxT"), 1)
            prework(xa[0])
            ps = filled(act, "cols")
            cp(cols[:, 0:15], ps[:, 0:15]).then_inc(freed("cols"), 1)
            ps = filled(act, "gateT")
            cp(gateT[:, :], ps[:, 0:E]).then_inc(freed("gateT"), 1)
            cross(xa[0])
            prework(xa[1])
            ffn(0)
            cross(xa[1], ahead=AHEAD)
            self_attention()
            ffn(1)

        @block.vector
        def _(dve):
            V = nc.vector
            tt = V.tensor_tensor

            def seq(ins):
                link(dve, "dve", ins)

            def norm(stage, b):
                src = y if stage == 4 else x
                if stage == 0:
                    dve.wait_ge(W["x"], 16 * (b + 1))
                for q in range(QT):
                    ins = V.bn_stats(stats[:, b, q, :], src[:, b, q, :])
                seq(ins)
                for q in range(QT):
                    ins = V.bn_aggr(mv[:, b, q, :], stats[:, b, q, :])
                ins.then_inc(stats_ready, 1)
                dve.wait_ge(rstd_ready, B * stage + b + 1)
                r = r2 if stage == 0 else rstd
                for q in range(QT):
                    dst = y if stage == 3 else xh
                    ins = V.tensor_scalar(dst[:, b, q, :], src[:, b, q, :], mv[:, b, q, 0:1], r[:, b, q:q + 1],
                                          ALU.subtract, ALU.mult)
                if stage == 3:
                    seq(ins)
                    ins = tt(xh[:, b, :, :], y[:, b, :, :],
                             r2[:, b, :].unsqueeze(2).broadcast_to([P, QT, D]), ALU.mult)
                ins.then_inc(xh_ready, 1)

            def prework(a):
                n = a.n
                for c0 in range(0, a.H // 2, 4):
                    ps = filled(dve, ("wqT", n, c0))
                    V.tensor_copy(a.WqT[:, c0:c0 + 4, :].rearrange("p c k -> p (c k)"), ps[:, :])\
                        .then_inc(freed(("wqT", n, c0)), 1)
                for h in range(1, a.H, 2):
                    ps = filled(dve, ("kp", n, h))
                    v = ps[:, 0:B * T].rearrange("p (b k) -> p b k", b=B)
                    V.tensor_copy(a.KP[:, :, h, :], v).then_inc(freed(("kp", n, h)), 1)
                if n == 0:
                    dve.wait_ge(consts, 1)
                for b in range(B):
                    for k in range(1, len(CHUNKS), 2):
                        c0, size, hs = CHUNKS[k]
                        ps = filled(dve, ("v", n, b, k))
                        v = ps[0:size, 0:a.G * len(hs) * DH].rearrange("p (g j d) -> p g j d", g=a.G, d=DH)
                        for j in range(len(hs)):
                            ins = V.tensor_scalar(a.VB[0:size, b, :, FIRST[k] + j, 0:DH], v[:, :, j, :],
                                                  own[0:size, FIRST[k] + j:FIRST[k] + j + 1], None, ALU.mult)
                        ins.then_inc(freed(("v", n, b, k)), 1)

            def parts(u):
                m, r = mx[:, u % 2, :, :], mr[:, u % 2, :, :]
                hi, lo = (mparts[:, u % 2, :, a, :] for a in range(2))
                seq(V.tensor_copy(hi, m))
                seq(tt(r, m, hi, ALU.subtract))
                V.tensor_copy(lo, r).then_inc(mp_ready, 1)

            def self_in(b):
                for i in range(2):
                    ps = filled(dve, ("qk", b, i))
                    if b:
                        dve.wait_ge(parked[i], 16 * PARKS[i])
                    p1, p2, p3 = qk[i]
                    V.tensor_copy(p1, ps[:, :]).then_inc(part_ready, 1)
                    dve.wait_ge(part_ready, 3 * (2 * b + i) + 1)
                    tt(qkr[:, i, :], ps[:, :], p1, ALU.subtract).then_inc(freed(("qk", b, i)), 1)
                    taken(dve, ("qk", b, i))
                    V.tensor_copy(p2, qkr[:, i, :]).then_inc(part_ready, 1)
                    dve.wait_ge(part_ready, 3 * (2 * b + i) + 2)
                    tt(p3, qkr[:, i, :], p2, ALU.subtract).then_inc(part_ready, 1)

            def cross(a, ahead=None):
                n, uu = a.n, units[a.n]

                def maxima(u, q0, q1):
                    if u == len(uu):
                        return
                    for q in range(q0, q1):
                        ps = filled(dve, ("s", n, u, q))
                        seq(V.tensor_reduce(mx[:, u % 2, q, :],
                                            ps[:, :].rearrange("p (i k) -> p i k", i=2)[:, :, 0:2 * T].rearrange(
                                                "p i (j k) -> p i j k", j=2), AX.X, ALU.max))
                        V.tensor_scalar(nm[:, u % 2, q, :], mx[:, u % 2, q, :], -XSCALE, None, ALU.mult)\
                            .then_inc(nm_ready, 1)

                def outputs(u, q):
                    ps = filled(dve, ("pv", n, u, q))
                    v = ps[:, 0:G4 * (DH + 1)].rearrange("p (h d) -> p h d", h=G4)
                    z = rz[:, u % 2, q, :]
                    seq(V.reciprocal(z, v[:, :, DH]))
                    if n == 0:
                        seq(tt(z, z, allow[:, q, 2:3].broadcast_to([P, G4]), ALU.add))
                    tt(Ou[:, u % 2, q, :].rearrange("p (h d) -> p h d", h=G4), v[:, :, 0:DH],
                       z.unsqueeze(2).broadcast_to([P, G4, DH]), ALU.mult).then_inc(freed(("pv", n, u, q)), 1)

                def project(b):
                    dve.wait_ge(xb_ready, B * 2 * n + b + 1)
                    ps = filled(dve, ("proj", n, b))
                    row = x[:, b, :, :].rearrange("p q d -> p (q d)")
                    tt(row, ps[:, :], row, ALU.add).then_inc(freed(("proj", n, b)), 1)

                maxima(0, 0, QT)
                for u in range(len(uu)):
                    row_end = u and uu[u - 1][1] == a.G - 1
                    for k in range(1, len(CHUNKS), 2):
                        size = CHUNKS[k][1]
                        ps = filled(dve, ("pt", n, u, k))
                        V.tensor_copy(PT[0:size, k, :], ps[0:size, :]).then_inc(freed(("pt", n, u, k)), 1)
                    maxima(u + 1, 0, 2)
                    if ahead == u:
                        self_in(0)
                    outputs(u, 0)
                    maxima(u + 1, 2, 3)
                    outputs(u, 1)
                    maxima(u + 1, 3, 4)
                    outputs(u, 2)
                    if row_end:
                        project(uu[u - 1][0])
                    outputs(u, 3)
                    if row_end:
                        taken(dve, ("proj", n, uu[u - 1][0]))
                        norm(2 * n + 1, uu[u - 1][0])
                project(B - 1)
                taken(dve, ("proj", n, B - 1))
                norm(2 * n + 1, B - 1)

            def gate(n, b):
                l, e_, m, z = lg[:, b, :, :], ex[:, b, :, :], g1[:, b, :, 0:1], g1[:, b, :, 1:2]
                wide = [P, QT, E]
                ps = filled(dve, ("gate", n, b))
                V.tensor_copy(l.rearrange("p q e -> p (q e)"), ps[:, 0:QT * E]).then_inc(freed(("gate", n, b)), 1)
                taken(dve, ("gate", n, b))
                seq(V.tensor_reduce(g1[:, b, :, 0], l, AX.X, ALU.max))
                tt(e_, l, m.broadcast_to(wide), ALU.subtract).then_inc(lg_ready, 1)
                dve.wait_ge(ex_ready, B * n + b + 1)
                if n == 0:
                    seq(V.tensor_reduce(g1[:, b, :, 1], e_, AX.X, ALU.add))
                    seq(V.reciprocal(g1[:, b, :, 1], g1[:, b, :, 1]))
                    seq(tt(e_, e_, z.broadcast_to(wide), ALU.mult))
                    ranked = ex
                else:
                    ranked = lg
                for q in range(QT):
                    seq(V.max(top[:, b, q, :], ranked[:, b, q, :]))
                    seq(V.max_index(topi[:, b, q, :], top[:, b, q, :], ranked[:, b, q, :]))
                seq(V.tensor_copy(topf[:, b, :, :], topi[:, b, :, :]))
                if n == 0 and b == 0:
                    dve.wait_ge(consts, 3)
                for k in range(2):
                    ins = tt(oh[:, b, :, k, :], iota[:, :].unsqueeze(1).broadcast_to(wide),
                             topf[:, b, :, k:k + 1].broadcast_to(wide), ALU.is_equal)
                    seq(ins)
                seq(tt(oh[:, b, :, 0, :], oh[:, b, :, 0, :], oh[:, b, :, 1, :], ALU.add))
                c = comb[:, b, :, :]
                seq(tt(c, e_, oh[:, b, :, 0, :], ALU.mult))
                seq(V.tensor_reduce(g1[:, b, :, 2], c, AX.X, ALU.add))
                if n == 0:
                    seq(V.tensor_scalar(g1[:, b, :, 2], g1[:, b, :, 2], 1e-20, None, ALU.add))
                seq(V.reciprocal(g1[:, b, :, 3], g1[:, b, :, 2]))
                ins = tt(c, c, g1[:, b, :, 3:4].broadcast_to(wide), ALU.mult)
                seq(ins)
                p1, p2, p3 = (cparts[:, b, :, k, :] for k in range(3))
                r = cr[:, b, :, :]
                seq(V.tensor_copy(p1, c))
                seq(tt(r, c, p1, ALU.subtract))
                seq(V.tensor_copy(p2, r))
                tt(p3, r, p2, ALU.subtract).then_inc(cparts_ready, 1)

            def ffn(n):
                for b in range(B):
                    gate(n, b)
                spread = E if n == 0 else E // 2
                for b in range(B):
                    for e in range(spread):
                        ps = filled(dve, ("cb", n, b, e))
                        if b == 0 or e == 0:
                            taken(dve, ("up", n, b, e))
                        h = hidden(b)[:, e, :]
                        if e == 0:
                            taken(dve, ("up", n, b, spread - 1 + (n == 0)))
                        tt(h, h, ps[:, :], ALU.mult).then_inc(freed(("cb", n, b, e)), 1)
                    dve.wait_ge(xb_ready, B * (1 + 2 * n) + b + 1)
                    ps = filled(dve, ("dn", n, b))
                    row = x[:, b, :, :].rearrange("p q d -> p (q d)")
                    ins = tt(row, row, ps[:, 0:S], ALU.add).then_inc(freed(("dn", n, b)), 1)
                    if n == 0:
                        taken(dve, ("dn", n, b))
                        norm(2, b)

            def self_attention():
                uu, G = units[2], HS // G4

                pairs = iter([(u, k) for u in range(len(uu)) for k in range(8)])

                def maxima(count):
                    for _ in range(count):
                        u, k = next(pairs, (None, None))
                        if u is None:
                            return
                        ps = filled(dve, ("ss", u, k))
                        j = 2 * (k % 2)
                        V.tensor_reduce(mx[:, u % 2, k // 2, j:j + 2], ps[:, :].rearrange("p (i k) -> p i k", i=2),
                                        AX.X, ALU.max).then_inc(freed(("ss", u, k)), 1)
                        if k == 7:
                            taken(dve, ("ss", u, 7))
                            parts(u)

                def back(u):
                    b, g = uu[u]
                    ps = filled(dve, ("sO", u))
                    v = ps[:, :].rearrange("p (q j d) -> p q j d", q=QT, j=G4)
                    z = zs[:, u % 2, :, :]
                    seq(V.reciprocal(z, v[:, :, :, DS]))
                    tt(On[:, :, G4 * g:G4 * (g + 1), :], v[:, :, :, 0:DS],
                       z.unsqueeze(3).broadcast_to([P, QT, G4, DS]), ALU.mult).then_inc(freed(("sO", u)), 1)

                def row_project(b):
                    ps = filled(dve, ("sproj", b))
                    row = y[:, b, :, :].rearrange("p q d -> p (q d)")
                    tt(row, ps[:, :], row, ALU.add).then_inc(freed(("sproj", b)), 1)
                    taken(dve, ("sproj", b))
                    norm(4, b)

                maxima(12)
                self_in(1)
                for u in range(len(uu)):
                    b, g = uu[u]
                    maxima(2)
                    if u:
                        back(u - 1)
                    maxima(3)
                    if u and g == 0:
                        row_project(b - 1)
                    maxima(3)
                back(len(uu) - 1)
                row_project(B - 1)

            dve.wait_ge(W["mask"], 16)
            V.tensor_scalar(maskb[:, :, :], masku[:, :, :], -BLOCKED, BLOCKED, ALU.mult, ALU.add)\
                .then_inc(mask_ready, 1)
            norm(0, 0)
            norm(0, 1)
            seq(V.tensor_copy(maskf[:, :, :], masku[:, :, :]))
            seq(V.tensor_reduce(allow[:, :, 0], maskf[:, :, :], AX.X, ALU.add))
            seq(V.reciprocal(allow[:, :, 1], allow[:, :, 0]))
            seq(V.tensor_scalar(allow[:, :, 2], allow[:, :, 1], 0.0, None, ALU.mult))
            prework(xa[0])
            cross(xa[0])
            prework(xa[1])
            ffn(0)
            cross(xa[1], ahead=AHEAD)
            self_attention()
            ffn(1)

        @block.gpsimd
        def _(pool):
            G = nc.gpsimd

            def seq(ins):
                link(pool, "pool", ins)

            for m in (ident, identb):
                seq(G.memset(m[:, :], 0.0))
            seq(G.affine_select(out=identb[:, :], in_=identb[:, :], compare_op=ALU.not_equal, fill=1.0, base=0,
                                pattern=[[-1, P]], channel_multiplier=1))
            G.affine_select(out=ident[:, :], in_=ident[:, :], compare_op=ALU.not_equal, fill=1.0, base=0,
                            pattern=[[-1, P]], channel_multiplier=1).then_inc(ident_ready, 1)
            pool.wait_ge(ident_ready, 1)
            seq(G.memset(mhalf[:, :], -0.5))
            seq(G.memset(own[:, :], 1.0))
            for i, (k, h) in enumerate(BLOCKS):
                c0 = CHUNKS[k][0]
                for base, sign in ((c0 - T * h, 1), (T * (h + 1) - 1 - c0, -1)):
                    seq(G.affine_select(out=own[:, i:i + 1], in_=own[:, i:i + 1], compare_op=ALU.is_ge, fill=0.0,
                                        base=base, pattern=[[0, 1]], channel_multiplier=sign))
            G.memset(v2[:, :, :], 0.0).then_inc(consts, 1)
            pool.wait_ge(consts, 1)

            def ones(a):
                return G.tensor_copy(a.VB[:, :, :, :, DH], own[:, :].unsqueeze(1).unsqueeze(1).broadcast_to(
                    [P, B, a.G, len(BLOCKS)]))

            ones(xa[0]).then_inc(consts, 1)
            pool.wait_ge(consts, 2)

            def norm(stage, b):
                pool.wait_ge(stats_ready, B * stage + b + 1)
                half = mhalf[:, 0:QT]
                twice = stage in (0, 3)
                seq(G.tensor_scalar(ve[:, b, :], mv[:, b, :, 1], EPS, None, ALU.add))
                ins = G.tensor_tensor(rstd[:, b, :], ve[:, b, :], half, ALU.pow)
                if twice:
                    seq(ins)
                    seq(G.tensor_tensor(v2[:, b, :], mv[:, b, :, 1], rstd[:, b, :], ALU.mult))
                    seq(G.tensor_tensor(v2[:, b, :], v2[:, b, :], rstd[:, b, :], ALU.mult))
                    seq(G.tensor_scalar(v2[:, b, :], v2[:, b, :], EPS, None, ALU.add))
                    ins = G.tensor_tensor(r2[:, b, :], v2[:, b, :], half, ALU.pow)
                    if stage == 0:
                        seq(ins)
                        ins = G.tensor_tensor(r2[:, b, :], r2[:, b, :], rstd[:, b, :], ALU.mult)
                ins.then_inc(rstd_ready, 1)

            def add_bias(stage, b):
                pool.wait_ge(xh_ready, B * stage + b + 1)
                if stage == 0 and b == 0:
                    pool.wait_ge(W["bo"], 48)
                o = x[:, b, :, :]
                G.tensor_tensor(o, o, bo[:, stage, :].unsqueeze(1).broadcast_to([P, QT, D]), ALU.add)\
                    .then_inc(xb_ready, 1)

            def expert_selections():
                taken(pool, ("kT", 0, H0 // 2 - 1))
                seq(G.memset(selc[:, :, :], 0.0))
                for part in range(3):
                    seq(G.affine_select(out=selc[:, :, :], in_=selc[:, :, :], compare_op=ALU.not_equal, fill=1.0,
                                        base=-E * part, pattern=[[-1, E], [0, P]], channel_multiplier=1))
                seq(G.iota(iotai[:, :], pattern=[[1, E]], base=0, channel_multiplier=0))
                G.tensor_copy(iota[:, :], iotai[:, :]).then_inc(consts, 1)
                pool.wait_ge(consts, 3)

            norm(0, 0)
            norm(0, 1)
            seq(ones(xa[1]))
            add_bias(0, 0)
            add_bias(0, 1)
            pool.wait_ge(xb_ready, B)
            expert_selections()
            pool.wait_ge(W["Ws"], 64)
            for i in range(2):
                for par in range(2):
                    G.tensor_copy(Wqk[:, i, 64 * par:64 * (par + 1)].rearrange("p (d c) -> p c d", d=DS),
                                  Ws[:, i, :].rearrange("p (c par d) -> p par c d", par=2, d=DS)[:, par, :, :])\
                        .then_inc(wqk_ready, 1)
                    pool.wait_ge(wqk_ready, 2 * i + par + 1)
            for stage in (1, 2):
                for b in range(B):
                    norm(stage, b)
                    add_bias(stage, b)
            pool.wait_ge(xb_ready, 3 * B)
            for b in range(B):
                seq(G.memset(stackk[b][:, :, :], 0.0))
                for par in range(2):
                    r = slice(32 + 64 * par, 64 + 64 * par)
                    seq(G.memset(stackk[b][r, par:HS:2, :], -1.0))
                    seq(G.memset(stackq[b][r, :, :], 0.0))
                if b == 0:
                    seq(G.memset(VS[b][:, :, :, DS:STRIP], 0.0))
                    G.memset(VS[b][:, :, :, DS:DS + 1], 1.0).then_inc(vpads_ready, 1)
                    pool.wait_ge(vpads_ready, 1)
                G.memset(zs[:, :, :, :], 0.0).then_inc(kpads_ready, 1)
                pool.wait_ge(kpads_ready, b + 1)
            norm(3, 0)
            norm(3, 1)
            pool.wait_ge(rstd_ready, 4 * B)
            seq(G.memset(VS[1][:, :, :, DS:STRIP], 0.0))
            G.memset(VS[1][:, :, :, DS:DS + 1], 1.0).then_inc(vpads_ready, 1)
            for b in range(B):
                norm(4, b)
                pool.wait_ge(xh_ready, B * 4 + b + 1)
                G.tensor_tensor(x[:, b, :, :], x[:, b, :, :], y[:, b, :, :], ALU.add).then_inc(xb_ready, 1)

        @block.sync
        def _(sp):
            def load(dst, src, name):
                sp.dma_start(dst, src).then_inc(W[name], 16)

            def row(v):
                return v.rearrange("(a d) -> a d", a=1)

            for b in range(B):
                load(x[:, b, :, :], t["x"][b].rearrange("(q p) d -> p q d", p=P), "x")
            load(xa[0].Wq[:, :], t["L0_xattn_Wq"], "Wq0")
            load(masku[:, :, :], t["mask_1x1xSxS2_bk0"][0, 0].rearrange("(q p) k -> p q k", p=P), "mask")
            for i, k in enumerate(("L0_xattn_ln_gamma", "L0_xattn_ln_beta", "L1_ffn_g1", "L1_ffn_b1",
                                   "L1_ffn_g2", "L1_ffn_b2")):
                load(rows[i:i + 1, :], row(t[k]), "rows")
            load(rows[6:14, :], t["L0_ffn_up_b"], "rows")
            load(rows[14:15, :], row(t["L0_ffn_sh_up_b"]), "rows")
            load(gwr[:, :], t["L0_ffn_gate_w"], "gate")
            for i, k in enumerate(("L0_xattn_bo", "L0_ffn_sh_down_b", "L1_xattn_bo")):
                load(bo[:, i, :], t[k].partition_broadcast(P), "bo")
            load(xa[0].Wo[:, :, :], t["L0_xattn_Wo"].rearrange("(c p) d -> p c d", p=P), "Wo0")
            load(xa[1].Wq[:, :], t["L1_xattn_Wq"], "Wq1")
            load(xa[1].Wk[:, :], t["L1_xattn_Wk"], "Wk1")
            load(xa[1].Wv[:, :], t["L1_xattn_Wv"], "Wv1")
            load(upw[:, 0:E, :], t["L0_ffn_up_w"].rearrange("e d h -> d e h"), "upw")
            load(upw[:, E, :], t["L0_ffn_sh_up_w"], "upw")
            load(dnw[:, 0:E, :], t["L0_ffn_down_w"].rearrange("e h d -> h e d"), "dnw")
            load(dnw[:, E, :], t["L0_ffn_sh_down_w"], "dnw")
            load(dnb[:, :], t["L0_ffn_down_b"], "dnw")
            load(xa[1].Wo[:, :, :], t["L1_xattn_Wo"].rearrange("(c p) d -> p c d", p=P), "Wo1")
            for i, k in enumerate(("Wq", "Wk", "Wv", "Wo")):
                load(Ws[:, i, :], t[f"L1_ffn_{k}"], "Ws")
            load(Wg[:, :], t["L1_ffn_Wg"], "Wg")
            load(W1[:, :, :], t["L1_ffn_W1"].rearrange("e d h -> d e h"), "W1")
            load(W2[:, :, :], t["L1_ffn_W2"].rearrange("(c i) h d -> (i h) c d", i=2), "W2")

            def fill_stacks(b):
                for i in range(2):
                    copies = (((0, slice(0, 3)), (1, slice(3, 5)), (2, slice(5, 6))),
                              ((0, slice(0, 4, 3)), (0, slice(5, 6)), (1, slice(1, 5, 3)), (2, slice(2, 3))))[i]
                    for j, to in copies:
                        sp.wait_ge(part_ready, 3 * (2 * b + i) + j + 1)
                        for par in range(2):
                            dst = scratch[b, i, par, to].rearrange("r p s -> p r s")
                            src = qk[i][j][64 * par:64 * (par + 1), :].unsqueeze(1)
                            sp.dma_start(dst, src.broadcast_to([64, dst.shape[1], S])).then_inc(parked[i], 16)
                for i in range(2):
                    sp.wait_ge(parked[i], 16 * PARKS[i] * (b + 1))
                    if i == 0:
                        sp.wait_ge(kpads_ready, b + 1)
                    for par in range(2):
                        src = scratch[b, i, par].rearrange("r (d c) s -> (r d) c s", d=DS)
                        rows_ = slice(64 * par, 64 * par + 6 * DS)
                        dst = stackq[b][rows_, :, :] if i == 0 else stackk[b][rows_, par:HS:2, :]
                        sp.dma_start(dst, src).then_inc(stacked, 16)

            def fill_maxima(u):
                b, g = units[2][u]
                taken(sp, ("smT", u))
                for part in range(2):
                    for pair in range(2):
                        m0 = G4 * part + 2 * pair
                        sp.dma_start(stackq[b][48 + part:P:64, 2 * g + pair, :], mT[m0:m0 + 2, u % 2, :])\
                            .then_inc(mrow_ready, 16)

            fill_stacks(0)
            fill_maxima(0)
            fill_stacks(1)
            for u in range(1, len(units[2])):
                fill_maxima(u)
            for b in range(B):
                taken(sp, ("dn", 1, b))
                sp.dma_start(out[b].rearrange("(q p) d -> p q d", p=P), x[:, b, :, :]).then_inc(stored, 16)
            sp.wait_ge(stored, 16 * B)


_INS = ["x", "ctx_768", "mask_1x1xSxS2_bk0", "L0_xattn_ln_gamma", "L0_xattn_ln_beta", "L0_xattn_Wq",
        "L0_xattn_Wkv", "L0_xattn_Wo", "L0_xattn_bo", "L0_ffn_gate_w", "L0_ffn_up_w", "L0_ffn_up_b",
        "L0_ffn_down_w", "L0_ffn_down_b", "L0_ffn_sh_up_w", "L0_ffn_sh_up_b", "L0_ffn_sh_down_w",
        "L0_ffn_sh_down_b", "L1_xattn_Wq", "L1_xattn_Wk", "L1_xattn_Wv", "L1_xattn_Wo", "L1_xattn_bo",
        "L1_ffn_Wq", "L1_ffn_Wk", "L1_ffn_Wv", "L1_ffn_Wo", "L1_ffn_g1", "L1_ffn_b1", "L1_ffn_g2", "L1_ffn_b2",
        "L1_ffn_Wg", "L1_ffn_W1", "L1_ffn_W2"]


def kernel(**inputs):
    import numpy as _np
    import concourse.bacc as _bacc
    from concourse import mybir as _mybir
    from concourse.bass_utils import run_bass_kernel_spmd as _run

    nc = _bacc.Bacc("TRN2", target_bir_lowering=False, num_devices=1)
    arrays, aps = {}, {}
    for name in _INS:
        a = _np.ascontiguousarray(inputs[name])
        arrays[f"in_{name}_dram"] = a
        aps[name] = nc.dram_tensor(f"in_{name}_dram", a.shape, _mybir.dt.from_np(a.dtype),
                                   kind="ExternalInput").ap()
    shape = inputs["x"].shape
    out = nc.dram_tensor("out_0_dram", shape, _mybir.dt.float32, kind="ExternalOutput").ap()
    build(nc, aps, out)
    r = _run(nc, [arrays], core_ids=[0])
    return r.results[0]["out_0_dram"]
```

```python
import struct
from contextlib import ExitStack

import concourse.bass as bass
from concourse import mybir

F32 = mybir.dt.float32
BF16 = mybir.dt.bfloat16
U32 = mybir.dt.uint32
ALU = mybir.AluOpType
ACT = mybir.ActivationFunctionType
AX = mybir.AxisListType

P = 128
EPS = 1e-5
MINUS_ONES = struct.unpack("<f", bytes([0x80, 0xBF] * 2))[0]
BLOCKED = -float(2.0 ** 100)


def build(nc, t, out):
    B, S, D = t["x"].shape
    _, T, C = t["ctx_768"].shape
    QT = S // P
    R = T - P
    STRIP = 32
    G4 = 4
    DH = 64
    H0 = t["L0_xattn_Wq"].shape[1] // DH
    H1 = t["L1_xattn_Wq"].shape[1] // DH
    E = t["L0_ffn_up_w"].shape[0]
    HS, DS = 16, 8
    XSCALE = float(DH) ** -0.5
    SSCALE = float(DS) ** -0.5
    EH = t["L1_ffn_W1"].shape[2]
    CHUNKS = [(c, min(P, G4 * T - c), list(range(c // T, (min(c + P, G4 * T) - 1) // T + 1)))
              for c in range(0, G4 * T, P)]
    BLOCKS = [(k, h) for k, (_, _, hs) in enumerate(CHUNKS) for h in hs]
    FIRST = [BLOCKS.index((k, hs[0])) for k, (_, _, hs) in enumerate(CHUNKS)]
    assert (B, S, D, DH, QT) == (2, 512, 128, 64, 4) and R <= STRIP and HS * DS == D and 2 * EH == P

    ctx = ExitStack()
    with ctx:
        def sb(name, shape, dt=F32):
            return ctx.enter_context(nc.sbuf_tensor(name, shape, dt))

        def sem(name):
            return ctx.enter_context(nc.semaphore(name))

        class Room:
            def __init__(self, tensor):
                self.tensor, self.used = tensor, 0

            def take(self, n, dt=F32):
                v = self.tensor[:, self.used:self.used + n]
                self.used += n
                return v if dt is F32 else v.bitcast(dt)

        NPT = 16
        PT = sb("PT", [P, NPT, S])
        m = Room(PT[:, 10:NPT, :].rearrange("p c s -> p (c s)"))
        x = sb("x", [P, B, QT, D])
        OT_ = sb("OT", [P, (H0 // 2 + 1) * S])
        xh = sb("xh", [P, B, QT, D])
        xT = sb("xT", [P, B, S])
        ident = sb("ident", [P, P])
        identb = sb("identb", [P, P], BF16)
        rows = sb("rows", [16, P])
        cols = sb("cols", [P, 16])
        bo = sb("bo", [P, 3, D])
        mhalf = sb("mhalf", [P, 16])
        stats = sb("stats", [P, B, QT, 6])
        mv = sb("mv", [P, B, QT, 2])
        ve = sb("ve", [P, B, QT])
        rstd = sb("rstd", [P, B, QT])
        v2 = sb("v2", [P, B, QT])
        r2 = sb("r2", [P, B, QT])
        ctxm = m.take(B * C).rearrange("p (b c) -> p b c", b=B)
        ctxr = m.take(B * C).rearrange("p (b c) -> p b c", b=B)[0:STRIP]
        ctxT = m.take(B * G4 * T).rearrange("p (b r k) -> p b r k", b=B, r=G4)
        masku = m.take(QT * T // 4, mybir.dt.uint8).rearrange("p (q k) -> p q k", q=QT)
        maskb = m.take(QT * T // 2, BF16).rearrange("p (q k) -> p q k", q=QT)
        Wqk = m.take(2 * D).rearrange("p (i d) -> p i d", i=2)
        maskf = OT_[:, 0:QT * T].rearrange("p (q k) -> p q k", q=QT)
        allow = sb("allow", [P, QT, 4])
        own = sb("own", [P, len(BLOCKS)])
        class Layer:
            pass

        xa = []
        for n, H in enumerate((H0, H1)):
            a = Layer()
            a.n, a.H, a.G = n, H, H // G4
            words = H * DH * 2 + H // 2 * D + (H * B * T if n else 0) + B * H * T
            words += B * H // G4 * len(BLOCKS) * DH
            if n == 0:
                self_words = (B + 3 + 2 + B * HS // 4 + B * HS // 2) * S + QT * HS * STRIP
                words = max(words + 2 * (E + 1) * P, self_words)
            a.space = sb(f"space{n}", [P, words])
            m = Room(a.space)
            a.Wk = sb(f"Wk{n}", [P, H * DH])
            a.Wv = sb(f"Wv{n}", [P, H * DH])
            a.Wq = m.take(H * DH)
            a.WqT = m.take(H // 2 * P).rearrange("p (c k) -> p c k", k=P)
            a.Wo = m.take(H // 2 * D).rearrange("p (c d) -> p c d", d=D)
            kt = m.take(H * B * T) if n else PT[:, 0:10, :].rearrange("p c s -> p (c s)")[:, 0:H * B * T]
            a.KT = kt.rearrange("p (h b k) -> p h b k", h=H, b=B)
            a.KP = m.take(B * H * T).rearrange("p (b h k) -> p b h k", b=B, h=H)
            a.VB = m.take(B * a.G * len(BLOCKS) * DH).rearrange("p (b g k d) -> p b g k d", b=B, g=a.G, d=DH)
            if n == 0:
                upw = m.take((E + 1) * P).rearrange("p (e h) -> p e h", h=P)
                dnw = m.take((E + 1) * D).rearrange("p (e d) -> p e d", d=D)
            xa.append(a)
        OT = OT_[:, :].rearrange("p (c s) -> p c s", s=S)
        spare = sb("spare", [P, 2 * QT * G4 * DH])
        PQ_SLOTS = 6
        first_slots = PT[:, 5:10, :].rearrange("p c s -> p (c s)")

        def pq(n, u, q):
            i = (QT * u + q) % PQ_SLOTS
            w = G4 * T
            return first_slots[:, i * w:(i + 1) * w] if i < 4 else spare[:, (i - 4) * w:(i - 3) * w]

        def hidden(n, b):
            if n == b:
                return PT[:, 0:E + 1, :]
            return OT if n == 0 else OT[:, B:, :]

        mx = sb("mx", [P, 2, QT, G4])
        nm = sb("nm", [P, 2, QT, G4])
        mr = sb("mr", [P, 2, QT, G4])
        mparts = sb("mparts", [P, 2, QT, 2, G4], BF16)
        cT = sb("cT", [3 * E, 2, S], BF16)
        mT = xa[1].Wk[0:2 * G4, :].bitcast(BF16).rearrange("p (i s) -> p i s", i=2)
        z = sb("z", [P, 2, QT, G4])
        rz = sb("rz", [P, 2, QT, G4])
        gwr = sb("gwr", [E, D])
        gateT = sb("gateT", [P, E])
        dnb = sb("dnb", [E, D])
        Wg = sb("Wg", [P, E])
        W1 = sb("W1", [P, E, EH])
        W2 = sb("W2", [P, E // 2, D])
        lg = sb("lg", [P, B, QT, E])
        ex = sb("ex", [P, B, QT, E])
        g1 = sb("g1", [P, B, QT, 4])
        top = sb("top", [P, B, QT, 8])
        topi = sb("topi", [P, B, QT, 8], U32)
        topf = sb("topf", [P, B, QT, 8])
        iota = sb("iota", [P, E])
        iotai = sb("iotai", [P, E], mybir.dt.int32)
        oh = sb("oh", [P, B, QT, 2, E])
        comb = sb("comb", [P, B, QT, E])
        combT = xa[0].Wv[0:E, :].rearrange("p (b s) -> p b s", b=B)
        cr = sb("cr", [P, B, QT, E])
        cparts = sb("cparts", [P, B, QT, 3, E], BF16)
        selc = xa[0].Wk[0:3 * E, S:2 * S].bitcast(BF16).rearrange("p (e k) -> p e k", k=P)
        Ws = sb("Ws", [P, 4, D])
        m = Room(xa[0].space)
        y = m.take(B * QT * D).rearrange("p (b q d) -> p b q d", b=B, q=QT)
        qk = [[m.take(S // 2, BF16) for _ in range(3)] for _ in range(2)]
        qkr = m.take(2 * S).rearrange("p (i s) -> p i s", i=2)
        stackq = [m.take(HS // 2 * S // 2, BF16).rearrange("p (c s) -> p c s", s=S) for _ in range(B)]
        stackk = [m.take(HS * S // 2, BF16).rearrange("p (h s) -> p h s", s=S) for _ in range(B)]
        wide_v = QT * HS * STRIP
        VS = [m.take(wide_v), xa[1].space[:, 0:wide_v]]
        VS = [v.rearrange("p (q h d) -> p q h d", q=QT, h=HS) for v in VS]
        m = Room(spare)
        OS = m.take(2 * S).rearrange("p (i s) -> p i s", i=2)
        On = m.take(QT * HS * DS).rearrange("p (q h d) -> p q h d", q=QT, h=HS)
        zs = sb("zs", [P, 2, QT, G4])
        scratch = nc.dram_tensor("parts_scratch", [B, 2, 6, P, S], BF16).ap()

        pS = [ctx.enter_context(nc.psum_tensor(f"pS{i}", [P, 1024], F32)) for i in range(2)]
        pT = [ctx.enter_context(nc.psum_tensor(f"pT{i}", [P, 512], F32)) for i in range(2)]
        pC = [ctx.enter_context(nc.psum_tensor(f"pC{i}", [P, 512], F32)) for i in range(2)]
        RING = {"S": pS, "T": pT, "C": pC}
        FULL = {r: [sem(f"{r}{i}_full") for i in range(2)] for r in RING}
        FREE = {r: [sem(f"{r}{i}_free") for i in range(2)] for r in RING}
        uses = {r: 0 for r in RING}
        at = {}

        W = {k: sem(f"ld_{k}") for k in ("x", "ctx", "rows", "mask", "Wq0", "Wk0", "Wv0", "Wo0", "bo", "gate",
                                         "upw", "dnw", "Wq1", "Wk1", "Wv1", "Wo1", "Wg", "Ws", "W1", "W2")}
        ident_ready = sem("ident_ready")
        consts = sem("consts")
        ctx_ready = sem("ctx_ready")
        ctx_pads = sem("ctx_pads")
        kt_pads = sem("kt_pads")
        p_ready = sem("p_ready")
        nm_ready = sem("nm_ready")
        stats_ready = sem("stats_ready")
        rstd_ready = sem("rstd_ready")
        xh_ready = sem("xh_ready")
        xb_ready = sem("xb_ready")
        mask_ready = sem("mask_ready")
        mp_ready = sem("mp_ready")
        lg_ready = sem("lg_ready")
        ex_ready = sem("ex_ready")
        rounded = [sem("q_rounded"), sem("k_rounded")]
        thirds = [sem("q_thirds"), sem("k_thirds")]
        cparts_ready = sem("cparts_ready")
        kpads_ready = sem("kpads_ready")
        wqk_ready = sem("wqk_ready")
        vpads_ready = sem("vpads_ready")
        parked = [sem("q_parked"), sem("k_parked")]
        stacked = sem("stacked")
        mrow_ready = sem("mrow_ready")
        p_used = sem("p_used")
        stored = sem("stored")
        chain = {e: sem(f"{e}_chain") for e in ("dve", "act", "pool")}
        links = dict.fromkeys(chain, 0)

        block = ctx.enter_context(nc.Block())
        units = [[(b, g) for b in range(B) for g in range(H // G4)] for H in (H0, H1, HS)]
        AHEAD = units[1].index((1, H1 // G4 - 1))
        PARKS = (3, 4)
        STACK_LOADS = 4

        def filled(eng, key):
            ring, buf, turn = at[key]
            eng.wait_ge(FULL[ring][buf], turn + 1)
            return RING[ring][buf]

        def freed(key):
            ring, buf, _ = at[key]
            return FREE[ring][buf]

        def taken(eng, key):
            eng.wait_ge(freed(key), at[key][2] + 1)

        def link(eng, name, ins):
            links[name] += 1
            ins.then_inc(chain[name], 1)
            eng.wait_ge(chain[name], links[name])

        @block.tensor
        def _(pe):
            mm = nc.tensor.matmul
            tr = nc.tensor.transpose

            def claim(ring, key):
                buf, turn = uses[ring] % 2, uses[ring] // 2
                uses[ring] += 1
                assert key not in at, key
                at[key] = (ring, buf, turn)
                if turn:
                    pe.wait_ge(FREE[ring][buf], turn)
                return RING[ring][buf]

            def full(key):
                return FULL[at[key][0]][at[key][1]]

            def xt(stage, b, ring="C"):
                pe.wait_ge(xh_ready, stage * B + b + 1)
                ps = claim(ring, ("xT", stage, b))
                for q in range(QT):
                    last = tr(ps[:, q * P:(q + 1) * P], xh[:, b, q, :], ident[:, :])
                last.then_inc(full(("xT", stage, b)), 1)

            def context():
                pe.wait_ge(ident_ready, 1)
                pe.wait_ge(W["ctx"], 32)
                ps = claim("T", "ctxT")
                for b in range(B):
                    tr(ps[0:C, b * T:b * T + P], ctxm[:, b, :], ident[:, :])
                    last = tr(ps[0:C, b * T + P:(b + 1) * T], ctxr[0:R, b, :], ident[0:R, 0:R])
                last.then_inc(full("ctxT"), 1)

            def columns():
                pe.wait_ge(W["rows"], 16 * 8)
                ps = claim("C", "cols")
                tr(ps[:, 0:15], rows[0:15, :], ident[0:15, 0:15]).then_inc(full("cols"), 1)
                pe.wait_ge(W["gate"], 16)
                ps = claim("C", "gateT")
                tr(ps[:, 0:E], gwr[:, :], ident[0:E, 0:E]).then_inc(full("gateT"), 1)

            def weightsT(a):
                n = a.n
                pe.wait_ge(W[f"Wq{n}"], 16)
                for c0 in range(0, a.H // 2, 4):
                    ps = claim("T", ("wqT", n, c0))
                    for c in range(c0, c0 + 4):
                        last = tr(ps[:, (c - c0) * P:(c - c0 + 1) * P], a.Wq[:, c * P:(c + 1) * P], ident[:, :])
                    last.then_inc(full(("wqT", n, c0)), 1)

            def keysT(a):
                n = a.n
                pe.wait_ge(W[f"Wk{n}"], 16)
                pe.wait_ge(ctx_ready, 1)
                pe.wait_ge(ctx_pads, n + 1)
                for c in range(a.H // 2):
                    ps = claim("C", ("kT", n, c))
                    mm(ps[:, 0:B * T].rearrange("p (b k) -> p b k", b=B), a.Wk[:, c * P:(c + 1) * P],
                       ctxT[:, :, 0, :], start=True, stop=True).then_inc(full(("kT", n, c)), 1)

            def keys(a, h):
                n, c = a.n, h // 2
                taken(pe, ("wqT", n, c // 4 * 4))
                taken(pe, ("kT", n, c))
                if n == 0 and h == 0:
                    pe.wait_ge(kt_pads, 1)
                ps = claim("T", ("kp", n, h))
                mm(ps[:, 0:B * T], a.WqT[:, c, :], a.KT[:, h, :, :].rearrange("p b k -> p (b k)"),
                   start=True, stop=True).then_inc(full(("kp", n, h)), 1)

            def context_values(a, b, ks):
                n = a.n
                if b == 0 and ks[0] == 0:
                    pe.wait_ge(W[f"Wv{n}"], 16)
                    taken(pe, "ctxT")
                wv = a.Wv[:, :].rearrange("c (g j d) -> c g j d", j=G4, d=DH)
                for k in ks:
                    c0, size, hs = CHUNKS[k]
                    ps = claim("C", ("v", n, b, k))
                    o = ps[0:size, 0:a.G * len(hs) * DH].rearrange("p (g j d) -> p g j d", g=a.G, d=DH)
                    mm(o, ctxT[:, b, :, :].rearrange("c r k -> c (r k)")[:, c0:c0 + size],
                       wv[:, :, hs[0]:hs[-1] + 1, :], start=True, stop=True).then_inc(full(("v", n, b, k)), 1)

            def scores(a, u, q):
                n, uu = a.n, units[a.n]
                if u == len(uu):
                    return
                b, g = uu[u]
                if q == 0:
                    if n == 0 and u == 0:
                        pe.wait_ge(mask_ready, 1)
                    if g == 0:
                        xt(2 * n, b)
                        taken(pe, ("xT", 2 * n, b))
                    taken(pe, ("kp", n, G4 * g + 2))
                    taken(pe, ("kp", n, G4 * g + 3))
                ps = claim("S", ("s", n, u, q))
                for i in range(2):
                    last = mm(ps[:, 512 * i:512 * i + 2 * T], xT[:, b, q * P:(q + 1) * P],
                              a.KP[:, b, G4 * g + 2 * i:G4 * g + 2 * i + 2, :].rearrange("p h k -> p (h k)"),
                              start=True, stop=(n == 1))
                    if n == 0:
                        last = mm(ps[:, 512 * i:512 * i + 2 * T].rearrange("p (j k) -> p j k", j=2),
                                  identb[:, :], maskb[:, q, :].unsqueeze(1).broadcast_to([P, 2, T]),
                                  start=False, stop=True)
                last.then_inc(full(("s", n, u, q)), 1)

            def cross(a, ahead=None):
                n, uu = a.n, units[a.n]

                def turn(u):
                    pe.wait_ge(p_ready, QT * (n * len(units[0]) + u + 1))
                    for k, (c0, size, hs) in enumerate(CHUNKS):
                        ps = claim("TTCTC"[k], ("pt", n, u, k))
                        for q in range(QT):
                            last = tr(ps[0:size, q * P:(q + 1) * P], pq(n, u, q)[:, c0:c0 + size], ident[:, :])
                        last.then_inc(full(("pt", n, u, k)), 1)

                def values(u, c):
                    b, g = uu[u]
                    pair = {2 * c, 2 * c + 1}
                    for k in (len(CHUNKS) - 1, len(CHUNKS) - 2):
                        if g == 0:
                            taken(pe, ("v", n, b, k))
                        taken(pe, ("pt", n, u, k))
                    ps = claim("C", ("o", n, u, c))
                    parts_ = sorted(((k, sorted(pair & set(hs))) for k, (_, _, hs) in enumerate(CHUNKS)
                                     if pair & set(hs)), key=lambda e: -len(e[1]))
                    for i, (k, hs) in enumerate(parts_):
                        size, block = CHUNKS[k][1], BLOCKS.index((k, hs[0]))
                        last = mm(ps[DH * (hs[0] - 2 * c):DH * (hs[-1] - 2 * c + 1), :],
                                  a.VB[0:size, b, g, block:block + len(hs), :].rearrange("p j d -> p (j d)"),
                                  PT[0:size, k, :], start=(i == 0), stop=(i == len(parts_) - 1),
                                  skip_group_check=True)
                    last.then_inc(full(("o", n, u, c)), 1)

                def project(u):
                    b, g = uu[u]
                    pe.wait_ge(W[f"Wo{n}"], 16)
                    taken(pe, ("o", n, u, 1))
                    ps = claim("C", ("proj", n, b))
                    for q in range(QT):
                        for c in range(a.H // 2):
                            last = mm(ps[:, q * D:(q + 1) * D], OT[:, c, q * P:(q + 1) * P], a.Wo[:, c, :],
                                      start=(c == 0), stop=(c == a.H // 2 - 1))
                    last.then_inc(full(("proj", n, b)), 1)

                if n == 0:
                    scores(a, 0, 0)
                scores(a, 0, 1)
                if n == 0:
                    context_values(a, 0, (0, 1, 2, 3, 4))
                scores(a, 0, 2)
                if n == 0:
                    context_values(a, 1, (0, 1))
                scores(a, 0, 3)
                if n == 0:
                    context_values(a, 1, (2, 3, 4))
                for u in range(len(uu)):
                    row_end = u and uu[u - 1][1] == a.G - 1
                    scores(a, u + 1, 0)
                    scores(a, u + 1, 1)
                    if row_end:
                        project(u - 1)
                    turn(u)
                    scores(a, u + 1, 2)
                    if ahead == u:
                        self_in(0)
                    scores(a, u + 1, 3)
                    values(u, 0)
                    values(u, 1)
                if n == 0:
                    weightsT(xa[1])
                    keysT(xa[1])
                    for h in range(4):
                        keys(xa[1], h)
                project(len(uu) - 1)

            def gate(n, b, ring="C"):
                taken(pe, ("xT", 1 + 3 * n, b))
                if n == 0:
                    taken(pe, "gateT")
                else:
                    pe.wait_ge(W["Wg"], 16)
                ps = claim(ring, ("gate", n, b))
                for q in range(QT):
                    last = mm(ps[:, q * E:(q + 1) * E], xT[:, b, q * P:(q + 1) * P],
                              gateT[:, :] if n == 0 else Wg[:, :], start=True, stop=True)
                last.then_inc(full(("gate", n, b)), 1)

            def up(n, b, e):
                if e == 0:
                    pe.wait_ge(W["upw"] if n == 0 else W["W1"], 32 if n == 0 else 16)
                if n == 0:
                    ps = claim("T", ("up", n, b, e))
                    last = mm(ps[:, :], upw[:, e, :], xT[:, b, :], start=True, stop=True)
                else:
                    ps = claim("S", ("up", n, b, e))
                    for i in range(2):
                        w = W1[:, 4 * e + 2 * i:4 * e + 2 * i + 2, :].rearrange("p e h -> p (e h)")
                        last = mm(ps[:, S * i:S * (i + 1)], w, xT[:, b, :], start=True, stop=True)
                last.then_inc(full(("up", n, b, e)), 1)

            def weight_rows(n, b, ring="C"):
                pe.wait_ge(cparts_ready, B * n + b + 1)
                ps = claim(ring, ("cT", n, b))
                for q in range(QT):
                    last = tr(ps[0:3 * E, q * 64:(q + 1) * 64].bitcast(BF16),
                              cparts[:, b, q, :, :].rearrange("p a e -> p (a e)"), identb[:, :])
                last.then_inc(full(("cT", n, b)), 1)
                if n == 0:
                    ps = claim("C", ("combT", b))
                    for q in range(QT):
                        last = tr(ps[0:E, q * P:(q + 1) * P], comb[:, b, q, :], ident[:, :])
                    last.then_inc(full(("combT", b)), 1)

            def weights(n, b, e):
                taken(pe, ("cT", n, b))
                if (n, b, e) == (0, 0, 0):
                    pe.wait_ge(consts, 2)
                if n == 0:
                    ps = claim("T", ("cb", n, b, e))
                    last = mm(ps[:, :], selc[:, e, :], cT[:, b, :], start=True, stop=True)
                else:
                    ps = claim("S", ("cb", n, b, e))
                    for i in range(4):
                        last = mm(ps[EH * (i % 2):EH * (i % 2 + 1), S * (i // 2):S * (i // 2 + 1)],
                                  selc[:, 4 * e + i, 0:EH], cT[:, b, :], start=True, stop=True)
                last.then_inc(full(("cb", n, b, e)), 1)

            def downs(n, b, e, qs=range(QT)):
                first, last_e = (-2, E - 1) if n == 0 else (0, E // 2 - 1)
                if e == first and qs[0] == 0:
                    claim("S", ("dn", n, b))
                    pe.wait_ge(W["dnw"] if n == 0 else W["W2"], 48 if n == 0 else 16)
                ps = RING["S"][at[("dn", n, b)][1]]
                if e == -2:
                    taken(pe, ("combT", b))
                elif e == -1:
                    taken(pe, ("up", n, b, E))
                elif n == 0:
                    taken(pe, ("cb", n, b, e))
                else:
                    taken(pe, ("cb", n, b, e // 2))
                for q in qs:
                    t_ = slice(q * P, (q + 1) * P)
                    if e == -2:
                        h, w = combT[:, b, t_], dnb[:, :]
                    else:
                        k = e % (E + 1) if n == 0 else e
                        h, w = hidden(n, b)[:, k, t_], dnw[:, k, :] if n == 0 else W2[:, k, :]
                    last = mm(ps[:, q * D:(q + 1) * D], h, w, start=(e == first and q == 0),
                              stop=(e == last_e), skip_group_check=True)
                if e == last_e and qs[-1] == QT - 1:
                    last.then_inc(full(("dn", n, b)), 1)

            def ffn0():
                for b in range(B):
                    xt(1, b)
                    gate(0, b)
                    if b == 1:
                        for r in range(B):
                            context_values(xa[1], r, (0, 1, 2, 3, 4))
                    for e in range(E + 1):
                        up(0, b, e)
                weight_rows(0, 0)
                weights(0, 0, 0)
                weights(0, 0, 1)
                for b in range(B):
                    downs(0, b, -2)
                    downs(0, b, -1)
                    for e in range(E):
                        downs(0, b, e)
                        if b == 0 and e == 3:
                            weight_rows(0, 1)
                        if e + 2 < E:
                            weights(0, b, e + 2)
                        elif b == 0:
                            weights(0, 1, e + 2 - E)
                        if b == 0 and e % 2:
                            keys(xa[1], 4 + e // 2)
                        if b == 1 and e == 5:
                            scores(xa[1], 0, 0)

            def ffn1_first(u, kt):
                u -= len(units[2]) - 3
                if (u, kt) == (0, 0):
                    xt(4, 0, "T")
                if (u, kt) == (0, 1):
                    gate(1, 0, "S")
                if (u, kt) == (0, 2):
                    up(1, 0, 0)
                if (u, kt) == (0, 3):
                    up(1, 0, 1)
                if (u, kt) == (1, 1):
                    weight_rows(1, 0, "T")
                if u == 1 and kt >= 2:
                    weights(1, 0, kt - 2)
                if u == 2:
                    downs(1, 0, kt, (0, 1))

            def ffn1_last():
                xt(4, 1)
                gate(1, 1)
                for e in range(2):
                    up(1, 1, e)
                weight_rows(1, 1)
                for e in range(2):
                    weights(1, 1, e)
                for e in range(E // 2):
                    downs(1, 1, e)

            def self_in(b):
                pe.wait_ge(W["Ws"], 64)
                pe.wait_ge(wqk_ready, 2)
                xt(3, b)
                taken(pe, ("xT", 3, b))
                for i in range(2):
                    ps = claim("C", ("qk", b, i))
                    mm(ps[:, :], Wqk[:, i, :], xT[:, b, :],
                       start=True, stop=True).then_inc(full(("qk", b, i)), 1)
                ps = claim("C", ("vs", b))
                for q in range(QT):
                    last = mm(ps[:, q * D:(q + 1) * D], xT[:, b, q * P:(q + 1) * P], Ws[:, 2, :],
                              start=True, stop=True)
                last.then_inc(full(("vs", b)), 1)

            def self_attention():
                uu, G = units[2], HS // G4

                pairs = iter([(u, k) for u in range(len(uu)) for k in range(8)])

                def score_pair():
                    u, k = next(pairs, (None, None))
                    if u is None:
                        return
                    b, g = uu[u]
                    if g == 0 and k == 0:
                        pe.wait_ge(stacked, 16 * STACK_LOADS * (b + 1))
                    q = k // 2
                    ps = claim("S", ("ss", u, k))
                    for i in range(2):
                        h = G4 * g + 2 * (k % 2) + i
                        last = mm(ps[:, 512 * i:512 * i + 512], stackq[b][:, h // 2, q * P:(q + 1) * P],
                                  stackk[b][:, h, :], start=True, stop=True)
                    last.then_inc(full(("ss", u, k)), 1)

                def values(u, kt, pv):
                    b, g = uu[u]
                    taken(pe, ("sst", u, kt, G4 - 1))
                    for j in range(G4):
                        last = mm(pv[STRIP * j:STRIP * (j + 1), :], VS[b][:, kt, G4 * g + j, :],
                                  PT[:, (4 * kt + j) % NPT, :], start=(kt == 0), stop=(kt == QT - 1))
                    last.then_inc(full(("spv", u)) if kt == QT - 1 else p_used, 1)

                def maxima(u):
                    pe.wait_ge(mp_ready, u + 1)
                    ps = claim("T", ("smT", u))
                    for q in range(QT):
                        last = tr(ps[0:8, q * 64:(q + 1) * 64].bitcast(BF16),
                                  mparts[:, u % 2, q, :, :].rearrange("p a h -> p (a h)"), identb[:, :])
                    last.then_inc(full(("smT", u)), 1)

                def back(u):
                    taken(pe, ("spv", u))
                    ps = claim("C", ("sO", u))
                    for q in range(QT):
                        last = tr(ps[:, q * P:(q + 1) * P], OS[:, u % 2, q * P:(q + 1) * P], ident[:, :])
                    last.then_inc(full(("sO", u)), 1)

                def row_outT(b):
                    taken(pe, ("sO", b * G + G - 1))
                    ps = claim("T", ("onT", b))
                    for q in range(QT):
                        last = tr(ps[:, q * P:(q + 1) * P], On[:, q, :, :].rearrange("p h d -> p (h d)"), ident[:, :])
                    last.then_inc(full(("onT", b)), 1)

                def row_project(b):
                    taken(pe, ("onT", b))
                    ps = claim("S", ("sproj", b))
                    for q in range(QT):
                        last = mm(ps[:, q * D:(q + 1) * D], OT[:, b, q * P:(q + 1) * P], Ws[:, 3, :],
                                  start=True, stop=True)
                    last.then_inc(full(("sproj", b)), 1)

                for _ in range(10):
                    score_pair()
                maxima(0)
                for _ in range(2):
                    score_pair()
                self_in(1)
                for u in range(len(uu)):
                    b, g = uu[u]
                    if g == 0:
                        taken(pe, ("vs", b))
                    pe.wait_ge(mrow_ready, 16 * 4 * (u + 1))
                    for kt in range(QT):
                        for j in range(G4):
                            h = G4 * g + j
                            ps = claim("T", ("sst", u, kt, j))
                            mm(ps[:, :], stackk[b][:, h, kt * P:(kt + 1) * P], stackq[b][:, h // 2, :],
                               start=True, stop=True).then_inc(full(("sst", u, kt, j)), 1)
                            if j == 1:
                                score_pair()
                                if u == len(uu) - 1:
                                    ffn1_first(u, kt)
                            if j == 2 and kt == 0:
                                pv = claim("C", ("spv", u))
                                if u:
                                    back(u - 1)
                            elif j == 2:
                                values(u, kt - 1, pv)
                        if kt == 2 and u + 1 < len(uu):
                            maxima(u + 1)
                        if u and g == 0 and kt == 1:
                            row_outT(b - 1)
                        if u and g == 0 and kt == 2:
                            row_project(b - 1)
                        score_pair()
                        if u < len(uu) - 1:
                            ffn1_first(u, kt)
                        else:
                            downs(1, 0, kt, (2, 3))
                    values(u, QT - 1, pv)
                back(len(uu) - 1)
                row_outT(B - 1)
                row_project(B - 1)

            context()
            weightsT(xa[0])
            keysT(xa[0])
            for h in range(H0):
                keys(xa[0], h)
            columns()
            cross(xa[0])
            ffn0()
            cross(xa[1], ahead=AHEAD)
            self_attention()
            ffn1_last()

        @block.scalar
        def _(act):
            A = nc.scalar
            cp = A.copy

            def xt(stage, b):
                ps = filled(act, ("xT", stage, b))
                if stage in (0, 3, 4):
                    c = {0: 0, 3: 2, 4: 4}[stage]
                    if (stage, b) == (0, 0):
                        taken(act, "cols")
                    A.activation(xT[:, b, :], ps[:, :], ACT.Identity, bias=cols[:, c + 1:c + 2],
                                 scale=cols[:, c:c + 1]).then_inc(freed(("xT", stage, b)), 1)
                else:
                    cp(xT[:, b, :], ps[:, :]).then_inc(freed(("xT", stage, b)), 1)

            def keysT(a):
                for c in range(0, a.H // 2, 2):
                    ps = filled(act, ("kT", a.n, c))
                    for i in range(2):
                        r = slice(DH * i, DH * (i + 1))
                        last = cp(a.KT[r, 2 * c + i, :, :].rearrange("p b k -> p (b k)"), ps[r, 0:B * T])
                    last.then_inc(freed(("kT", a.n, c)), 1)

            def keys(a, h):
                ps = filled(act, ("kp", a.n, h))
                cp(a.KP[:, :, h, :], ps[:, 0:B * T].rearrange("p (b k) -> p b k", b=B))\
                    .then_inc(freed(("kp", a.n, h)), 1)

            def context_values(a, b, ks):
                n = a.n
                for k in ks:
                    c0, size, hs = CHUNKS[k]
                    ps = filled(act, ("v", n, b, k))
                    v = ps[0:size, 0:a.G * len(hs) * DH].rearrange("p (g j d) -> p g j d", g=a.G, d=DH)
                    for j in range(len(hs)):
                        last = A.activation(a.VB[0:size, b, :, FIRST[k] + j, 0:DH], v[:, :, j, :], ACT.Copy,
                                            scale=own[0:size, FIRST[k] + j:FIRST[k] + j + 1])
                    last.then_inc(freed(("v", n, b, k)), 1)

            def self_in(b):
                xt(3, b)
                for k in range(2):
                    for i in range(2):
                        if k == 0:
                            src = filled(act, ("qk", b, i))[:, :]
                            if b:
                                act.wait_ge(parked[i], 16 * PARKS[i])
                        else:
                            taken(act, ("qk", b, i))
                            src = qkr[:, i, :]
                        cp(qk[i][k], src).then_inc(rounded[i], 1)
                ps = filled(act, ("vs", b))
                act.wait_ge(vpads_ready, b + 1)
                cp(VS[b][:, :, :, 0:DS], ps[:, :].rearrange("p (q h d) -> p q h d", q=QT, h=HS))\
                    .then_inc(freed(("vs", b)), 1)

            def cross(a, ahead=None):
                n, uu = a.n, units[a.n]

                def copy_chunk(u, k):
                    size = CHUNKS[k][1]
                    ps = filled(act, ("pt", n, u, k))
                    cp(PT[0:size, k, :], ps[0:size, :]).then_inc(freed(("pt", n, u, k)), 1)

                def outputs(u, c):
                    ps = filled(act, ("o", n, u, c))
                    cp(OT[:, 2 * uu[u][1] + c, :], ps[:, :]).then_inc(freed(("o", n, u, c)), 1)

                def exponentials(u, q0, q1):
                    if u == len(uu):
                        return
                    if uu[u][1] == 0 and q0 == 0:
                        xt(2 * n, uu[u][0])
                    for q in range(q0, q1):
                        ps = filled(act, ("s", n, u, q))
                        act.wait_ge(nm_ready, QT * (n * len(units[0]) + u) + q + 1)
                        for j in range(G4):
                            c = 512 * (j // 2) + T * (j % 2)
                            last = A.activation(pq(n, u, q)[:, j * T:(j + 1) * T], ps[:, c:c + T], ACT.Exp,
                                                bias=nm[:, u % 2, q, j:j + 1], scale=XSCALE,
                                                accum_out=z[:, u % 2, q, j:j + 1])
                        last.then_inc(freed(("s", n, u, q)), 1)

                exponentials(0, 0, 2)
                if n == 0:
                    act.wait_ge(consts, 1)
                    context_values(a, 0, (0, 2, 4))
                exponentials(0, 2, 3)
                if n == 0:
                    context_values(a, 1, (0,))
                exponentials(0, 3, 4)
                if n == 0:
                    context_values(a, 1, (2, 4))
                for u in range(len(uu)):
                    exponentials(u + 1, 0, 1)
                    copy_chunk(u, 0)
                    exponentials(u + 1, 1, 2)
                    copy_chunk(u, 4)
                    copy_chunk(u, 2)
                    if ahead == u:
                        self_in(0)
                    exponentials(u + 1, 2, 3)
                    outputs(u, 0)
                    exponentials(u + 1, 3, 4)
                    outputs(u, 1)
                if n == 0:
                    keysT(xa[1])
                    for h in (0, 2):
                        keys(xa[1], h)

            def gate(n, b):
                act.wait_ge(lg_ready, B * n + b + 1)
                A.activation(ex[:, b, :, :], ex[:, b, :, :], ACT.Exp).then_inc(ex_ready, 1)

            def up(n, b, e):
                ps = filled(act, ("up", n, b, e))
                if n == 0:
                    A.activation(hidden(n, b)[:, e, :], ps[:, :], ACT.Silu, bias=cols[:, 6 + e:7 + e]).then_inc(freed(("up", n, b, e)), 1)
                else:
                    A.activation(hidden(n, b)[:, 2 * e:2 * e + 2, :].rearrange("p e s -> p (e s)"), ps[:, :],
                                 ACT.Relu).then_inc(freed(("up", n, b, e)), 1)

            def weight_rows(n, b):
                ps = filled(act, ("cT", n, b))
                cp(cT[:, b, :], ps[0:3 * E, 0:256].bitcast(BF16)).then_inc(freed(("cT", n, b)), 1)
                if n == 0:
                    ps = filled(act, ("combT", b))
                    cp(combT[:, b, :], ps[0:E, :]).then_inc(freed(("combT", b)), 1)

            def ffn0():
                for b in range(B):
                    xt(1, b)
                    if b == 1:
                        gate(0, 0)
                        gate(0, 1)
                    for e in range(E + 1):
                        up(0, b, e)
                weight_rows(0, 0)
                keys(xa[1], 4)
                weight_rows(0, 1)
                keys(xa[1], 6)

            def ffn1_first(u, kt):
                u -= len(units[2]) - 3
                if (u, kt) == (0, 0):
                    xt(4, 0)
                if (u, kt) == (0, 2):
                    up(1, 0, 0)
                if (u, kt) == (0, 3):
                    gate(1, 0)
                    up(1, 0, 1)
                if (u, kt) == (1, 1):
                    weight_rows(1, 0)

            def ffn1_last():
                xt(4, 1)
                gate(1, 1)
                for e in range(2):
                    up(1, 1, e)
                weight_rows(1, 1)

            def self_attention():
                uu, G = units[2], HS // G4

                def maxima(u):
                    ps = filled(act, ("smT", u))
                    if u >= 2:
                        act.wait_ge(mrow_ready, 16 * 4 * (u - 1))
                    cp(mT[:, u % 2, :], ps[0:8, 0:256].bitcast(BF16)).then_inc(freed(("smT", u)), 1)

                def back(u):
                    ps = filled(act, ("spv", u))
                    cp(OS[:, u % 2, :], ps[:, :]).then_inc(freed(("spv", u)), 1)

                def row_outT(b):
                    ps = filled(act, ("onT", b))
                    cp(OT[:, b, :], ps[:, :]).then_inc(freed(("onT", b)), 1)

                maxima(0)
                self_in(1)
                for u in range(len(uu)):
                    b, g = uu[u]
                    if u:
                        back(u - 1)
                    for kt in range(QT):
                        if u:
                            if kt < QT - 1:
                                act.wait_ge(p_used, 3 * (u - 1) + kt + 1)
                            else:
                                filled(act, ("spv", u - 1))
                        for j in range(G4):
                            ps = filled(act, ("sst", u, kt, j))
                            A.activation(PT[:, 4 * kt + j, :], ps[:, :], ACT.Exp, scale=SSCALE)\
                                .then_inc(freed(("sst", u, kt, j)), 1)
                        if kt == 2 and u + 1 < len(uu):
                            maxima(u + 1)
                        if u and g == 0 and kt == 1:
                            row_outT(b - 1)
                        ffn1_first(u, kt)
                back(len(uu) - 1)
                row_outT(B - 1)

            act.dma_start(ctxm[:, :, :], t["ctx_768"][:, 0:P, :].rearrange("b k c -> k b c")).then_inc(W["ctx"], 16)
            act.dma_start(ctxr[0:R, :, :], t["ctx_768"][:, P:T, :].rearrange("b k c -> k b c")).then_inc(W["ctx"], 16)
            act.dma_start(xa[0].Wk[0:C, :], t["L0_xattn_Wkv"][:, 0:H0 * DH]).then_inc(W["Wk0"], 16)
            act.dma_start(xa[0].Wv[0:C, :], t["L0_xattn_Wkv"][:, H0 * DH:2 * H0 * DH]).then_inc(W["Wv0"], 16)
            ps = filled(act, "ctxT")
            rows_ = ps[0:C, 0:B * T].rearrange("c (b k) -> c b k", b=B)
            cp(ctxT[0:C, :, 0, :], rows_).then_inc(ctx_ready, 1)
            cp(ctxT[0:C, :, 1:G4, :], rows_.unsqueeze(2).broadcast_to([C, B, G4 - 1, T])).then_inc(freed("ctxT"), 1)
            keysT(xa[0])
            for h in range(0, H0, 2):
                keys(xa[0], h)
            ps = filled(act, "cols")
            cp(cols[:, 0:15], ps[:, 0:15]).then_inc(freed("cols"), 1)
            ps = filled(act, "gateT")
            cp(gateT[:, :], ps[:, 0:E]).then_inc(freed("gateT"), 1)
            cross(xa[0])
            ffn0()
            cross(xa[1], ahead=AHEAD)
            self_attention()
            ffn1_last()

        @block.vector
        def _(dve):
            V = nc.vector
            tt = V.tensor_tensor

            def seq(ins):
                link(dve, "dve", ins)

            def statistics(stage, b):
                src = y if stage == 4 else x
                if stage == 0:
                    dve.wait_ge(W["x"], 16 * B)
                for q in range(QT):
                    ins = V.bn_stats(stats[:, b, q, :], src[:, b, q, :])
                seq(ins)
                for q in range(QT):
                    ins = V.bn_aggr(mv[:, b, q, :], stats[:, b, q, :])
                ins.then_inc(stats_ready, 1)

            def normalise(stage, b):
                src = y if stage == 4 else x
                dve.wait_ge(rstd_ready, B * stage + b + 1)
                r = r2 if stage == 0 else rstd
                for q in range(QT):
                    dst = y if stage == 3 else xh
                    ins = V.tensor_scalar(dst[:, b, q, :], src[:, b, q, :], mv[:, b, q, 0:1], r[:, b, q:q + 1],
                                          ALU.subtract, ALU.mult)
                if stage == 3:
                    seq(ins)
                    ins = tt(xh[:, b, :, :], y[:, b, :, :],
                             r2[:, b, :].unsqueeze(2).broadcast_to([P, QT, D]), ALU.mult)
                ins.then_inc(xh_ready, 1)

            def weightsT(a):
                for c0 in range(0, a.H // 2, 4):
                    ps = filled(dve, ("wqT", a.n, c0))
                    V.tensor_copy(a.WqT[:, c0:c0 + 4, :].rearrange("p c k -> p (c k)"), ps[:, :])\
                        .then_inc(freed(("wqT", a.n, c0)), 1)

            def keysT(a):
                for c in range(1, a.H // 2, 2):
                    ps = filled(dve, ("kT", a.n, c))
                    for i in range(2):
                        r = slice(DH * i, DH * (i + 1))
                        ins = V.tensor_copy(a.KT[r, 2 * c + i, :, :].rearrange("p b k -> p (b k)"), ps[r, 0:B * T])
                    ins.then_inc(freed(("kT", a.n, c)), 1)

            def keys(a, h):
                ps = filled(dve, ("kp", a.n, h))
                V.tensor_copy(a.KP[:, :, h, :], ps[:, 0:B * T].rearrange("p (b k) -> p b k", b=B))\
                    .then_inc(freed(("kp", a.n, h)), 1)

            def context_values(a, b, ks):
                for k in ks:
                    c0, size, hs = CHUNKS[k]
                    ps = filled(dve, ("v", a.n, b, k))
                    v = ps[0:size, 0:a.G * len(hs) * DH].rearrange("p (g j d) -> p g j d", g=a.G, d=DH)
                    for j in range(len(hs)):
                        ins = V.tensor_scalar(a.VB[0:size, b, :, FIRST[k] + j, 0:DH], v[:, :, j, :],
                                              own[0:size, FIRST[k] + j:FIRST[k] + j + 1], None, ALU.mult)
                    ins.then_inc(freed(("v", a.n, b, k)), 1)

            def parts(u):
                m, r = mx[:, u % 2, :, :], mr[:, u % 2, :, :]
                hi, lo = (mparts[:, u % 2, :, a, :] for a in range(2))
                seq(V.tensor_copy(hi, m))
                seq(tt(r, m, hi, ALU.subtract))
                V.tensor_copy(lo, r).then_inc(mp_ready, 1)

            def self_in(b):
                for k in range(2):
                    for i in range(2):
                        dve.wait_ge(rounded[i], 2 * b + k + 1)
                        if k == 0:
                            src = filled(dve, ("qk", b, i))[:, :]
                            tt(qkr[:, i, :], src, qk[i][0], ALU.subtract).then_inc(freed(("qk", b, i)), 1)
                        else:
                            if b:
                                dve.wait_ge(parked[i], 16 * PARKS[i])
                            tt(qk[i][2], qkr[:, i, :], qk[i][1], ALU.subtract).then_inc(thirds[i], 1)

            def maxima(a, u, q0, q1):
                n, uu = a.n, units[a.n]
                if u == len(uu):
                    return
                for q in range(q0, q1):
                    ps = filled(dve, ("s", n, u, q))
                    seq(V.tensor_reduce(mx[:, u % 2, q, :],
                                        ps[:, :].rearrange("p (i k) -> p i k", i=2)[:, :, 0:2 * T].rearrange(
                                            "p i (j k) -> p i j k", j=2), AX.X, ALU.max))
                    V.tensor_scalar(nm[:, u % 2, q, :], mx[:, u % 2, q, :], -XSCALE, None, ALU.mult)\
                        .then_inc(nm_ready, 1)

            def cross(a, ahead=None):
                n, uu = a.n, units[a.n]

                def copy_chunk(u, k):
                    size = CHUNKS[k][1]
                    ps = filled(dve, ("pt", n, u, k))
                    V.tensor_copy(PT[0:size, k, :], ps[0:size, :]).then_inc(freed(("pt", n, u, k)), 1)

                def divide(u, q):
                    if u == len(uu):
                        return
                    taken(dve, ("s", n, u, q))
                    r = rz[:, u % 2, q, :]
                    seq(V.reciprocal(r, z[:, u % 2, q, :]))
                    if n == 0:
                        seq(tt(r, r, allow[:, q, 2:3].broadcast_to([P, G4]), ALU.add))
                    for j in range(G4):
                        o = pq(n, u, q)[:, j * T:(j + 1) * T]
                        ins = V.tensor_scalar(o, o, r[:, j:j + 1], None, ALU.mult)
                    ins.then_inc(p_ready, 1)

                def project(b):
                    dve.wait_ge(xb_ready, B * 2 * n + b + 1)
                    ps = filled(dve, ("proj", n, b))
                    row = x[:, b, :, :].rearrange("p q d -> p (q d)")
                    tt(row, ps[:, :], row, ALU.add).then_inc(freed(("proj", n, b)), 1)
                    taken(dve, ("proj", n, b))
                    statistics(2 * n + 1, b)

                if n == 0:
                    maxima(a, 0, 0, 2)
                    dve.wait_ge(consts, 1)
                    context_values(a, 0, (1, 3))
                    maxima(a, 0, 2, 3)
                    divide(0, 0)
                    context_values(a, 1, (1,))
                    maxima(a, 0, 3, 4)
                    divide(0, 1)
                    context_values(a, 1, (3,))
                    divide(0, 2)
                    divide(0, 3)
                    normalise(0, 1)
                else:
                    maxima(a, 0, 1, 3)
                    divide(0, 0)
                    maxima(a, 0, 3, 4)
                    for q in range(1, QT):
                        divide(0, q)
                    normalise(2, 1)
                for u in range(len(uu)):
                    row_end = u and uu[u - 1][1] == a.G - 1
                    if u:
                        divide(u, 3)
                    maxima(a, u + 1, 0, 1)
                    maxima(a, u + 1, 1, 2)
                    divide(u + 1, 0)
                    if row_end:
                        project(uu[u - 1][0])
                    copy_chunk(u, 1)
                    copy_chunk(u, 3)
                    divide(u + 1, 1)
                    if ahead == u:
                        self_in(0)
                    maxima(a, u + 1, 2, 3)
                    maxima(a, u + 1, 3, 4)
                    divide(u + 1, 2)
                    if row_end:
                        normalise(2 * n + 1, uu[u - 1][0])
                if n == 0:
                    weightsT(xa[1])
                    keysT(xa[1])
                    for h in (1, 3):
                        keys(xa[1], h)
                project(B - 1)
                if n == 0:
                    normalise(1, B - 1)

            def logits(n, b):
                l = lg[:, b, :, :]
                ps = filled(dve, ("gate", n, b))
                V.tensor_copy(l.rearrange("p q e -> p (q e)"), ps[:, 0:QT * E]).then_inc(freed(("gate", n, b)), 1)
                taken(dve, ("gate", n, b))
                seq(V.tensor_reduce(g1[:, b, :, 0], l, AX.X, ALU.max))
                tt(ex[:, b, :, :], l, g1[:, b, :, 0:1].broadcast_to([P, QT, E]), ALU.subtract).then_inc(lg_ready, 1)

            def gate(n, b):
                e_, z = ex[:, b, :, :], g1[:, b, :, 1:2]
                wide = [P, QT, E]
                dve.wait_ge(ex_ready, B * n + b + 1)
                if n == 0:
                    seq(V.tensor_reduce(g1[:, b, :, 1], e_, AX.X, ALU.add))
                    seq(V.reciprocal(g1[:, b, :, 1], g1[:, b, :, 1]))
                    seq(tt(e_, e_, z.broadcast_to(wide), ALU.mult))
                    ranked = ex
                else:
                    ranked = lg
                for q in range(QT):
                    seq(V.max(top[:, b, q, :], ranked[:, b, q, :]))
                    seq(V.max_index(topi[:, b, q, :], top[:, b, q, :], ranked[:, b, q, :]))
                seq(V.tensor_copy(topf[:, b, :, :], topi[:, b, :, :]))
                if n == 0 and b == 0:
                    dve.wait_ge(consts, 2)
                for k in range(2):
                    ins = tt(oh[:, b, :, k, :], iota[:, :].unsqueeze(1).broadcast_to(wide),
                             topf[:, b, :, k:k + 1].broadcast_to(wide), ALU.is_equal)
                    seq(ins)
                seq(tt(oh[:, b, :, 0, :], oh[:, b, :, 0, :], oh[:, b, :, 1, :], ALU.add))
                c = comb[:, b, :, :]
                seq(tt(c, e_, oh[:, b, :, 0, :], ALU.mult))
                seq(V.tensor_reduce(g1[:, b, :, 2], c, AX.X, ALU.add))
                if n == 0:
                    seq(V.tensor_scalar(g1[:, b, :, 2], g1[:, b, :, 2], 1e-20, None, ALU.add))
                seq(V.reciprocal(g1[:, b, :, 3], g1[:, b, :, 2]))
                ins = tt(c, c, g1[:, b, :, 3:4].broadcast_to(wide), ALU.mult)
                seq(ins)
                p1, p2, p3 = (cparts[:, b, :, k, :] for k in range(3))
                r = cr[:, b, :, :]
                seq(V.tensor_copy(p1, c))
                seq(tt(r, c, p1, ALU.subtract))
                seq(V.tensor_copy(p2, r))
                tt(p3, r, p2, ALU.subtract).then_inc(cparts_ready, 1)

            def weights(n, b, e):
                ps = filled(dve, ("cb", n, b, e))
                if e == 0:
                    ups = E + 1 if n == 0 else 2
                    taken(dve, ("up", n, b, ups - 1))
                    taken(dve, ("up", n, b, ups - 2))
                h = hidden(n, b)[:, e, :] if n == 0 else \
                    hidden(n, b)[:, 2 * e:2 * e + 2, :].rearrange("p e s -> p (e s)")
                tt(h, h, ps[:, :], ALU.mult).then_inc(freed(("cb", n, b, e)), 1)

            def downs(n, b):
                dve.wait_ge(xb_ready, B * (1 + 2 * n) + b + 1)
                ps = filled(dve, ("dn", n, b))
                row = x[:, b, :, :].rearrange("p q d -> p (q d)")
                tt(row, row, ps[:, 0:S], ALU.add).then_inc(freed(("dn", n, b)), 1)

            def ffn0():
                logits(0, 0)
                logits(0, 1)
                for b in range(B):
                    context_values(xa[1], b, (0, 1, 2, 3, 4))
                gate(0, 0)
                gate(0, 1)
                for e in range(2 * E):
                    weights(0, e // E, e % E)
                    if e in (5, 9):
                        keys(xa[1], 5 + 2 * (e // 8))
                    if e == E + 2:
                        downs(0, 0)
                        taken(dve, ("dn", 0, 0))
                        statistics(2, 0)
                    if e == E + 5:
                        normalise(2, 0)
                maxima(xa[1], 0, 0, 1)
                downs(0, 1)
                taken(dve, ("dn", 0, 1))
                statistics(2, 1)

            def ffn1_first(u, kt):
                u -= len(units[2]) - 3
                if (u, kt) == (0, 1):
                    logits(1, 0)
                if (u, kt) == (0, 3):
                    gate(1, 0)
                if u == 1 and kt >= 2:
                    weights(1, 0, kt - 2)
                if (u, kt) == (2, 3):
                    downs(1, 0)

            def ffn1_last():
                logits(1, 1)
                gate(1, 1)
                for e in range(2):
                    weights(1, 1, e)
                downs(1, 1)

            def self_attention():
                uu, G = units[2], HS // G4

                pairs = iter([(u, k) for u in range(len(uu)) for k in range(8)])

                def maxima(count):
                    for _ in range(count):
                        u, k = next(pairs, (None, None))
                        if u is None:
                            return
                        ps = filled(dve, ("ss", u, k))
                        j = 2 * (k % 2)
                        V.tensor_reduce(mx[:, u % 2, k // 2, j:j + 2], ps[:, :].rearrange("p (i k) -> p i k", i=2),
                                        AX.X, ALU.max).then_inc(freed(("ss", u, k)), 1)
                        if k == 7:
                            taken(dve, ("ss", u, 7))
                            parts(u)

                def back(u):
                    b, g = uu[u]
                    ps = filled(dve, ("sO", u))
                    v = ps[:, :].rearrange("p (q j d) -> p q j d", q=QT, j=G4)
                    z = zs[:, u % 2, :, :]
                    seq(V.reciprocal(z, v[:, :, :, DS]))
                    tt(On[:, :, G4 * g:G4 * (g + 1), :], v[:, :, :, 0:DS],
                       z.unsqueeze(3).broadcast_to([P, QT, G4, DS]), ALU.mult).then_inc(freed(("sO", u)), 1)

                def row_project(b):
                    ps = filled(dve, ("sproj", b))
                    row = y[:, b, :, :].rearrange("p q d -> p (q d)")
                    tt(row, ps[:, 0:S], row, ALU.add).then_inc(freed(("sproj", b)), 1)
                    taken(dve, ("sproj", b))
                    statistics(4, b)

                maxima(8)
                normalise(3, 1)
                maxima(4)
                self_in(1)
                for u in range(len(uu)):
                    b, g = uu[u]
                    for kt in range(QT):
                        maxima(2)
                        if kt == 0 and u:
                            back(u - 1)
                        if u and g == 0 and kt == 2:
                            row_project(b - 1)
                        if u and g == 0 and kt == 3:
                            normalise(4, b - 1)
                        ffn1_first(u, kt)
                back(len(uu) - 1)
                row_project(B - 1)
                normalise(4, B - 1)

            V.memset(xa[0].KT[DH:P, 0:H0:2, :, :], 0.0)
            V.memset(xa[0].KT[0:DH, 1:H0:2, :, :], 0.0).then_inc(kt_pads, 1)
            weightsT(xa[0])
            keysT(xa[0])
            for h in range(1, H0, 2):
                keys(xa[0], h)
                if h in (1, 5):
                    statistics(0, h // 4)
                if h == 11:
                    normalise(0, 0)
            dve.wait_ge(W["mask"], 16)
            V.tensor_scalar(maskb[:, :, :], masku[:, :, :], -BLOCKED, BLOCKED, ALU.mult, ALU.add)\
                .then_inc(mask_ready, 1)
            seq(V.tensor_copy(maskf[:, :, :], masku[:, :, :]))
            seq(V.tensor_reduce(allow[:, :, 0], maskf[:, :, :], AX.X, ALU.add))
            seq(V.reciprocal(allow[:, :, 1], allow[:, :, 0]))
            seq(V.tensor_scalar(allow[:, :, 2], allow[:, :, 1], 0.0, None, ALU.mult))
            cross(xa[0])
            ffn0()
            cross(xa[1], ahead=AHEAD)
            self_attention()
            ffn1_last()

        @block.gpsimd
        def _(pool):
            G = nc.gpsimd

            def seq(ins):
                link(pool, "pool", ins)

            for m in (ident, identb):
                seq(G.memset(m[:, :], 0.0))
            seq(G.affine_select(out=identb[:, :], in_=identb[:, :], compare_op=ALU.not_equal, fill=1.0, base=0,
                                pattern=[[-1, P]], channel_multiplier=1))
            G.affine_select(out=ident[:, :], in_=ident[:, :], compare_op=ALU.not_equal, fill=1.0, base=0,
                            pattern=[[-1, P]], channel_multiplier=1).then_inc(ident_ready, 1)
            pool.wait_ge(ident_ready, 1)
            seq(G.memset(ctxT[C:P, :, :, :], 0.0))
            seq(G.memset(xa[0].Wk[C:P, :], 0.0))
            G.memset(xa[0].Wv[C:P, :], 0.0).then_inc(ctx_pads, 1)
            pool.wait_ge(ctx_pads, 1)
            seq(G.memset(mhalf[:, :], -0.5))
            seq(G.memset(own[:, :], 1.0))
            for i, (k, h) in enumerate(BLOCKS):
                c0 = CHUNKS[k][0]
                for base, sign in ((c0 - T * h, 1), (T * (h + 1) - 1 - c0, -1)):
                    seq(G.affine_select(out=own[:, i:i + 1], in_=own[:, i:i + 1], compare_op=ALU.is_ge, fill=0.0,
                                        base=base, pattern=[[0, 1]], channel_multiplier=sign))
            G.memset(v2[:, :, :], 0.0).then_inc(consts, 1)
            pool.wait_ge(consts, 1)

            def norm(stage, b):
                pool.wait_ge(stats_ready, B * stage + b + 1)
                half = mhalf[:, 0:QT]
                twice = stage in (0, 3)
                seq(G.tensor_scalar(ve[:, b, :], mv[:, b, :, 1], EPS, None, ALU.add))
                ins = G.tensor_tensor(rstd[:, b, :], ve[:, b, :], half, ALU.pow)
                if twice:
                    seq(ins)
                    seq(G.tensor_tensor(v2[:, b, :], mv[:, b, :, 1], rstd[:, b, :], ALU.mult))
                    seq(G.tensor_tensor(v2[:, b, :], v2[:, b, :], rstd[:, b, :], ALU.mult))
                    seq(G.tensor_scalar(v2[:, b, :], v2[:, b, :], EPS, None, ALU.add))
                    ins = G.tensor_tensor(r2[:, b, :], v2[:, b, :], half, ALU.pow)
                    if stage == 0:
                        seq(ins)
                        ins = G.tensor_tensor(r2[:, b, :], r2[:, b, :], rstd[:, b, :], ALU.mult)
                ins.then_inc(rstd_ready, 1)

            def add_bias(stage, b):
                pool.wait_ge(xh_ready, B * stage + b + 1)
                if stage == 0 and b == 0:
                    pool.wait_ge(W["bo"], 48)
                o = x[:, b, :, :]
                G.tensor_tensor(o, o, bo[:, stage, :].unsqueeze(1).broadcast_to([P, QT, D]), ALU.add)\
                    .then_inc(xb_ready, 1)

            def expert_selections():
                for c in (H0 // 2 - 2, H0 // 2 - 1):
                    taken(pool, ("kT", 0, c))
                seq(G.memset(selc[:, :, :], 0.0))
                for part in range(3):
                    seq(G.affine_select(out=selc[:, :, :], in_=selc[:, :, :], compare_op=ALU.not_equal, fill=1.0,
                                        base=-E * part, pattern=[[-1, E], [0, P]], channel_multiplier=1))
                seq(G.iota(iotai[:, :], pattern=[[1, E]], base=0, channel_multiplier=0))
                G.tensor_copy(iota[:, :], iotai[:, :]).then_inc(consts, 1)
                pool.wait_ge(consts, 2)

            norm(0, 0)
            norm(0, 1)
            pool.wait_ge(rstd_ready, B)
            seq(G.memset(xa[1].Wk[C:P, :], 0.0))
            seq(G.memset(xa[1].Wv[C:P, :], 0.0))
            seq(G.memset(xa[1].KT[DH:P, 0:H1:2, :, :], 0.0))
            G.memset(xa[1].KT[0:DH, 1:H1:2, :, :], 0.0).then_inc(ctx_pads, 1)
            pool.wait_ge(ctx_pads, 2)
            add_bias(0, 0)
            add_bias(0, 1)
            pool.wait_ge(xb_ready, B)
            expert_selections()
            pool.wait_ge(W["Ws"], 64)
            for i in range(2):
                G.tensor_copy(Wqk[:, i, :].rearrange("p (d par c) -> p c par d", d=DS, par=2),
                              Ws[:, i, :].rearrange("p (c par d) -> p c par d", par=2, d=DS)).then_inc(wqk_ready, 1)
                pool.wait_ge(wqk_ready, i + 1)
            for stage in (1, 2):
                for b in range(B):
                    norm(stage, b)
                    add_bias(stage, b)
            pool.wait_ge(xb_ready, 3 * B)
            for b in range(B):
                seq(G.memset(stackk[b][:, :, :].bitcast(F32), 0.0))
                for par in range(2):
                    r = slice(32 + 64 * par, 64 + 64 * par)
                    seq(G.memset(stackk[b][r, par:HS:2, :].bitcast(F32), MINUS_ONES))
                    seq(G.memset(stackq[b][r, :, :].bitcast(F32), 0.0))
                if b == 0:
                    seq(G.memset(VS[b][:, :, :, DS:STRIP], 0.0))
                    G.memset(VS[b][:, :, :, DS:DS + 1], 1.0).then_inc(vpads_ready, 1)
                    pool.wait_ge(vpads_ready, 1)
                G.memset(zs[:, :, :, :], 0.0).then_inc(kpads_ready, 1)
                pool.wait_ge(kpads_ready, b + 1)
            norm(3, 0)
            norm(3, 1)
            pool.wait_ge(rstd_ready, 4 * B)
            seq(G.memset(VS[1][:, :, :, DS:STRIP], 0.0))
            G.memset(VS[1][:, :, :, DS:DS + 1], 1.0).then_inc(vpads_ready, 1)
            for b in range(B):
                norm(4, b)
                pool.wait_ge(xh_ready, B * 4 + b + 1)
                G.tensor_tensor(x[:, b, :, :], x[:, b, :, :], y[:, b, :, :], ALU.add).then_inc(xb_ready, 1)

        @block.sync
        def _(sp):
            def load(dst, src, name):
                sp.dma_start(dst, src).then_inc(W[name], 16)

            def row(v):
                return v.rearrange("(a d) -> a d", a=1)

            load(xa[0].Wq[:, :], t["L0_xattn_Wq"], "Wq0")
            for b in range(B):
                load(x[:, b, :, :], t["x"][b].rearrange("(q p) d -> p q d", p=P), "x")
            load(masku[:, :, :], t["mask_1x1xSxS2_bk0"][0, 0].rearrange("(q p) k -> p q k", p=P), "mask")
            for i, k in enumerate(("L0_xattn_ln_gamma", "L0_xattn_ln_beta", "L1_ffn_g1", "L1_ffn_b1",
                                   "L1_ffn_g2", "L1_ffn_b2")):
                load(rows[i:i + 1, :], row(t[k]), "rows")
            load(rows[6:14, :], t["L0_ffn_up_b"], "rows")
            load(rows[14:15, :], row(t["L0_ffn_sh_up_b"]), "rows")
            load(gwr[:, :], t["L0_ffn_gate_w"], "gate")
            for i, k in enumerate(("L0_xattn_bo", "L0_ffn_sh_down_b", "L1_xattn_bo")):
                load(bo[:, i, :], t[k].partition_broadcast(P), "bo")
            load(xa[0].Wo[:, :, :], t["L0_xattn_Wo"].rearrange("(c p) d -> p c d", p=P), "Wo0")
            load(xa[1].Wq[:, :], t["L1_xattn_Wq"], "Wq1")
            load(xa[1].Wk[0:C, :], t["L1_xattn_Wk"], "Wk1")
            load(xa[1].Wv[0:C, :], t["L1_xattn_Wv"], "Wv1")
            load(upw[:, 0:E, :], t["L0_ffn_up_w"].rearrange("e d h -> d e h"), "upw")
            load(upw[:, E, :], t["L0_ffn_sh_up_w"], "upw")
            load(dnw[:, 0:E, :], t["L0_ffn_down_w"].rearrange("e h d -> h e d"), "dnw")
            load(dnw[:, E, :], t["L0_ffn_sh_down_w"], "dnw")
            load(dnb[:, :], t["L0_ffn_down_b"], "dnw")
            load(xa[1].Wo[:, :, :], t["L1_xattn_Wo"].rearrange("(c p) d -> p c d", p=P), "Wo1")
            for i, k in enumerate(("Wq", "Wk", "Wv", "Wo")):
                load(Ws[:, i, :], t[f"L1_ffn_{k}"], "Ws")
            load(Wg[:, :], t["L1_ffn_Wg"], "Wg")
            load(W1[:, :, :], t["L1_ffn_W1"].rearrange("e d h -> d e h"), "W1")
            load(W2[:, :, :], t["L1_ffn_W2"].rearrange("(c i) h d -> (i h) c d", i=2), "W2")

            def fill_stacks(b):
                for i in range(2):
                    copies = (((0, slice(0, 3)), (1, slice(3, 5)), (2, slice(5, 6))),
                              ((0, slice(0, 4, 3)), (0, slice(5, 6)), (1, slice(1, 5, 3)), (2, slice(2, 3))))[i]
                    for j, to in copies:
                        sp.wait_ge(rounded[i] if j < 2 else thirds[i], (2 * b + j if j < 2 else b) + 1)
                        dst = scratch[b, i, to].rearrange("r p s -> p r s")
                        src = qk[i][j].unsqueeze(1).broadcast_to([P, dst.shape[1], S])
                        sp.dma_start(dst, src).then_inc(parked[i], 16)
                for i in range(2):
                    sp.wait_ge(parked[i], 16 * PARKS[i] * (b + 1))
                    if i == 0:
                        sp.wait_ge(kpads_ready, b + 1)
                    for par in range(2):
                        src = scratch[b, i].rearrange("r (d e c) s -> e (r d) c s", d=DS, e=2)[par]
                        rows_ = slice(64 * par, 64 * par + 6 * DS)
                        dst = stackq[b][rows_, :, :] if i == 0 else stackk[b][rows_, par:HS:2, :]
                        sp.dma_start(dst, src).then_inc(stacked, 16)

            def fill_maxima(u):
                b, g = units[2][u]
                taken(sp, ("smT", u))
                for part in range(2):
                    for pair in range(2):
                        m0 = G4 * part + 2 * pair
                        sp.dma_start(stackq[b][48 + part:P:64, 2 * g + pair, :], mT[m0:m0 + 2, u % 2, :])\
                            .then_inc(mrow_ready, 16)

            fill_stacks(0)
            fill_maxima(0)
            fill_stacks(1)
            for u in range(1, len(units[2])):
                fill_maxima(u)
            for b in range(B):
                taken(sp, ("dn", 1, b))
                sp.dma_start(out[b].rearrange("(q p) d -> p q d", p=P), x[:, b, :, :]).then_inc(stored, 16)
            sp.wait_ge(stored, 16 * B)


_INS = ["x", "ctx_768", "mask_1x1xSxS2_bk0", "L0_xattn_ln_gamma", "L0_xattn_ln_beta", "L0_xattn_Wq",
        "L0_xattn_Wkv", "L0_xattn_Wo", "L0_xattn_bo", "L0_ffn_gate_w", "L0_ffn_up_w", "L0_ffn_up_b",
        "L0_ffn_down_w", "L0_ffn_down_b", "L0_ffn_sh_up_w", "L0_ffn_sh_up_b", "L0_ffn_sh_down_w",
        "L0_ffn_sh_down_b", "L1_xattn_Wq", "L1_xattn_Wk", "L1_xattn_Wv", "L1_xattn_Wo", "L1_xattn_bo",
        "L1_ffn_Wq", "L1_ffn_Wk", "L1_ffn_Wv", "L1_ffn_Wo", "L1_ffn_g1", "L1_ffn_b1", "L1_ffn_g2", "L1_ffn_b2",
        "L1_ffn_Wg", "L1_ffn_W1", "L1_ffn_W2"]


def kernel(**inputs):
    import numpy as _np
    import concourse.bacc as _bacc
    from concourse import mybir as _mybir
    from concourse.bass_utils import run_bass_kernel_spmd as _run

    nc = _bacc.Bacc("TRN2", target_bir_lowering=False, num_devices=1)
    arrays, aps = {}, {}
    for name in _INS:
        a = _np.ascontiguousarray(inputs[name])
        arrays[f"in_{name}_dram"] = a
        aps[name] = nc.dram_tensor(f"in_{name}_dram", a.shape, _mybir.dt.from_np(a.dtype),
                                   kind="ExternalInput").ap()
    shape = inputs["x"].shape
    out = nc.dram_tensor("out_0_dram", shape, _mybir.dt.float32, kind="ExternalOutput").ap()
    build(nc, aps, out)
    r = _run(nc, [arrays], core_ids=[0])
    return r.results[0]["out_0_dram"]
```
